# Optimizing a Trainium2 kernel written in Bass

```python
import numpy as np
import jax
import jax.numpy as jnp

def _softmax(x, axis=-1):
    return jax.nn.softmax(x, axis=axis)

def _gelu(x):
    return jax.nn.gelu(x, approximate=True)

def _silu(x):
    return jax.nn.silu(x)

def _sigmoid(x):
    return jax.nn.sigmoid(x)

def _layernorm(x, axis=-1, eps=1e-05):
    m = jnp.mean(x, axis=axis, keepdims=True)
    v = jnp.var(x, axis=axis, keepdims=True)
    return (x - m) / jnp.sqrt(v + eps)

def _scatter_add(tgt, idx, src, axis=0):
    return tgt.at[idx].add(src)

def _segment_sum(src, seg, n):
    return jax.ops.segment_sum(src, seg, n)
kernel_name = 'mk_gnn_ffn_d2_gnn_r16_ba2c1b'

def setup_inputs(seed: int=0):
    np.random.seed(seed)
    _w = jnp.asarray

    def _rec_inputs():
        import jax
        import jax.numpy as jnp
        _gk = jax.random.key(seed)
        x = -0.0002117 + 1 * jax.random.normal(jax.random.fold_in(_gk, 1), (3125, 512), jnp.float32)
        src = jax.random.randint(jax.random.fold_in(_gk, 2), (50000,), 0, 3125, jnp.int32)
        dst = jax.random.randint(jax.random.fold_in(_gk, 3), (50000,), 0, 3125, jnp.int32)
        _o = jnp.argsort(dst, stable=True)
        src = src[_o]
        dst = dst[_o]
        return (x, src, dst)
    x, src, dst = _rec_inputs()

    def _L0_gnn_setup():
        import jax, jax.numpy as jnp
        import numpy as np
        N, E, H, D_IN, D_PRIME = (3125, 50000, 8, 512, 64)

        def _segment_softmax(scores, seg, num_segments):
            smax = jax.ops.segment_max(scores, seg, num_segments=num_segments)
            ex = jnp.exp(scores - smax[seg])
            denom = jax.ops.segment_sum(ex, seg, num_segments=num_segments)
            return ex / denom[seg]
        key = jax.random.key(seed)
        ks = jax.random.split(key, 6)
        x = jax.random.normal(ks[0], (N, D_IN), dtype=jnp.float32)
        edge_index = jax.random.randint(ks[1], (2, E), 0, N)
        Ws = jax.random.normal(ks[2], (H, D_IN, D_PRIME), dtype=jnp.float32) * 0.05
        Wb = jax.random.normal(ks[3], (H, D_PRIME), dtype=jnp.float32) * 0.05
        a_w = jax.random.normal(ks[4], (H, 2 * D_PRIME), dtype=jnp.float32) * 0.05
        a_b = jax.random.normal(ks[5], (H,), dtype=jnp.float32) * 0.05
        return dict(x=x, edge_index=edge_index, Ws=Ws, Wb=Wb, a_w=a_w, a_b=a_b)
    _L0_gnn_all = _L0_gnn_setup()
    _L0_gnn_in = {k: v for k, v in _L0_gnn_all.items() if k in ('Ws', 'Wb', 'a_w', 'a_b')}
    del _L0_gnn_all

    def _L0_ffn_setup():
        import jax, jax.numpy as jnp
        import numpy as np
        B, T, D = (4, 512, 512)
        E, F, CAP = (8, 128, 256)
        key = jax.random.key(seed)
        ks = jax.random.split(key, 6)
        s = 0.02
        return {'x': jax.random.normal(ks[0], (B, T, D), dtype=jnp.float32), 'Wr': jax.random.normal(ks[1], (D, E), dtype=jnp.float32) * s, 'W1': jax.random.normal(ks[2], (E, D, F), dtype=jnp.float32) * s, 'b1': jax.random.normal(ks[3], (E, F), dtype=jnp.float32) * s, 'W2': jax.random.normal(ks[4], (E, F, D), dtype=jnp.float32) * s, 'b2': jax.random.normal(ks[5], (E, D), dtype=jnp.float32) * s}
    _L0_ffn_all = _L0_ffn_setup()
    _L0_ffn_in = {k: v for k, v in _L0_ffn_all.items() if k in ('Wr', 'W1', 'b1', 'W2', 'b2')}
    del _L0_ffn_all

    def _L1_gnn_setup():
        import jax, jax.numpy as jnp
        import numpy as np
        N_NODES = 625
        N_EDGES = 10000
        D_IN = 512
        D_OUT = 512
        key = jax.random.key(seed)
        k_x, k_e, k_wl, k_wr = jax.random.split(key, 4)
        x = jax.random.normal(k_x, (N_NODES, D_IN), dtype=jnp.float32)
        edge_index = jax.random.randint(k_e, (2, N_EDGES), 0, N_NODES, dtype=jnp.int64)
        scale = 1.0 / np.sqrt(D_IN)
        W_l = jax.random.normal(k_wl, (D_IN, D_OUT), dtype=jnp.float32) * scale
        W_r = jax.random.normal(k_wr, (D_IN, D_OUT), dtype=jnp.float32) * scale
        b = jnp.zeros((D_OUT,), dtype=jnp.float32)
        return {'x': x, 'edge_index': edge_index, 'W_l': W_l, 'W_r': W_r, 'b': b}
    _L1_gnn_all = _L1_gnn_setup()
    _L1_gnn_in = {k: v for k, v in _L1_gnn_all.items() if k in ('W_l', 'W_r', 'b')}
    del _L1_gnn_all

    def _L1_ffn_setup():
        import jax, jax.numpy as jnp
        import numpy as np
        E = 64
        K = 2
        D = 512
        H = 256
        NSH = 2
        ROUTE_SCALE = 2.5
        CAP = 1024
        STD = 0.02
        key = jax.random.key(seed)
        ks = jax.random.split(key, 8)
        x = jax.random.normal(ks[0], (4, 128, D), dtype=jnp.float32)
        gate_w = jax.random.normal(ks[1], (E, D), dtype=jnp.float32) * STD
        w1 = jax.random.normal(ks[2], (E, D, H), dtype=jnp.float32) * STD
        w3 = jax.random.normal(ks[3], (E, D, H), dtype=jnp.float32) * STD
        w2 = jax.random.normal(ks[4], (E, H, D), dtype=jnp.float32) * STD
        sw1 = jax.random.normal(ks[5], (D, H * NSH), dtype=jnp.float32) * STD
        sw3 = jax.random.normal(ks[6], (D, H * NSH), dtype=jnp.float32) * STD
        sw2 = jax.random.normal(ks[7], (H * NSH, D), dtype=jnp.float32) * STD
        return {'x': x, 'gate_w': gate_w, 'w1': w1, 'w3': w3, 'w2': w2, 'sw1': sw1, 'sw3': sw3, 'sw2': sw2}
    _L1_ffn_all = _L1_ffn_setup()
    _L1_ffn_in = {k: v for k, v in _L1_ffn_all.items() if k in ('gate_w', 'w1', 'w3', 'w2', 'sw1', 'sw3', 'sw2')}
    del _L1_ffn_all
    return {'x': x, 'src': src, 'dst': dst, 'L0_gnn_Ws': _L0_gnn_in['Ws'], 'L0_gnn_Wb': _L0_gnn_in['Wb'], 'L0_gnn_a_w': _L0_gnn_in['a_w'], 'L0_gnn_a_b': _L0_gnn_in['a_b'], 'L0_ffn_Wr': _L0_ffn_in['Wr'], 'L0_ffn_W1': _L0_ffn_in['W1'], 'L0_ffn_b1': _L0_ffn_in['b1'], 'L0_ffn_W2': _L0_ffn_in['W2'], 'L0_ffn_b2': _L0_ffn_in['b2'], 'L1_gnn_W_l': _L1_gnn_in['W_l'], 'L1_gnn_W_r': _L1_gnn_in['W_r'], 'L1_gnn_b': _L1_gnn_in['b'], 'L1_ffn_gate_w': _L1_ffn_in['gate_w'], 'L1_ffn_w1': _L1_ffn_in['w1'], 'L1_ffn_w3': _L1_ffn_in['w3'], 'L1_ffn_w2': _L1_ffn_in['w2'], 'L1_ffn_sw1': _L1_ffn_in['sw1'], 'L1_ffn_sw3': _L1_ffn_in['sw3'], 'L1_ffn_sw2': _L1_ffn_in['sw2']}

def reference(x, src, dst, L0_gnn_Ws, L0_gnn_Wb, L0_gnn_a_w, L0_gnn_a_b, L0_ffn_Wr, L0_ffn_W1, L0_ffn_b1, L0_ffn_W2, L0_ffn_b2, L1_gnn_W_l, L1_gnn_W_r, L1_gnn_b, L1_ffn_gate_w, L1_ffn_w1, L1_ffn_w3, L1_ffn_w2, L1_ffn_sw1, L1_ffn_sw3, L1_ffn_sw2):
    import jax
    import jax.numpy as jnp

    def _L0_gnn_ref(x, edge_index, Ws, Wb, a_w, a_b):
        import jax, jax.numpy as jnp
        import numpy as np
        N, E, H, D_IN, D_PRIME = (3125, 50000, 8, 512, 64)

        def _segment_softmax(scores, seg, num_segments):
            smax = jax.ops.segment_max(scores, seg, num_segments=num_segments)
            ex = jnp.exp(scores - smax[seg])
            denom = jax.ops.segment_sum(ex, seg, num_segments=num_segments)
            return ex / denom[seg]
        v_src, v_tgt = (edge_index[0], edge_index[1])
        n = x.shape[0]
        outs = []
        for h in range(Ws.shape[0]):
            Wx = x @ Ws[h] + Wb[h]
            d = Wx.shape[-1]
            s = Wx[v_tgt] @ a_w[h, :d] + Wx[v_src] @ a_w[h, d:] + a_b[h]
            s = jax.nn.leaky_relu(s, negative_slope=0.2)
            alpha = _segment_softmax(s, v_tgt, n)
            outs.append(jax.ops.segment_sum(alpha[:, None] * Wx[v_src], v_tgt, num_segments=n))
        return jnp.stack(outs, axis=1).reshape(n, -1)

    def _L0_ffn_ref(x, Wr, W1, b1, W2, b2):
        import jax, jax.numpy as jnp
        import numpy as np
        B, T, D = (4, 512, 512)
        E, F, CAP = (8, 128, 256)
        Bb, Tt, Dd = x.shape
        N = Bb * Tt
        C = min(CAP, N)
        x_flat = x.reshape(N, Dd)
        logits = x_flat @ Wr
        probs = jax.nn.softmax(logits, axis=0)
        vals, idx = jax.lax.top_k(probs.T, C)
        selected = x_flat[idx]
        h = jax.nn.gelu(jnp.einsum('ecd,edf->ecf', selected, W1) + b1[:, None, :], approximate=False)
        out_e = jnp.einsum('ecf,efd->ecd', h, W2) + b2[:, None, :]
        weighted = vals[..., None] * out_e
        output = jnp.zeros_like(x_flat).at[idx.reshape(-1)].add(weighted.reshape(-1, Dd))
        return output.reshape(Bb, Tt, Dd)

    def _L1_gnn_ref(x, edge_index, W_l, W_r, b):
        import jax, jax.numpy as jnp
        import numpy as np
        N_NODES = 625
        N_EDGES = 10000
        D_IN = 512
        D_OUT = 512
        src = edge_index[0]
        dst = edge_index[1]
        n = x.shape[0]
        msg = x[src]
        agg = jax.ops.segment_sum(msg, dst, num_segments=n)
        deg = jax.ops.segment_sum(jnp.ones((src.shape[0],), x.dtype), dst, num_segments=n)
        mean = agg / jnp.maximum(deg, 1.0)[:, None]
        h = mean @ W_l + b + x @ W_r
        return h * jax.nn.sigmoid(h)

    def _L1_ffn_ref(x, gate_w, w1, w3, w2, sw1, sw3, sw2):
        import jax, jax.numpy as jnp
        import numpy as np
        E = 64
        K = 2
        D = 512
        H = 256
        NSH = 2
        ROUTE_SCALE = 2.5
        CAP = 1024
        STD = 0.02
        bs, slen, d = x.shape
        xf = x.reshape(-1, d)
        logits = xf @ gate_w.T
        scores = jax.nn.sigmoid(logits.astype(jnp.float32))
        top_scores, top_idx = jax.lax.top_k(scores, K)
        top_scores = top_scores / (top_scores.sum(-1, keepdims=True) + 1e-20)
        top_scores = top_scores * ROUTE_SCALE
        flat_e = top_idx.reshape(-1)
        x_pairs = jnp.repeat(xf, K, axis=0)
        oh = jax.nn.one_hot(flat_e, E, dtype=jnp.int32)
        pos = jnp.take_along_axis(jnp.cumsum(oh, axis=0), flat_e[:, None], axis=1)[:, 0] - 1
        buf = jnp.zeros((E, CAP, d), dtype=xf.dtype).at[flat_e, pos].set(x_pairs, mode='drop')
        h = jax.nn.silu(jnp.einsum('ecd,edh->ech', buf, w1)) * jnp.einsum('ecd,edh->ech', buf, w3)
        y = jnp.einsum('ech,ehd->ecd', h, w2)
        valid = (pos < CAP)[:, None]
        y_pairs = jnp.where(valid, y[flat_e, jnp.minimum(pos, CAP - 1)], 0.0)
        routed = (y_pairs.reshape(-1, K, d) * top_scores[..., None].astype(xf.dtype)).sum(axis=1)
        shared = jax.nn.silu(xf @ sw1) * (xf @ sw3) @ sw2
        return (shared + routed).reshape(bs, slen, d)
    edge_index = jnp.stack([src, dst])
    x = x + _L0_gnn_ref(_layernorm(x, axis=-1), edge_index, L0_gnn_Ws, L0_gnn_Wb, L0_gnn_a_w, L0_gnn_a_b)
    x = x + _L0_ffn_ref(_layernorm(x, axis=-1)[None], L0_ffn_Wr, L0_ffn_W1, L0_ffn_b1, L0_ffn_W2, L0_ffn_b2)[0]
    x = x + _L1_gnn_ref(_layernorm(x, axis=-1), edge_index, L1_gnn_W_l, L1_gnn_W_r, L1_gnn_b)
    x = x + _L1_ffn_ref(_layernorm(x, axis=-1)[None], L1_ffn_gate_w, L1_ffn_w1, L1_ffn_w3, L1_ffn_w2, L1_ffn_sw1, L1_ffn_sw3, L1_ffn_sw2)[0]
    return x

_drawn_inputs = setup_inputs


def setup_inputs(seed=0):
    import zlib

    import numpy as np

    out = dict(_drawn_inputs(seed))
    spreads = {'L1_gnn_b': (0.0, 0.1)}
    factors = {'L0_gnn_a_b': 8.0,
     'L0_ffn_Wr': 8.0,
     'L0_ffn_W1': 8.0,
     'L0_ffn_b1': 183.542,
     'L0_ffn_W2': 8.0,
     'L0_ffn_b2': 200.0}
    for name, (base, spread) in spreads.items():
        noise = np.random.default_rng([zlib.crc32(name.encode()), seed]).standard_normal(out[name].shape)
        drawn = base * np.exp(spread * noise) if base else spread * noise
        out[name] = jnp.asarray(drawn.astype(out[name].dtype))
    for name, factor in factors.items():
        out[name] = (out[name] * factor).astype(out[name].dtype)
    return out
```

```python
from contextlib import ExitStack

import numpy as np

import concourse.bass as bass
from concourse import mybir

ALU = mybir.AluOpType
ACT = mybir.ActivationFunctionType
AX = mybir.AxisListType
F32 = mybir.dt.float32
BF16 = mybir.dt.bfloat16
I32 = mybir.dt.int32
U32 = mybir.dt.uint32
ds = bass.ds

P = 128
N = 3125
D = 512
KT = D // P
NT = -(-N // P)
NP = NT * P
TAIL = N - (NT - 1) * P
E = 50000
H0 = 8
HD = D // H0
SUP = 2
NSUP = -(-E // (P * SUP))
NET = NSUP * SUP
ESLOT = NET * P
NX = NT - 1
NIT = NSUP + NX
EC = 4
ER = NET // EC
BIG = 1.0e30
FAR = 1 << 20
ROW = D + 2 * H0
EXW = H0 + 1
EPS = 1e-5
E0, F0, CAP0 = 8, 128, 256
E1, F1, TOP, CAP1 = 64, 256, 2, 1024
ROUTE_SCALE = 2.5
NOV = (N * TOP) // P
NI1 = E1 + NOV
assert NI1 <= P and NET % EC == 0 and ER <= P and NET * P >= E


def pairs(eng, count, body):
    for u in range(2):
        body(u, 0, u)
    with eng.Fori(1, count // 2) as k:
        for u in range(2):
            body(k * 2 + u, k, u)
    if count % 2:
        body(count - 1, count // 2, 0)


def wait(eng, sem, value):
    if not isinstance(value, int) or value > 0:
        eng.wait_ge(sem, value)


def last(n):
    return isinstance(n, int) and n == NT - 1


class Chain:

    def __init__(self, eng, sem, base=0):
        self.eng, self.sem, self.base, self.n = eng, sem, base, 0

    def __call__(self, ins):
        self.n += 1
        ins.then_inc(self.sem, 1)
        self.eng.wait_ge(self.sem, self.base + self.n)


class Phase:

    def __init__(self, nc, name):
        self.nc, self.name, self.ctx, self.sems = nc, name, ExitStack(), []

    def __enter__(self):
        self.ctx.__enter__()
        return self

    def __exit__(self, *a):
        return self.ctx.__exit__(*a)

    def sb(self, name, shape, dt=F32):
        return self.ctx.enter_context(self.nc.sbuf_tensor(f"{self.name}_{name}", shape, dt))

    def ps(self, name, shape, dt=F32):
        return self.ctx.enter_context(self.nc.psum_tensor(f"{self.name}_{name}", shape, dt))

    def sem(self, name):
        s = self.ctx.enter_context(self.nc.semaphore(f"{self.name}_{name}"))
        self.sems.append(s.num)
        return s

    def gather_sem(self, name):
        return self.nc.alloc_semaphore(f"{self.name}_{name}")

    def block(self, counted):
        if counted & set(self.sems):
            with self.nc.Block() as b:
                @b.gpsimd
                def _(g):
                    for n in sorted(counted):
                        if n - 1 not in counted:
                            end = n
                            while end in counted:
                                end += 1
                            g.sem_clear(range(n, end))
            counted.clear()
        counted |= set(self.sems)
        return self.ctx.enter_context(self.nc.Block())


class Shared:

    def __init__(self):
        self.counted = set()


class Norm:

    def __init__(self, p, nc):
        self.nc = nc
        self.st = p.sb("ln_st", [P, 6])
        self.mv = p.sb("ln_mv", [P, 2])
        self.sd = p.sb("ln_sd", [P, 2])
        self.junk = p.sb("ln_junk", [P, 1])
        self.chain = p.sem("ln_chain")
        self.var = p.sem("ln_var")
        self.root = p.sem("ln_root")

    def vector(self, v, n, x, out, done):
        ch, vv = Chain(v, self.chain, n * 3), self.nc.vector
        ch(vv.bn_stats(self.st[:], x))
        vv.tensor_scalar(self.junk[:], self.st[:, 0:1], 1.0, None, ALU.mult)
        ch(vv.bn_aggr(self.mv[:], self.st[:]))
        vv.tensor_scalar(self.sd[:, 0:1], self.mv[:, 1:2], EPS, None, ALU.add).then_inc(self.var, 1)
        v.wait_ge(self.root, n + 1)
        ch(vv.reciprocal(self.sd[:, 1:2], self.sd[:, 1:2]))
        vv.tensor_scalar(out, x, self.mv[:, 0:1], self.sd[:, 1:2], ALU.subtract, ALU.mult).then_inc(done, 1)

    def scalar(self, c, n):
        c.wait_ge(self.var, n + 1)
        self.nc.scalar.activation(self.sd[:, 1:2], self.sd[:, 0:1], ACT.Sqrt).then_inc(self.root, 1)


def build(nc, a, out, stop):
    dram = lambda name, shape, dt=F32: nc.dram_tensor(name, shape, dt, kind="Internal").ap()
    tab0 = dram("tab0", [NP, ROW])
    tabs = dram("tabs", [NP, H0])
    esrc = dram("esrc", [NSUP, SUP * P], I32)
    edst = dram("edst", [NSUP + 2, SUP * P], I32)
    xmid = dram("xmid", [NP, D])
    tab1 = dram("tab1", [NP, D + E0])
    sid = dram("sid", [E0, CAP0], I32)
    tab2 = dram("tab2", [NP, D])
    tab3 = dram("tab3", [NP, D])
    xsh = dram("xsh", [NP, D])
    ys = dram("ys", [NI1 * P, D])

    with ExitStack() as top:
        sb = lambda name, shape, dt=F32: top.enter_context(nc.sbuf_tensor(name, shape, dt))
        K = Shared()
        K.ident = sb("ident", [P, P])
        K.iota = sb("iota", [P, P])
        K.ones = sb("ones", [P, P])
        K.part = sb("part", [P, 1])
        K.src = sb("src_of_item", [P, NIT * SUP], I32)
        K.rel = sb("rel_of_item", [P, NIT * SUP])
        K.blk = sb("blk_of_item", [1, NIT], I32)
        K.junk = sb("junk", [P, D])
        K.xsup = sb("xsup", [1, NX], I32)
        phase_project(nc, K, a, tab0, tabs, esrc, edst)
        phase_tables(nc, K, esrc, edst)
        with nc.sbuf_tensor("acc", [P, NT, D + EXW], F32) as acc:
            with nc.sbuf_tensor("ex", [P, NIT * SUP, EXW], F32) as ex:
                phase_scores(nc, K, tab0, tabs, edst, ex)
                phase_aggregate(nc, K, "g0", tab0, ROW, ex, acc)
            with nc.sbuf_tensor("logits0", [P, NT, E0], F32) as lg:
                phase_attend(nc, K, a, acc, xmid, tab1, lg)
                phase_route0(nc, K, lg, tab1, sid)
        phase_experts0(nc, K, a, tab1, sid, xmid)
        if stop == 2:
            return phase_copy(nc, K, xmid, out)
        phase_norm2(nc, K, xmid, tab2)
        K.mv = sb("ln_mv3", [P, NT, 2])
        with nc.sbuf_tensor("acc1", [P, NT, D + 1], F32) as acc:
            phase_aggregate(nc, K, "g1", tab2, D, None, acc)
            phase_sage(nc, K, a, acc, tab2, xmid, K.mv)
        if stop == 3:
            return phase_copy(nc, K, xmid, out)
        K.slot = sb("slot_of_item", [P, NI1], I32)
        K.ovf = sb("ovf", [1, P], I32)
        K.nov = sb("nov", [1, 1], I32)
        K.pair = sb("pair_slot", [P, NT, TOP], I32)
        K.gate = sb("pair_gate", [P, NT, TOP])
        with nc.sbuf_tensor("scores1", [P, NT, E1], F32) as sc:
            phase_shared(nc, K, a, xmid, tab3, xsh, sc)
            phase_route1(nc, K, sc)
        phase_experts1(nc, K, a, tab3, ys)
        phase_combine(nc, K, xsh, ys, out)


def phase_project(nc, K, a, tab0, tabs, esrc, edst):
    with Phase(nc, "pj") as p:
        w = p.sb("w", [P, KT, D + 2 * H0])
        aw = p.sb("aw", [P, H0, 2 * HD])
        prod = p.sb("prod", [P, D])
        wb = p.sb("wb", [P, D])
        ab = p.sb("ab", [P, H0])
        cst = p.sb("cst", [P, 2 * H0])
        ctmp = p.sb("ctmp", [P, 2 * H0])
        xt = p.sb("xt", [P, 2, D])
        xn = p.sb("xn", [P, 2, D])
        xnT = p.sb("xnT", [P, 2, D])
        ln = Norm(p, nc)
        row = p.sb("row", [P, 2, ROW])
        pad = p.sb("pad", [1, 3, SUP * P], I32)
        psT = [p.ps(f"psT{u}", [P, D]) for u in range(2)]
        psW = [p.ps(f"psW{u}", [P, D]) for u in range(2)]
        psS = [p.ps(f"psS{u}", [P, D]) for u in range(2)]
        consts = p.sem("consts")
        idz = p.sem("idz")
        wl = p.sem("wl")
        padr = p.sem("padr")
        edge = p.sem("edge")
        wready = p.sem("wready")
        xl = [p.sem(f"xl{u}") for u in range(2)]
        normed = p.sem("normed")
        turned = p.sem("turned")
        turned_sb = p.sem("turned_sb")
        prodn = p.sem("prodn")
        evac = p.sem("evac")
        st_row = [p.sem(f"st_row{u}") for u in range(2)]
        vch = p.sem("vch")
        wch = p.sem("wch")
        b = p.block(K.counted)

        @b.gpsimd
        def _(g):
            nc.gpsimd.memset(K.ident[:], 0.0).then_inc(idz, 1)
            nc.gpsimd.iota(K.iota[:], [[1, P]], base=0, channel_multiplier=0,
                           allow_small_or_imprecise_dtypes=True).then_inc(consts, 1)
            nc.gpsimd.iota(K.part[:], [[0, 1]], base=0, channel_multiplier=1,
                           allow_small_or_imprecise_dtypes=True).then_inc(consts, 1)
            g.wait_ge(idz, 1)
            nc.gpsimd.affine_select(out=K.ident[:], in_=K.ident[:], compare_op=ALU.not_equal, fill=1.0,
                                    base=0, pattern=[[-1, P]], channel_multiplier=1).then_inc(consts, 1)
            nc.gpsimd.memset(pad[:, 0, :], 0).then_inc(padr, 1)
            nc.gpsimd.memset(pad[:, 1, :], FAR).then_inc(padr, 1)
            nc.gpsimd.memset(pad[:, 2, :], 2 * FAR).then_inc(padr, 1)

        @b.sync
        def _(s):
            for kt in range(KT):
                s.dma_start(w[:, kt, 0:D].rearrange("p (h d) -> p h d", h=H0),
                            a["L0_gnn_Ws"][:, kt * P:(kt + 1) * P, :].rearrange("h p d -> p h d")).then_inc(wl, 16)
            s.dma_start(aw[:].rearrange("p h d -> p (h d)"),
                        a["L0_gnn_a_w"].rearrange("h d -> (h d)").partition_broadcast(P)).then_inc(wl, 16)
            s.dma_start(wb[:], a["L0_gnn_Wb"].rearrange("h d -> (h d)").partition_broadcast(P)).then_inc(wl, 16)
            s.dma_start(ab[:], a["L0_gnn_a_b"].partition_broadcast(P)).then_inc(wl, 16)

            def load(n, k, u):
                wait(s, normed, n - 1)
                rows = TAIL if last(n) else P
                src = a["x"][n * P:N, :] if last(n) else a["x"][ds(n * P, P), :]
                s.dma_start(xt[0:rows, u, :], src).then_inc(xl[u], 16)
            pairs(s, NT, load)

        @b.scalar
        def _(c):
            flat = lambda t: t.rearrange("s e -> (s e)")
            c.dma_start(flat(esrc)[0:E], a["src"]).then_inc(edge, 16)
            c.dma_start(flat(edst)[SUP * P:SUP * P + E], a["dst"]).then_inc(edge, 16)
            c.wait_ge(padr, 3)
            c.dma_start(flat(esrc)[E:ESLOT].unsqueeze(0), pad[:, 0, 0:ESLOT - E]).then_inc(edge, 16)
            c.dma_start(flat(edst)[0:SUP * P].unsqueeze(0), pad[:, 2, :]).then_inc(edge, 16)
            c.dma_start(flat(edst)[SUP * P + E:SUP * P + ESLOT].unsqueeze(0),
                        pad[:, 1, 0:ESLOT - E]).then_inc(edge, 16)
            c.dma_start(flat(edst)[SUP * P + ESLOT:].unsqueeze(0), pad[:, 2, :]).then_inc(edge, 16)

            def store(n, k, u):
                c.wait_ge(evac, n + 1)
                c.dma_start(tab0[ds(n * P, P), :], row[:, u, :]).then_inc(st_row[u], 16)
                c.dma_start(tabs[ds(n * P, P), :], row[:, u, D:D + H0]).then_inc(st_row[u], 16)

            def step(n, k, u):
                if not last(n):
                    ln.scalar(c, n + 1)
                c.wait_ge(turned, n + 1)
                nc.scalar.activation(xnT[:, u, :], psT[u][:], ACT.Copy).then_inc(turned_sb, 1)
                if not (isinstance(n, int) and n == 0):
                    store(n - 1, k + u - 1, 1 - u)
            ln.scalar(c, 0)
            pairs(c, NT, step)
            store(NT - 1, NT // 2, 0)
            c.wait_ge(edge, 6 * 16)
            for u in range(2):
                c.wait_ge(st_row[u], 32 * ((NT + 1 - u) // 2))

        @b.tensor
        def _(t):
            t.wait_ge(consts, 4)

            def tile(n, k, u):
                t.wait_ge(normed, n + 1)
                for kt in range(KT):
                    ins = nc.tensor.transpose(psT[u][:, kt * P:(kt + 1) * P], xn[:, u, kt * P:(kt + 1) * P], K.ident[:])
                ins.then_inc(turned, 1)
                t.wait_ge(turned_sb, n + 1)
                wait(t, evac, n - 1)
                if isinstance(n, int) and n == 0:
                    t.wait_ge(wready, 1)
                for kt in range(KT):
                    nc.tensor.matmul(psW[u][:], xnT[:, u, kt * P:(kt + 1) * P], w[:, kt, 0:D],
                                     start=(kt == 0), stop=(kt == KT - 1))
                    ins = nc.tensor.matmul(psS[u][:, 0:2 * H0], xnT[:, u, kt * P:(kt + 1) * P], w[:, kt, D:ROW],
                                           start=(kt == 0), stop=(kt == KT - 1))
                ins.then_inc(prodn, 1)
            pairs(t, NT, tile)

        @b.vector
        def _(v):
            nc.vector.memset(K.ones[:], 1.0).then_inc(consts, 1)
            wc = Chain(v, wch)
            v.wait_ge(wl, 16 * (KT + 3))
            for kt in range(KT + 1):
                src = w[:, kt, 0:D] if kt < KT else wb[:]
                dst = w[:, kt, D:ROW] if kt < KT else ctmp[:]
                for half, col in ((1, 0), (0, H0)):
                    wc(nc.vector.tensor_tensor(prod[:].rearrange("p (h d) -> p h d", h=H0),
                                               src.rearrange("p (h d) -> p h d", h=H0),
                                               aw[:, :, half * HD:(half + 1) * HD], ALU.mult))
                    wc(nc.vector.tensor_reduce(dst[:, col:col + H0], prod[:].rearrange("p (h d) -> p h d", h=H0),
                                               AX.X, ALU.add))
            wc(nc.vector.memset(cst[:, 0:H0], 0.0))
            wc(nc.vector.tensor_tensor(ctmp[:, 0:H0], ctmp[:, 0:H0], ctmp[:, H0:2 * H0], ALU.add))
            nc.vector.tensor_tensor(cst[:, H0:2 * H0], ctmp[:, 0:H0], ab[:], ALU.add).then_inc(wready, 1)
            v.wait_ge(wready, 1)

            def norm(n, k, u):
                v.wait_ge(xl[u], k * 16 + 16)
                ln.vector(v, n, xt[:, u, :], xn[:, u, :], normed)

            def evacuate(n, k, u):
                v.wait_ge(prodn, n + 1)
                wait(v, st_row[u], k * 32)
                nc.vector.tensor_tensor(row[:, u, 0:D], psW[u][:], wb[:], ALU.add)
                nc.vector.tensor_tensor(row[:, u, D:ROW], psS[u][:, 0:2 * H0], cst[:], ALU.add).then_inc(evac, 1)

            def step(n, k, u):
                if not last(n):
                    norm(n + 1, k + u, 1 - u)
                evacuate(n, k, u)
            norm(0, 0, 0)
            pairs(v, NT, step)


def phase_tables(nc, K, esrc, edst):
    with Phase(nc, "tb") as p:
        rowi = p.sb("rowi", [ER, 2, EC, P], I32)
        rowf = p.sb("rowf", [ER, 2, EC, P])
        cnt = p.sb("cnt", [ER, NX])
        xst = p.sb("xst", [NX, 1])
        xsti = p.sb("xsti", [NX, 4], I32)
        xsupf = p.sb("xsupf", [NX, 1])
        xi = p.sb("xi", [NX, 2, SUP * P], I32)
        xf = p.sb("xf", [NX, 2, SUP * P])
        xlow = p.sb("xlow", [NX, 1])
        xbad = p.sb("xbad", [NX, 1])
        xrel = p.sb("xrel", [NX, SUP * P])
        b0i = p.sb("b0i", [1, NSUP], I32)
        b0f = p.sb("b0f", [1, NSUP])
        xsf = p.sb("xsf", [1, NX])
        dstT = p.sb("dstT", [P, NET])
        psA = [p.ps(f"psA{u}", [P, D]) for u in range(2)]
        psC = p.ps("psC", [P, D])
        psR = p.ps("psR", [P, D])
        psX = p.ps("psX", [P, D])
        psY = p.ps("psY", [P, D])
        ld = p.sem("ld")
        fx = p.sem("fx")
        lowr = p.sem("lowr")
        cntd = p.sem("cntd")
        turned = p.sem("turned")
        gat = p.gather_sem("gat")
        xin = p.sem("xin")
        vch = p.sem("vch")
        vall = p.sem("vall")
        bcast = p.sem("bcast")
        flat = lambda t: t.rearrange("s e -> (s e)")
        tiles = lambda t: t.rearrange("(c r e) -> r c e", c=EC, e=P)
        b = p.block(K.counted)

        @b.sync
        def _(s):
            s.dma_start(rowi[:, 0], tiles(flat(esrc))).then_inc(ld, 16)
            s.dma_start(rowi[:, 1], tiles(flat(edst)[SUP * P:SUP * P + ESLOT])).then_inc(ld, 16)
            with nc.allow_non_contiguous_dma(reason="one word per super tile"):
                s.dma_start(b0i[:], edst[1:1 + NSUP, 0:1].rearrange("s o -> o s")).then_inc(ld, 16)

        @b.gpsimd
        def _(g):
            nc.gpsimd.iota(xlow[:], [[0, 1]], base=P, channel_multiplier=P,
                           allow_small_or_imprecise_dtypes=True).then_inc(lowr, 1)
            g.wait_ge(xin, 1)
            g.indirect_dma_start(xi[:, 0, :], None, esrc, bass.IndirectOffsetOnAxis(xsti[:, 2:3], 0)).then_inc(gat, 16)
            g.indirect_dma_start(xi[:, 1, :], None, edst, bass.IndirectOffsetOnAxis(xsti[:, 3:4], 0)).then_inc(gat, 16)
            g.wait_ge(gat, 32)

        @b.tensor
        def _(t):
            t.wait_ge(fx, 2)
            for c in range(EC):
                for w in range(2):
                    ins = nc.tensor.transpose(psA[w][:, c * P:c * P + ER], rowf[:, w, c, :], K.ident[0:ER, 0:ER])
            ins.then_inc(turned, 1)
            t.wait_ge(cntd, 1)
            nc.tensor.matmul(psC[0:NX, 0:1], cnt[:], K.ones[0:ER, 0:1], start=True, stop=True).then_inc(turned, 1)
            nc.tensor.matmul(psR[0:1, 0:NX], K.ones[0:ER, 0:1], cnt[:], start=True, stop=True).then_inc(turned, 1)
            t.wait_ge(fx, 3)
            nc.tensor.matmul(psY[:, 0:NSUP], K.ones[0:1, :], b0f[:], start=True, stop=True).then_inc(turned, 1)
            t.wait_ge(fx, 4)
            for h in range(SUP):
                nc.tensor.transpose(psX[:, h * NX:(h + 1) * NX], xf[:, 0, h * P:(h + 1) * P], K.ident[0:NX, 0:NX])
                ins = nc.tensor.transpose(psX[:, 128 + h * NX:128 + (h + 1) * NX], xrel[:, h * P:(h + 1) * P],
                                          K.ident[0:NX, 0:NX])
            ins.then_inc(turned, 1)

        @b.vector
        def _(v):
            ch = Chain(v, vch)
            vv = nc.vector
            v.wait_ge(ld, 48)
            vv.tensor_copy(rowf[:, 0], rowi[:, 0]).then_inc(fx, 1)
            vv.tensor_copy(rowf[:, 1], rowi[:, 1]).then_inc(fx, 1)
            v.wait_ge(fx, 2)
            for x in range(NX):
                ins = vv.tensor_scalar(K.junk[0:ER, :], rowf[:, 1].rearrange("p c e -> p (c e)"), float((x + 1) * P), 0.0,
                                       ALU.is_lt, ALU.add, accum_out=cnt[:, x:x + 1])
                if x < NX - 1:
                    ch(ins)
            ins.then_inc(cntd, 1)
            ch(vv.tensor_single_scalar(K.blk[0:1, 0:NSUP], b0i[:], 7, ALU.arith_shift_right))
            ch(vv.tensor_copy(b0f[:], K.blk[0:1, 0:NSUP]))
            vv.tensor_scalar(b0f[:], b0f[:], float(P), None, ALU.mult).then_inc(fx, 1)
            for x in range(NX):
                vv.memset(K.blk[0:1, NSUP + x:NSUP + x + 1], x + 1)
            v.wait_ge(turned, 1)
            for c in range(EC):
                vv.tensor_copy(K.src[:, c * ER:(c + 1) * ER], psA[0][:, c * P:c * P + ER])
                ch(vv.tensor_copy(dstT[:, c * ER:(c + 1) * ER], psA[1][:, c * P:c * P + ER]))
            v.wait_ge(turned, 3)
            ch(vv.tensor_copy(xsti[:, 0:1], psC[0:NX, 0:1]))
            ch(vv.tensor_single_scalar(xsti[:, 2:3], xsti[:, 0:1], 8, ALU.arith_shift_right))
            ch(vv.tensor_copy(xst[:], xsti[:, 2:3]))
            ch(vv.tensor_scalar(xst[:], xst[:], 1.0, None, ALU.add))
            vv.tensor_copy(xsti[:, 3:4], xst[:]).then_inc(xin, 1)
            ch(vv.tensor_copy(K.xsup[:], psR[0:1, 0:NX]))
            ch(vv.tensor_single_scalar(K.xsup[:], K.xsup[:], 8, ALU.arith_shift_right))
            v.wait_ge(turned, 4)
            vv.tensor_tensor(K.rel[:, 0:NET].rearrange("p (s h) -> p s h", h=SUP),
                             dstT[:].rearrange("p (s h) -> p s h", h=SUP),
                             psY[:, 0:NSUP].unsqueeze(2).to_broadcast([P, NSUP, SUP]), ALU.subtract)
            v.wait_ge(gat, 32)
            v.wait_ge(lowr, 1)
            ch(vv.tensor_copy(xf[:], xi[:]))
            ch(vv.tensor_scalar(xbad[:], xf[:, 1, 0:1], xlow[:], float(FAR), ALU.is_ge, ALU.mult))
            ch(vv.tensor_tensor(xbad[:], xbad[:], xlow[:], ALU.subtract))
            vv.tensor_scalar(xrel[:], xf[:, 1, :], xbad[:], None, ALU.add).then_inc(fx, 1)
            v.wait_ge(turned, 5)
            for h in range(SUP):
                vv.tensor_copy(K.src[:, NET + h::SUP], psX[:, h * NX:(h + 1) * NX])
                ch(vv.tensor_copy(K.rel[:, NET + h::SUP], psX[:, 128 + h * NX:128 + (h + 1) * NX]))


def phase_scores(nc, K, tab0, tabs, edst, ex):
    NI = NIT * SUP
    with Phase(nc, "sc") as p:
        S = p.sb("S", [P, NI, H0])
        M = p.sb("M", [P, NI, H0])
        T = p.sb("T", [P, NI, H0])
        tT = p.sb("tT", [P, NT, H0])
        oh = p.sb("oh", [P, 2, SUP, P])
        ohT = p.sb("ohT", [P, 2, SUP, P])
        SR = p.sb("SR", [ER, EC, H0, P])
        FR = p.sb("FR", [ER, EC, H0, P])
        BR = p.sb("BR", [ER, EC, H0, P])
        di = p.sb("di", [ER, 3, EC, P], I32)
        dn = p.sb("dn", [ER, 3, EC, P])
        pen = p.sb("pen", [ER, 2, EC, P])
        pent = p.sb("pent", [ER, 2, EC, H0])
        carry = p.sb("carry", [H0, 2, NET + 2])
        seq = p.sb("seq", [H0, 2, NET])
        pq = p.sb("pq", [H0, 2, NET])
        cin = p.sb("cin", [ER, 2, EC, H0])
        last_ = p.sb("last_", [ER, 2, EC, H0])
        psO = [p.ps(f"psO{u}", [P, D]) for u in range(2)]
        psT = [p.ps(f"psT{u}", [P, D]) for u in range(2)]
        psS = [p.ps(f"psS{u}", [P, D]) for u in range(4)]
        ld = p.sem("ld"); got = p.gather_sem("got"); ohd = p.sem("ohd"); oht = p.sem("oht"); ohc = p.sem("ohc")
        tdone = p.sem("tdone"); tcop = p.sem("tcop"); vch = p.sem("vch"); st = p.sem("st"); sc = p.sem("sc")
        mt = p.sem("mt"); mc = p.sem("mc"); sx = p.sem("sx"); sy = p.sem("sy"); zr = p.sem("zr"); er = p.sem("er")
        xch = p.sem("xch")
        flat = lambda t: t.rearrange("s e -> (s e)")
        tiles = lambda t: t.rearrange("(c r e) -> r c e", c=EC, e=P)
        b = p.block(K.counted)

        @b.sync
        def _(s):
            s.dma_start(tT[:], tab0[:, D + H0:ROW].rearrange("(t p) h -> p t h", p=P)).then_inc(ld, 16)
            for j in range(3):
                s.dma_start(di[:, j], tiles(flat(edst)[SUP * P - 1 + j:SUP * P - 1 + j + ESLOT])).then_inc(ld, 16)

        @b.gpsimd
        def _(g):
            for j in range(NET):
                g.indirect_dma_start(S[:, j, :], None, tabs,
                                     bass.IndirectOffsetOnAxis(K.src[:, j:j + 1], 0)).then_inc(got, 16)
            g.wait_ge(got, 16 * NET)

        @b.tensor
        def _(t):
            tens = nc.tensor
            t.wait_ge(ld, 64)

            def tscore(n, k, u):
                t.wait_ge(ohd, n + 1)
                blk = t.value_load(K.blk[0:1, ds(n, 1)], min_val=0, max_val=NT - 1)
                for h in range(SUP):
                    ins = tens.transpose(psO[u][:, h * P:(h + 1) * P], oh[:, u, h, :], K.ident[:])
                ins.then_inc(oht, 1)
                t.wait_ge(ohc, n + 1)
                wait(t, tcop, n - 1)
                for h in range(SUP):
                    ins = tens.matmul(psT[u][:, h * H0:(h + 1) * H0], ohT[:, u, h, :],
                                      tT[:, ds(blk, 1), :], start=True, stop=True)
                ins.then_inc(tdone, 1)
            pairs(t, NIT, tscore)
            t.wait_ge(got, 16 * NET)
            for h in range(H0):
                q = h % 4
                wait(t, sc, h - 3)
                for c in range(EC):
                    ins = tens.transpose(psS[q][0:ER, c * P:(c + 1) * P], S[:, c * ER:(c + 1) * ER, h], K.ident[:])
                ins.then_inc(st, 1)
            t.wait_ge(sx, 1)
            for d in range(2):
                for c in range(EC):
                    tens.transpose(psO[d][0:H0, c * ER:(c + 1) * ER], last_[:, d, c, :], K.ident[0:ER, 0:ER])
                    ins = tens.transpose(psT[d][0:H0, c * ER:(c + 1) * ER], pent[:, d, c, :], K.ident[0:ER, 0:ER])
            ins.then_inc(sy, 1)
            t.wait_ge(sx, 2)
            for d in range(2):
                for c in range(EC):
                    ins = tens.transpose(psS[0][0:ER, (d * EC + c) * H0:(d * EC + c + 1) * H0],
                                         carry[:, d, 2 * d + c * ER:2 * d + (c + 1) * ER], K.ident[0:H0, 0:H0])
            ins.then_inc(sy, 1)
            for h in range(H0):
                q = h % 4
                t.wait_ge(sx, 3 + h)
                wait(t, mc, h - 3)
                for c in range(EC):
                    ins = tens.transpose(psS[q][:, c * P:c * P + ER], FR[:, c, h, :], K.ident[0:ER, 0:ER])
                ins.then_inc(mt, 1)

        @b.scalar
        def _(c_):
            sc_ = nc.scalar

            def copy(n, k, u):
                c_.wait_ge(oht, n + 1)
                wait(c_, tdone, n - 1)
                sc_.activation(ohT[:, u], psO[u][:, 0:SUP * P].rearrange("p (h e) -> p h e", h=SUP),
                               ACT.Copy).then_inc(ohc, 1)
            pairs(c_, NIT, copy)
            for h in range(H0):
                c_.wait_ge(st, h + 1)
                sc_.activation(SR[:, :, h, :], psS[h % 4][0:ER, :].rearrange("p (c e) -> p c e", c=EC),
                               ACT.Copy).then_inc(sc, 1)
            for h in range(H0):
                c_.wait_ge(mt, h + 1)
                sc_.activation(M[:, 0:NET, h].rearrange("p (c r) -> p c r", c=EC),
                               psS[h % 4][:, :].rearrange("p (c e) -> p c e", c=EC)[:, :, 0:ER],
                               ACT.Copy).then_inc(mc, 1)
            c_.wait_ge(zr, 1)
            sc_.activation(ex[:, :, 0:H0], S[:], ACT.Exp).then_inc(er, 1)
            c_.wait_ge(er, 1)

        @b.vector
        def _(v):
            vv = nc.vector
            ch = Chain(v, vch)
            v.wait_ge(ld, 64)
            ch(vv.tensor_copy(dn[:], di[:]))
            for d in range(2):
                vv.tensor_tensor(pen[:, d], dn[:, 1], dn[:, 2 * d], ALU.not_equal)
            ch(vv.memset(ex[:, :, H0:EXW], 1.0))
            ch(vv.tensor_scalar(pen[:], pen[:], -BIG, None, ALU.mult))
            for d in range(2):
                ch(vv.tensor_reduce(cin[:, d, :, 0:1], pen[:, d], AX.X, ALU.min))
            ch(vv.tensor_copy(pent[:], cin[:, :, :, 0:1].to_broadcast([ER, 2, EC, H0])))

            def onehot(n, k, u):
                wait(v, oht, n - 1)
                for h in range(SUP):
                    ins = vv.tensor_scalar(oh[:, u, h, :], K.iota[:], K.rel[:, ds(n * SUP + h, 1)], None, ALU.is_equal)
                ins.then_inc(ohd, 1)

            def tcopy(n, k, u):
                v.wait_ge(tdone, n + 1)
                vv.tensor_scalar(T[:, ds(n * SUP, SUP), :], psT[u][:, 0:SUP * H0].rearrange("p (h e) -> p h e", h=SUP),
                                 0.0, None, ALU.add).then_inc(tcop, 1)

            def step(n, k, u):
                if not isinstance(n, int) or n < NIT - 1:
                    onehot(n + 1, k, 1 - u)
                tcopy(n, k, u)
            onehot(0, 0, 0)
            for u in range(2):
                step(u, 0, u)
            with v.Fori(1, NIT // 2 - 1) as k:
                for u in range(2):
                    step(k * 2 + u, k, u)
            for u in range(2):
                step(NIT - 2 + u, 0, u)
            v.wait_ge(tcop, NIT)

            v.wait_ge(sc, H0)
            out2 = (FR, BR)
            rev = lambda t, d: t if d == 0 else t[:, ::-1]

            def scans(first):
                for h in range(H0):
                    for c in range(EC):
                        for d in range(2):
                            init = -BIG if first else cin[:, d, c, h:h + 1]
                            ins = vv.tensor_tensor_scan(rev(out2[d][:, c, h, :], d), rev(pen[:, d, c, :], d),
                                                        rev(SR[:, c, h, :], d), init, ALU.add, ALU.max)
                    ch(ins)
                    if not first:
                        vv.tensor_tensor(FR[:, :, h, :], FR[:, :, h, :], BR[:, :, h, :], ALU.max).then_inc(sx, 1)
            scans(True)
            vv.tensor_copy(last_[:, 0], FR[:, :, :, P - 1])
            vv.tensor_copy(last_[:, 1], BR[:, :, :, 0]).then_inc(sx, 1)
            v.wait_ge(sy, 1)
            ch(vv.memset(carry[:], -BIG))
            for d in range(2):
                vv.tensor_copy(seq[:, d, :], psO[d][0:H0, 0:NET])
                ch(vv.tensor_copy(pq[:, d, :], psT[d][0:H0, 0:NET]))
            for d in range(2):
                ins = vv.tensor_tensor_scan(rev(carry[:, d, 1:1 + NET], d), rev(pq[:, d, :], d),
                                            rev(seq[:, d, :], d), -BIG, ALU.add, ALU.max)
            ins.then_inc(sx, 1)
            v.wait_ge(sy, 2)
            ch(vv.tensor_copy(cin[:], psS[0][0:ER, 0:2 * EC * H0].rearrange("p (d c h) -> p d c h", d=2, c=EC)))
            scans(False)
            v.wait_ge(mc, H0)

            def repeat(x, k, u):
                r = v.value_load(K.xsup[0:1, ds(x, 1)], min_val=0, max_val=NSUP - 1)
                for t in (S, M):
                    ins = vv.tensor_scalar(t[:, ds(x * SUP + NET, SUP), :], t[:, ds(r * SUP, SUP), :], 0.0, None, ALU.add)
                ins.then_inc(xch, 1)
            pairs(v, NX, repeat)
            v.wait_ge(xch, NX)
            for t in (S, M):
                ins = vv.tensor_tensor(t[:], t[:], T[:], ALU.add)
            ch(ins)
            for t in (S, M):
                ins = vv.scalar_tensor_tensor(t[:], t[:], 0.2, t[:], ALU.mult, ALU.max)
            ch(ins)
            vv.tensor_tensor(S[:], S[:], M[:], ALU.subtract).then_inc(zr, 1)


GQ = 4


def phase_aggregate(nc, K, name, table, row, ex, acc):
    with Phase(nc, name) as p:
        nw = EXW if ex is not None else 1
        G = p.sb("G", [P, GQ, SUP, row])
        oh = p.sb("oh", [P, 2, SUP, P])
        psA = [p.ps(f"psA{u}", [P, D]) for u in range(2)]
        psB = [p.ps(f"psB{u}", [P, D]) for u in range(2)]
        got = [p.gather_sem(f"got{q}") for q in range(GQ)]
        ready = p.sem("ready")
        summed = p.sem("summed")
        added = p.sem("added")
        zero = p.sem("zero")
        one = p.sem("one")
        b = p.block(K.counted)

        def quads(eng, body):
            for q in range(GQ):
                body(q, 0, q)
            with eng.Fori(1, NIT // GQ - 1) as k:
                for q in range(GQ):
                    body(k * GQ + q, k, q)
            for q in range(GQ):
                body(NIT - GQ + q, NIT // GQ - 1, q)
        assert NIT % GQ == 0

        @b.gpsimd
        def _(g):
            for n in range(NIT):
                q = n % GQ
                wait(g, summed, n - GQ + 1)
                for h in range(SUP):
                    j = n * SUP + h
                    g.indirect_dma_start(G[:, q, h, :], None, table,
                                         bass.IndirectOffsetOnAxis(K.src[:, j:j + 1], 0)).then_inc(got[q], 16)

        @b.tensor
        def _(t):
            def item(n, k, q):
                u = q % 2
                t.wait_ge(ready, n + 1)
                if ex is None:
                    t.wait_ge(got[q], k * 32 + 32)
                wait(t, added, n - 1)
                for h in range(SUP):
                    nc.tensor.matmul(psA[u][:], oh[:, u, h, :], G[:, q, h, 0:D], start=(h == 0), stop=(h == SUP - 1))
                for h in range(SUP):
                    w = K.ones[:, 0:1] if ex is None else ex[:, ds(n * SUP + h, 1), :]
                    ins = nc.tensor.matmul(psB[u][:, 0:nw], oh[:, u, h, :], w, start=(h == 0), stop=(h == SUP - 1))
                ins.then_inc(summed, 1)
            quads(t, item)

        @b.vector
        def _(v):
            vv = nc.vector
            vv.memset(acc[:, :, 0:D + nw], 0.0).then_inc(zero, 1)
            v.wait_ge(zero, 1)

            def prep(n, k, q):
                u = q % 2
                wait(v, summed, n - 1)
                for h in range(SUP):
                    ins = vv.tensor_scalar(oh[:, u, h, :], K.iota[:], K.rel[:, ds(n * SUP + h, 1)], None, ALU.is_equal)
                if ex is not None:
                    v.wait_ge(got[q], k * 32 + 32)
                    for h in range(SUP):
                        rows = G[:, q, h, 0:D].rearrange("p (h d) -> p h d", h=H0)
                        w = ex[:, ds(n * SUP + h, 1), 0:H0].rearrange("p o h -> p (o h)").unsqueeze(2)
                        ins = vv.tensor_tensor(rows, rows, w.to_broadcast([P, H0, HD]), ALU.mult)
                ins.then_inc(ready, 1)

            def add(n, k, q):
                u = q % 2
                blk = v.value_load(K.blk[0:1, ds(n, 1)], min_val=0, max_val=NT - 1)
                v.wait_ge(summed, n + 1)
                wait(v, added, n)
                a1 = acc[:, ds(blk, 1), 0:D].rearrange("p o d -> p (o d)")
                a2 = acc[:, ds(blk, 1), D:D + nw].rearrange("p o d -> p (o d)")
                vv.tensor_tensor(a1, a1, psA[u][:], ALU.add)
                vv.tensor_tensor(a2, a2, psB[u][:, 0:nw], ALU.add).then_inc(added, 1)

            def step(n, k, q):
                if not isinstance(n, int) or n < NIT - 1:
                    prep(n + 1, k + (q + 1) // GQ, (q + 1) % GQ)
                add(n, k, q)
            prep(0, 0, 0)
            quads(v, step)
            v.wait_ge(added, NIT)


def phase_copy(nc, K, src, out):
    with Phase(nc, "cp") as p:
        d = p.sem("d")
        b = p.block(K.counted)

        @b.sync
        def _(s):
            s.dma_start(out, src[0:N]).then_inc(d, 16)
            s.wait_ge(d, 16)


def rows_of(n):
    return TAIL if last(n) else P


def tile_rows(t, n):
    return t[n * P:N, :] if last(n) else t[ds(n * P, P), :]


def phase_attend(nc, K, a, acc, xmid, tab1, lg):
    with Phase(nc, "at") as p:
        wr = p.sb("wr", [P, KT, E0])
        xt = p.sb("xt", [P, 2, D])
        x1 = p.sb("x1", [P, 2, D])
        den = p.sb("den", [P, NT, H0])
        xn = p.sb("xn", [P, 2, D])
        xnT = p.sb("xnT", [P, 2, D])
        psT = [p.ps(f"psT{u}", [P, D]) for u in range(2)]
        psL = [p.ps(f"psL{u}", [P, D]) for u in range(2)]
        ln = Norm(p, nc)
        wl = p.sem("wl"); normed = p.sem("normed"); turned = p.sem("turned"); copied = p.sem("copied")
        prod = p.sem("prod"); read = p.sem("read"); vch = p.sem("vch"); dch = p.sem("dch")
        xl = [p.sem(f"xl{u}") for u in range(2)]
        st = [p.sem(f"st{u}") for u in range(2)]
        b = p.block(K.counted)

        @b.sync
        def _(s):
            s.dma_start(wr[:], a["L0_ffn_Wr"].rearrange("(kt p) e -> p kt e", p=P)).then_inc(wl, 16)

            def load(n, k, u):
                wait(s, normed, n - 1)
                s.dma_start(xt[0:rows_of(n), u, :], tile_rows(a["x"], n)).then_inc(xl[u], 16)
            pairs(s, NT, load)

        @b.scalar
        def _(c):
            def step(n, k, u):
                ln.scalar(c, n)
                c.wait_ge(normed, n + 1)
                c.dma_start(xmid[ds(n * P, P), :], x1[:, u, :]).then_inc(st[u], 16)
                c.dma_start(tab1[ds(n * P, P), 0:D], xn[:, u, :]).then_inc(st[u], 16)
                c.wait_ge(turned, n + 1)
                nc.scalar.activation(xnT[:, u, :], psT[u][:], ACT.Copy).then_inc(copied, 1)
            pairs(c, NT, step)
            for u in range(2):
                c.wait_ge(st[u], 32 * ((NT + 1 - u) // 2))

        @b.tensor
        def _(t):
            t.wait_ge(wl, 16)

            def tile(n, k, u):
                t.wait_ge(normed, n + 1)
                for kt in range(KT):
                    ins = nc.tensor.transpose(psT[u][:, kt * P:(kt + 1) * P], xn[:, u, kt * P:(kt + 1) * P], K.ident[:])
                ins.then_inc(turned, 1)
                t.wait_ge(copied, n + 1)
                wait(t, read, n - 1)
                for kt in range(KT):
                    ins = nc.tensor.matmul(psL[u][:, 0:E0], xnT[:, u, kt * P:(kt + 1) * P], wr[:, kt, :],
                                           start=(kt == 0), stop=(kt == KT - 1))
                ins.then_inc(prod, 1)
            pairs(t, NT, tile)

        @b.vector
        def _(v):
            vv = nc.vector
            d = Chain(v, dch)
            d(vv.tensor_scalar(den[:], acc[:, :, D:D + H0], 1e-30, None, ALU.max))
            d(vv.reciprocal(den[:], den[:]))

            def norm(n, k, u):
                v.wait_ge(xl[u], k * 16 + 16)
                wait(v, st[u], k * 32)
                ch = Chain(v, vch, n * 2)
                o = x1[:, u, :]
                ch(vv.tensor_tensor(o.rearrange("p (h d) -> p h d", h=H0),
                                    acc[:, ds(n, 1), 0:D].rearrange("p o (h d) -> p (o h) d", h=H0),
                                    den[:, ds(n, 1), :].rearrange("p o h -> p (o h)").unsqueeze(2)
                                    .to_broadcast([P, H0, HD]), ALU.mult))
                ch(vv.tensor_tensor(o, o, xt[:, u, :], ALU.add))
                ln.vector(v, n, o, xn[:, u, :], normed)

            def step(n, k, u):
                if not last(n):
                    norm(n + 1, k + u, 1 - u)
                v.wait_ge(prod, n + 1)
                vv.tensor_scalar(lg[:, ds(n, 1), :].rearrange("p o e -> p (o e)"), psL[u][:, 0:E0], 0.0, None,
                                 ALU.add).then_inc(read, 1)
            norm(0, 0, 0)
            pairs(v, NT, step)
            v.wait_ge(read, NT)


def phase_route0(nc, K, lg, tab1, sid):
    BITS = 30
    W = NT * E0
    S = 16
    with Phase(nc, "r0") as p:
        pv = p.sb("pv", [P, 1])
        v_ = p.sb("v", [P, NT, E0])
        m8 = p.sb("m8", [P, E0])
        m1 = p.sb("m1", [E0, 1])
        dg = p.sb("dg", [E0, E0])
        rs = p.sb("rs", [P, E0])
        thr = p.sb("thr", [P, E0], I32)
        cand = p.sb("cand", [P, E0], I32)
        bit = p.sb("bit", [P, 1], I32)
        msk = p.sb("msk", [P, E0], I32)
        hit = p.sb("hit", [P, NT, E0])
        gt = p.sb("gt", [P, NT, E0])
        need = p.sb("need", [P, E0])
        tot = p.sb("tot", [P, NT, E0])
        inc = p.sb("inc", [P, NT, E0])
        rank = p.sb("rank", [P, NT, E0])
        zero = p.sb("zero", [P, NT])
        tri = p.sb("tri", [P, P])
        ri = p.sb("ri", [P, 3, NT, E0], I32)
        rf = p.sb("rf", [P, 2, NT, E0])
        tio = p.sb("tio", [P, NT])
        oa = p.sb("oa", [P, W, S], BF16)
        ob = p.sb("ob", [P, W, 2, S], BF16)
        obm = p.sb("obm", [P, W, S], BF16)
        idf = p.sb("idf", [S, E0, S])
        idi = p.sb("idi", [S, E0, S], I32)
        ps = [p.ps(f"ps{u}", [P, D]) for u in range(4)]
        psC = [p.ps(f"psC{u}", [P, D]) for u in range(2)]
        g1 = p.sem("g1"); vch = p.sem("vch"); tv = p.sem("tv"); vt = p.sem("vt"); ex = p.sem("ex"); xe = p.sem("xe")
        lc = p.sem("lc"); cs = p.sem("cs"); cd = p.sem("cd"); dd = p.sem("dd"); st = p.sem("st")
        b = p.block(K.counted)

        @b.gpsimd
        def _(g):
            nc.gpsimd.affine_select(out=tri[:], in_=K.ones[:], compare_op=ALU.is_gt, fill=0.0, base=0,
                                    pattern=[[1, P]], channel_multiplier=-1).then_inc(g1, 1)
            nc.gpsimd.iota(tio[:], [[1, NT]], base=0, channel_multiplier=0,
                           allow_small_or_imprecise_dtypes=True).then_inc(g1, 1)

        @b.sync
        def _(s):
            s.wait_ge(dd, 1)
            s.dma_start(tab1[:, D:D + E0].rearrange("(t p) e -> p t e", p=P), v_[:]).then_inc(st, 16)
            s.wait_ge(dd, 2)
            s.dma_start(sid.rearrange("e (a b) -> a e b", b=S), idi[:]).then_inc(st, 16)
            s.wait_ge(st, 32)

        @b.scalar
        def _(c):
            c.wait_ge(ex, 1)
            nc.scalar.activation(v_[:], v_[:], ACT.Exp).then_inc(xe, 1)

        flat = lambda t: t[:].rearrange("p t e -> p (t e)")

        @b.tensor
        def _(t):
            tens = nc.tensor
            t.wait_ge(tv, 1)
            tens.transpose(ps[0][0:E0, 0:P], m8[:], K.ident[:]).then_inc(vt, 1)
            t.wait_ge(tv, 2)
            tens.matmul(ps[1][:, 0:E0], K.ones[0:E0, :], dg[:], start=True, stop=True).then_inc(vt, 1)
            t.wait_ge(tv, 3)
            tens.matmul(ps[2][:, 0:E0], K.ones[:], rs[:], start=True, stop=True).then_inc(vt, 1)

            def count(n, k, u):
                t.wait_ge(cs, n + 1)
                tens.matmul(psC[u][:, 0:E0], K.ones[:], m8[:], start=True, stop=True).then_inc(cd, 1)
            pairs(t, BITS, count)
            t.wait_ge(tv, 4)
            t.wait_ge(g1, 2)
            tens.matmul(ps[0][:, 0:E0], K.ones[:], m8[:], start=True, stop=True)
            tens.matmul(ps[1][:, 0:W], tri[:], flat(hit), start=True, stop=True)
            tens.matmul(ps[2][:, 0:W], K.ones[:], flat(hit), start=True, stop=True).then_inc(vt, 1)
            t.wait_ge(tv, 5)
            tens.matmul(ps[1][:, 0:W], tri[:], flat(hit), start=True, stop=True)
            tens.matmul(ps[2][:, 0:W], K.ones[:], flat(hit), start=True, stop=True).then_inc(vt, 1)
            t.wait_ge(tv, 6)
            for e in range(E0):
                for k in range(NT):
                    ins = tens.matmul(ps[3][0:S, e * 2 * S:(e + 1) * 2 * S], oa[:, k * E0 + e, :],
                                      ob[:, k * E0 + e, :, :].rearrange("p a b -> p (a b)"),
                                      start=(k == 0), stop=(k == NT - 1))
            ins.then_inc(vt, 1)

        @b.vector
        def _(v):
            vv = nc.vector
            ch = Chain(v, vch)
            eh = lambda t: t[:].rearrange("p t e -> p e t")
            bc = lambda t: t.unsqueeze(1).to_broadcast([P, NT, E0])
            v.wait_ge(g1, 2)
            ch(vv.tensor_reduce(pv[:], K.ident[:, 0:TAIL], AX.X, ALU.add))
            ch(vv.memset(zero[:], 0.0))
            lastl = lg[:, NT - 1, :]
            ch(vv.tensor_scalar(lastl, lastl, pv[:], None, ALU.mult))
            ch(vv.tensor_scalar(rank[:, 0, 0:1], pv[:], BIG, -BIG, ALU.mult, ALU.add))
            ch(vv.tensor_scalar(lastl, lastl, rank[:, 0, 0:1], None, ALU.add))
            vv.tensor_reduce(m8[:], eh(lg), AX.X, ALU.max).then_inc(tv, 1)
            v.wait_ge(vt, 1)
            ch(vv.tensor_reduce(m1[:], ps[0][0:E0, 0:P], AX.X, ALU.max))
            vv.tensor_scalar(dg[:], K.ident[0:E0, 0:E0], m1[:], None, ALU.mult).then_inc(tv, 1)
            v.wait_ge(vt, 2)
            vv.tensor_tensor(v_[:], lg[:], bc(ps[1][:, 0:E0]), ALU.subtract).then_inc(ex, 1)
            v.wait_ge(xe, 1)
            vv.tensor_reduce(rs[:], eh(v_), AX.X, ALU.add).then_inc(tv, 1)
            v.wait_ge(vt, 3)
            ch(vv.reciprocal(need[:], ps[2][:, 0:E0]))
            vv.tensor_tensor(v_[:], v_[:], bc(need[:]), ALU.mult).then_inc(dd, 1)
            v.wait_ge(st, 16)
            ch(vv.tensor_scalar(v_[:, NT - 1, :], v_[:, NT - 1, :], pv[:], None, ALU.add))
            ch(vv.tensor_scalar(v_[:, NT - 1, :], v_[:, NT - 1, :], 1.0, None, ALU.subtract))
            ch(vv.memset(thr[:], 0))
            ch(vv.memset(bit[:], 1 << (BITS - 1)))

            def step(n, k, u):
                c = Chain(v, lc, n * 5)
                c(vv.tensor_tensor(cand[:], thr[:], bit[:].to_broadcast([P, E0]), ALU.bitwise_or))
                c(vv.tensor_tensor(hit[:], v_[:], bc(cand[:].bitcast(F32)), ALU.is_ge))
                vv.tensor_reduce(m8[:], eh(hit), AX.X, ALU.add).then_inc(cs, 1)
                v.wait_ge(cd, n + 1)
                c(vv.tensor_scalar(msk[:], psC[u][:, 0:E0], CAP0 - 0.5, -1.0, ALU.is_gt, ALU.mult))
                c(vv.scalar_tensor_tensor(thr[:], msk[:], bit[:], thr[:], ALU.bitwise_and, ALU.bitwise_or))
                c(vv.tensor_single_scalar(bit[:], bit[:], 1, ALU.logical_shift_right))
            pairs(v, BITS, step)
            tf = bc(thr[:].bitcast(F32))
            ch(vv.tensor_tensor(gt[:], v_[:], tf, ALU.is_gt))
            ch(vv.tensor_tensor(hit[:], v_[:], tf, ALU.is_equal))
            vv.tensor_reduce(m8[:], eh(gt), AX.X, ALU.add).then_inc(tv, 1)

            def ranks():
                ch(vv.tensor_copy(flat(tot), ps[2][:, 0:W]))
                for e in range(E0):
                    ins = vv.tensor_tensor_scan(inc[:, :, e], tot[:, :, e], zero[:], 0.0, ALU.add, ALU.add)
                ch(ins)
                ch(vv.tensor_tensor(inc[:], inc[:], tot[:], ALU.subtract))
                ch(vv.tensor_tensor(flat(rank), flat(inc), ps[1][:, 0:W], ALU.add))
            v.wait_ge(vt, 4)
            ch(vv.tensor_scalar(need[:], ps[0][:, 0:E0], -1.0, float(CAP0), ALU.mult, ALU.add))
            ranks()
            ch(vv.tensor_tensor(rank[:], rank[:], bc(need[:]), ALU.is_lt))
            ch(vv.tensor_tensor(hit[:], hit[:], rank[:], ALU.mult))
            vv.tensor_tensor(hit[:], hit[:], gt[:], ALU.add).then_inc(tv, 1)
            v.wait_ge(vt, 5)
            ranks()
            ch(vv.tensor_copy(ri[:, 0], rank[:]))
            ch(vv.tensor_single_scalar(ri[:, 1], ri[:, 0], 4, ALU.arith_shift_right))
            ch(vv.tensor_single_scalar(ri[:, 2], ri[:, 0], S - 1, ALU.bitwise_and))
            ch(vv.tensor_copy(rf[:], ri[:, 1:3]))
            ch(vv.tensor_scalar(gt[:], hit[:], -1000.0, 1000.0, ALU.mult, ALU.add))
            ch(vv.tensor_tensor(rf[:, 0], rf[:, 0], gt[:], ALU.add))
            io = K.iota[:, 0:S].unsqueeze(1).to_broadcast([P, W, S])
            for j, o in ((0, oa), (1, obm)):
                ch(vv.tensor_tensor(o[:], io, rf[:, j].rearrange("p t e -> p (t e)").unsqueeze(2).to_broadcast([P, W, S]),
                                    ALU.is_equal))
            ch(vv.tensor_scalar(ob[:, :, 0, :], obm[:], K.part[:], None, ALU.mult))
            vv.tensor_tensor(ob[:, :, 1, :].rearrange("p (t e) s -> p t e s", e=E0),
                             obm[:].rearrange("p (t e) s -> p t e s", e=E0),
                             tio[:].unsqueeze(2).unsqueeze(3).to_broadcast([P, NT, E0, S]), ALU.mult).then_inc(tv, 1)
            v.wait_ge(vt, 6)
            r = ps[3][0:S, 0:E0 * 2 * S].rearrange("a (e w b) -> a e w b", w=2, b=S)
            ch(vv.tensor_scalar(idf[:], r[:, :, 1, :], float(P), None, ALU.mult))
            ch(vv.tensor_tensor(idf[:], idf[:], r[:, :, 0, :], ALU.add))
            vv.tensor_copy(idi[:], idf[:]).then_inc(dd, 1)


def phase_experts0(nc, K, a, tab1, sid, xmid):
    HC = CAP0 // P
    NJ = E0 * HC
    R = D + E0
    with Phase(nc, "e0") as p:
        ix = p.sb("ix", [P, NJ], I32)
        g = p.sb("g", [P, NJ, R])
        w1 = p.sb("w1", [P, E0, KT, F0])
        w2 = p.sb("w2", [F0, E0, D])
        b1 = p.sb("b1", [F0, E0])
        b2 = p.sb("b2", [P, E0, D])
        xT = p.sb("xT", [P, 2, KT, CAP0])
        hT = p.sb("hT", [F0, 2, CAP0])
        y = p.sb("y", [P, 2, HC, D])
        psT = [p.ps(f"psT{u}", [P, D]) for u in range(4)]
        psH = [p.ps(f"psH{u}", [P, D]) for u in range(2)]
        psY = [p.ps(f"psY{u}", [P, D]) for u in range(2)]
        il = p.sem("il"); wl = p.sem("wl"); got = p.gather_sem("got"); turned = p.sem("turned"); cop = p.sem("cop")
        hd = p.sem("hd"); act = p.sem("act"); yd = p.sem("yd"); yb = p.sem("yb"); yr = p.sem("yr"); sca = p.gather_sem("sca")
        b = p.block(K.counted)

        @b.sync
        def _(s):
            with nc.allow_non_contiguous_dma(reason="slot tokens to one per partition"):
                s.dma_start(ix[:], sid.rearrange("e (c p) -> p (e c)", p=P)).then_inc(il, 16)
            for e in range(E0):
                s.dma_start(w1[:, e], a["L0_ffn_W1"][e].rearrange("(kt p) f -> p kt f", p=P)).then_inc(wl, 16)
            s.dma_start(w2[:], a["L0_ffn_W2"].rearrange("e f d -> f e d")).then_inc(wl, 16)
            with nc.allow_non_contiguous_dma(reason="biases to one per partition"):
                s.dma_start(b1[:], a["L0_ffn_b1"].rearrange("e f -> f e")).then_inc(wl, 16)
            s.dma_start(b2[:].rearrange("p e d -> p (e d)"),
                        a["L0_ffn_b2"].rearrange("e d -> (e d)").partition_broadcast(P)).then_inc(wl, 16)

        @b.gpsimd
        def _(q):
            q.wait_ge(il, 16)
            for j in range(NJ):
                q.indirect_dma_start(g[:, j, :], None, tab1,
                                     bass.IndirectOffsetOnAxis(ix[:, j:j + 1], 0)).then_inc(got, 16)
            for e in range(E0):
                q.wait_ge(yr, HC * (e + 1))
                if e:
                    q.wait_ge(sca, 16 * HC * e)
                for c in range(HC):
                    j = e * HC + c
                    q.indirect_dma_start(xmid, bass.IndirectOffsetOnAxis(ix[:, j:j + 1], 0), y[:, e % 2, c, :], None,
                                         bounds_check=NP - 1, compute_op=ALU.add).then_inc(sca, 16)
            q.wait_ge(sca, 16 * HC * E0)

        @b.tensor
        def _(t):
            tens = nc.tensor
            t.wait_ge(got, 16 * NJ)
            t.wait_ge(wl, 16 * (E0 + 3))
            for e in range(E0):
                u = e % 2
                for c in range(HC):
                    wait(t, cop, 2 * e - 1 + c)
                    for kt in range(KT):
                        ins = tens.transpose(psT[2 * u + c][:, kt * P:(kt + 1) * P],
                                             g[:, e * HC + c, kt * P:(kt + 1) * P], K.ident[:])
                    ins.then_inc(turned, 1)
                t.wait_ge(cop, HC * (e + 1))
                wait(t, act, e - 1)
                for kt in range(KT):
                    ins = tens.matmul(psH[u][:, 0:CAP0], w1[:, e, kt, :], xT[:, u, kt, :],
                                      start=(kt == 0), stop=(kt == KT - 1))
                ins.then_inc(hd, 1)
                t.wait_ge(act, e + 1)
                for c in range(HC):
                    wait(t, yb, HC * e + c - 1)
                    tens.matmul(psY[c][:], hT[:, u, c * P:(c + 1) * P], w2[:, e, :],
                                start=True, stop=True).then_inc(yd, 1)

        @b.scalar
        def _(c_):
            for e in range(E0):
                u = e % 2
                for c in range(HC):
                    c_.wait_ge(turned, HC * e + c + 1)
                    wait(c_, hd, e - 1)
                    nc.scalar.activation(xT[:, u, :, c * P:(c + 1) * P],
                                         psT[2 * u + c][:].rearrange("p (k t) -> p k t", k=KT), ACT.Copy).then_inc(cop, 1)
                c_.wait_ge(hd, e + 1)
                wait(c_, yd, HC * (e - 1))
                nc.scalar.activation(hT[:, u, :], psH[u][:, 0:CAP0], ACT.Gelu, bias=b1[:, e:e + 1]).then_inc(act, 1)
                for c in range(HC):
                    c_.wait_ge(yb, HC * e + c + 1)
                    j = e * HC + c
                    nc.scalar.activation(y[:, u, c, :], y[:, u, c, :], ACT.Copy,
                                         scale=g[:, j, D + e:D + e + 1]).then_inc(yr, 1)

        @b.vector
        def _(v):
            for e in range(E0):
                for c in range(HC):
                    v.wait_ge(yd, HC * e + c + 1)
                    wait(v, sca, 16 * HC * (e - 1))
                    nc.vector.tensor_tensor(y[:, e % 2, c, :], psY[c][:], b2[:, e, :], ALU.add).then_inc(yb, 1)


def phase_norm2(nc, K, xmid, tab2):
    with Phase(nc, "n2") as p:
        xt = p.sb("xt", [P, 2, D])
        xn = p.sb("xn", [P, 2, D])
        ln = Norm(p, nc)
        normed = p.sem("normed")
        xl = [p.sem(f"xl{u}") for u in range(2)]
        st = [p.sem(f"st{u}") for u in range(2)]
        b = p.block(K.counted)

        @b.sync
        def _(s):
            def load(n, k, u):
                wait(s, normed, n - 1)
                s.dma_start(xt[:, u, :], xmid[ds(n * P, P), :]).then_inc(xl[u], 16)
            pairs(s, NT, load)

        @b.scalar
        def _(c):
            def step(n, k, u):
                ln.scalar(c, n)
                c.wait_ge(normed, n + 1)
                c.dma_start(tab2[ds(n * P, P), :], xn[:, u, :]).then_inc(st[u], 16)
            pairs(c, NT, step)
            for u in range(2):
                c.wait_ge(st[u], 16 * ((NT + 1 - u) // 2))

        @b.vector
        def _(v):
            def step(n, k, u):
                v.wait_ge(xl[u], k * 16 + 16)
                wait(v, st[u], k * 16)
                ln.vector(v, n, xt[:, u, :], xn[:, u, :], normed)
            pairs(v, NT, step)


def phase_sage(nc, K, a, acc, tab2, xmid, mv):
    with Phase(nc, "sg") as p:
        w = p.sb("w", [P, 2 * KT, D])
        bb = p.sb("bb", [P, D])
        deg = p.sb("deg", [P, NT, 1])
        xt = p.sb("xt", [P, 2, D])
        xn = p.sb("xn", [P, 2, 2, D])
        xT = p.sb("xT", [P, 2, 2 * KT, P])
        h = p.sb("h", [P, 2, D])
        sg = p.sb("sg", [P, 2, D])
        x3 = p.sb("x3", [P, 2, D])
        bst = p.sb("bst", [P, 6])
        junk = p.sb("junk", [P, 1])
        bmv = p.sb("bmv", [P, 2])
        psT = [p.ps(f"psT{u}", [P, D]) for u in range(4)]
        psH = [p.ps(f"psH{u}", [P, D]) for u in range(2)]
        wl = p.sem("wl"); md = p.sem("md"); turned = p.sem("turned"); cop = p.sem("cop"); prod = p.sem("prod")
        hs = p.sem("hs"); sgd = p.sem("sgd"); xd = p.sem("xd"); vch = p.sem("vch"); dch = p.sem("dch"); fin = p.sem("fin")
        vf = p.sem("vf")
        xl = [p.sem(f"xl{u}") for u in range(2)]
        nl = [p.sem(f"nl{u}") for u in range(2)]
        st = [p.sem(f"st{u}") for u in range(2)]
        b = p.block(K.counted)

        @b.sync
        def _(s):
            s.dma_start(w[:, 0:KT], a["L1_gnn_W_l"].rearrange("(k p) d -> p k d", p=P)).then_inc(wl, 16)
            s.dma_start(w[:, KT:], a["L1_gnn_W_r"].rearrange("(k p) d -> p k d", p=P)).then_inc(wl, 16)
            s.dma_start(bb[:], a["L1_gnn_b"].partition_broadcast(P)).then_inc(wl, 16)

            def load(n, k, u):
                wait(s, turned, n - 1)
                s.dma_start(xn[:, u, 1, :], tab2[ds(n * P, P), :]).then_inc(nl[u], 16)
                wait(s, xd, n - 1)
                s.dma_start(xt[:, u, :], xmid[ds(n * P, P), :]).then_inc(xl[u], 16)
            pairs(s, NT, load)

        @b.scalar
        def _(c):
            def step(n, k, u):
                c.wait_ge(turned, n + 1)
                for j in range(2):
                    ins = nc.scalar.activation(xT[:, u, j * KT:(j + 1) * KT, :],
                                               psT[2 * u + j][:].rearrange("p (k t) -> p k t", k=KT), ACT.Copy)
                ins.then_inc(cop, 1)
                c.wait_ge(hs, n + 1)
                wait(c, xd, n - 1)
                nc.scalar.activation(sg[:, u, :], h[:, u, :], ACT.Sigmoid).then_inc(sgd, 1)
                c.wait_ge(xd, n + 1)
                c.dma_start(xmid[ds(n * P, P), :], x3[:, u, :]).then_inc(st[u], 16)
            pairs(c, NT, step)
            c.wait_ge(vf, 1)
            nc.scalar.activation(mv[:, :, 1:2], mv[:, :, 1:2], ACT.Sqrt).then_inc(fin, 1)
            for u in range(2):
                c.wait_ge(st[u], 16 * ((NT + 1 - u) // 2))

        @b.tensor
        def _(t):
            t.wait_ge(wl, 48)

            def tile(n, k, u):
                t.wait_ge(md, n + 1)
                t.wait_ge(nl[u], k * 16 + 16)
                for j in range(2):
                    for kt in range(KT):
                        ins = nc.tensor.transpose(psT[2 * u + j][:, kt * P:(kt + 1) * P],
                                                  xn[:, u, j, kt * P:(kt + 1) * P], K.ident[:])
                ins.then_inc(turned, 1)
                t.wait_ge(cop, n + 1)
                wait(t, hs, n - 1)
                for kt in range(2 * KT):
                    ins = nc.tensor.matmul(psH[u][:], xT[:, u, kt, :], w[:, kt, :], start=(kt == 0), stop=(kt == 2 * KT - 1))
                ins.then_inc(prod, 1)
            pairs(t, NT, tile)

        @b.vector
        def _(v):
            vv = nc.vector
            d = Chain(v, dch)
            d(vv.tensor_scalar(deg[:], acc[:, :, D:D + 1], 1.0, None, ALU.max))
            d(vv.reciprocal(deg[:], deg[:]))
            v.wait_ge(wl, 48)

            def mean(n, k, u):
                wait(v, turned, n - 1)
                vv.tensor_scalar(xn[:, u, 0, :], acc[:, ds(n, 1), 0:D].rearrange("p o d -> p (o d)"),
                                 deg[:, ds(n, 1), :].rearrange("p o d -> p (o d)"), None, ALU.mult).then_inc(md, 1)

            def step(n, k, u):
                if not last(n):
                    mean(n + 1, k + u, 1 - u)
                v.wait_ge(prod, n + 1)
                vv.tensor_tensor(h[:, u, :], psH[u][:], bb[:], ALU.add).then_inc(hs, 1)
                v.wait_ge(sgd, n + 1)
                ch = Chain(v, vch, n * 4)
                ch(vv.tensor_tensor(sg[:, u, :], sg[:, u, :], h[:, u, :], ALU.mult))
                v.wait_ge(xl[u], k * 16 + 16)
                wait(v, st[u], k * 16)
                vv.tensor_tensor(x3[:, u, :], sg[:, u, :], xt[:, u, :], ALU.add).then_inc(xd, 1)
                v.wait_ge(xd, n + 1)
                ch(vv.bn_stats(bst[:], x3[:, u, :]))
                vv.tensor_scalar(junk[:], bst[:, 0:1], 1.0, None, ALU.mult)
                ch(vv.bn_aggr(bmv[:], bst[:]))
                ch(vv.tensor_scalar(mv[:, ds(n, 1), :].rearrange("p o d -> p (o d)"), bmv[:], 0.0, None, ALU.add))
            mean(0, 0, 0)
            pairs(v, NT, step)
            vv.tensor_scalar(mv[:, :, 1:2], mv[:, :, 1:2], EPS, None, ALU.add).then_inc(vf, 1)
            v.wait_ge(fin, 1)
            d(vv.reciprocal(mv[:, :, 1:2], mv[:, :, 1:2]))


def phase_shared(nc, K, a, xmid, tab3, xsh, sc):
    with Phase(nc, "sh") as p:
        w13 = p.sb("w13", [P, 2, KT, D])
        w2 = p.sb("w2", [P, KT, D])
        gw = p.sb("gw", [E1, D])
        gT = p.sb("gT", [P, KT, E1])
        xt = p.sb("xt", [P, 3, D])
        xn = p.sb("xn", [P, 2, D])
        xT = p.sb("xT", [P, 2, KT, P])
        sg = p.sb("sg", [P, 2, D])
        hh = p.sb("hh", [P, 2, D])
        hT = p.sb("hT", [P, 2, KT, P])
        z = p.sb("z", [P, 2, D])
        psT = p.ps("psT", [P, D])
        psU = p.ps("psU", [P, D])
        psA = [p.ps(f"psA{u}", [P, D]) for u in range(2)]
        psB = [p.ps(f"psB{u}", [P, D]) for u in range(2)]
        psG = p.ps("psG", [P, D])
        psY = p.ps("psY", [P, D])
        wl = p.sem("wl"); nd = p.sem("nd"); turned = p.sem("turned"); cop = p.sem("cop"); ab = p.sem("ab")
        sgd = p.sem("sgd"); hd = p.sem("hd"); ht = p.sem("ht"); hc = p.sem("hc"); yd = p.sem("yd"); zd = p.sem("zd")
        scd = p.sem("scd"); gt = p.sem("gt"); gc = p.sem("gc"); vch = p.sem("vch")
        xl = [p.sem(f"xl{u}") for u in range(2)]
        sn = [p.sem(f"sn{u}") for u in range(2)]
        sz = [p.sem(f"sz{u}") for u in range(2)]
        b = p.block(K.counted)

        @b.sync
        def _(s):
            s.dma_start(gw[:], a["L1_ffn_gate_w"]).then_inc(wl, 16)
            for j, nm in enumerate(("L1_ffn_sw1", "L1_ffn_sw3")):
                s.dma_start(w13[:, j], a[nm].rearrange("(k p) d -> p k d", p=P)).then_inc(wl, 16)
            s.dma_start(w2[:], a["L1_ffn_sw2"].rearrange("(k p) d -> p k d", p=P)).then_inc(wl, 16)

            def load(n, k, u):
                wait(s, zd, n - 1)
                s.dma_start(xt[:, u, :], xmid[ds(n * P, P), :]).then_inc(xl[u], 16)
            pairs(s, NT, load)

        @b.scalar
        def _(c):
            c.wait_ge(gt, 1)
            nc.scalar.activation(gT[:], psG[:, 0:KT * E1].rearrange("p (k e) -> p k e", k=KT), ACT.Copy).then_inc(gc, 1)

            def step(n, k, u):
                c.wait_ge(nd, n + 1)
                c.dma_start(tab3[ds(n * P, P), :], xn[:, u, :]).then_inc(sn[u], 16)
                c.wait_ge(turned, n + 1)
                nc.scalar.activation(xT[:, u], psT[:].rearrange("p (k t) -> p k t", k=KT), ACT.Copy).then_inc(cop, 1)
                c.wait_ge(ab, n + 1)
                wait(c, hd, n - 1)
                nc.scalar.activation(sg[:, u, :], psA[u][:], ACT.Sigmoid)
                nc.scalar.activation(sc[:, ds(n, 1), :].rearrange("p o e -> p (o e)"), psG[:, 0:E1],
                                     ACT.Sigmoid).then_inc(sgd, 1)
                c.wait_ge(ht, n + 1)
                nc.scalar.activation(hT[:, u], psU[:].rearrange("p (k t) -> p k t", k=KT), ACT.Copy).then_inc(hc, 1)
                c.wait_ge(zd, n + 1)
                c.dma_start(xsh[ds(n * P, P), :], z[:, u, :]).then_inc(sz[u], 16)
            pairs(c, NT, step)
            c.wait_ge(sgd, NT)
            for u in range(2):
                c.wait_ge(sn[u], 16 * ((NT + 1 - u) // 2))
                c.wait_ge(sz[u], 16 * ((NT + 1 - u) // 2))

        @b.tensor
        def _(t):
            tens = nc.tensor
            t.wait_ge(wl, 64)
            for kt in range(KT):
                ins = tens.transpose(psG[:, kt * E1:(kt + 1) * E1], gw[:, kt * P:(kt + 1) * P], K.ident[0:E1, 0:E1])
            ins.then_inc(gt, 1)
            t.wait_ge(gc, 1)

            def up(n, k, u):
                t.wait_ge(nd, n + 1)
                for kt in range(KT):
                    ins = tens.transpose(psT[:, kt * P:(kt + 1) * P], xn[:, u, kt * P:(kt + 1) * P], K.ident[:])
                ins.then_inc(turned, 1)
                t.wait_ge(cop, n + 1)
                wait(t, hd, n - 1)
                wait(t, sgd, n)
                for kt in range(KT):
                    tens.matmul(psA[u][:], xT[:, u, kt, :], w13[:, 0, kt, :], start=(kt == 0), stop=(kt == KT - 1))
                    tens.matmul(psB[u][:], xT[:, u, kt, :], w13[:, 1, kt, :], start=(kt == 0), stop=(kt == KT - 1))
                    ins = tens.matmul(psG[:, 0:E1], xT[:, u, kt, :], gT[:, kt, :], start=(kt == 0), stop=(kt == KT - 1))
                ins.then_inc(ab, 1)

            def down(n, k, u):
                t.wait_ge(hd, n + 1)
                for kt in range(KT):
                    ins = tens.transpose(psU[:, kt * P:(kt + 1) * P], hh[:, u, kt * P:(kt + 1) * P], K.ident[:])
                ins.then_inc(ht, 1)
                t.wait_ge(hc, n + 1)
                wait(t, zd, n)
                for kt in range(KT):
                    ins = tens.matmul(psY[:], hT[:, u, kt, :], w2[:, kt, :], start=(kt == 0), stop=(kt == KT - 1))
                ins.then_inc(yd, 1)

            def step(n, k, u):
                up(n, k, u)
                down(n, k, u)
            pairs(t, NT, step)

        @b.vector
        def _(v):
            vv = nc.vector

            def norm(n, k, u):
                v.wait_ge(xl[u], k * 16 + 16)
                wait(v, sn[u], k * 16)
                mean = K.mv[:, ds(n, 1), 0:1].rearrange("p o d -> p (o d)")
                rstd = K.mv[:, ds(n, 1), 1:2].rearrange("p o d -> p (o d)")
                vv.tensor_scalar(xn[:, u, :], xt[:, u, :], mean, rstd, ALU.subtract, ALU.mult).then_inc(nd, 1)

            def step(n, k, u):
                if not last(n):
                    norm(n + 1, k + u, 1 - u)
                v.wait_ge(sgd, n + 1)
                ch = Chain(v, vch, n)
                ch(vv.tensor_tensor(sg[:, u, :], sg[:, u, :], psA[u][:], ALU.mult))
                wait(v, ht, n - 1)
                vv.tensor_tensor(hh[:, u, :], sg[:, u, :], psB[u][:], ALU.mult).then_inc(hd, 1)
                v.wait_ge(yd, n + 1)
                wait(v, sz[u], k * 16)
                vv.tensor_tensor(z[:, u, :], psY[:], xt[:, u, :], ALU.add).then_inc(zd, 1)
            norm(0, 0, 0)
            pairs(v, NT, step)


def phase_route1(nc, K, sc):
    W = NT * E1
    CH = 5
    TC = NT // CH
    with Phase(nc, "r1") as p:
        top = p.sb("top", [P, NT, 8])
        tix = p.sb("tix", [P, NT, 8], U32)
        exf = p.sb("exf", [P, NT, TOP])
        den = p.sb("den", [P, NT, 1])
        ok = p.sb("ok", [P, NT, TOP])
        oh = p.sb("oh", [P, TOP, NT, E1])
        both = p.sb("both", [P, NT, E1])
        within = p.sb("within", [P, NT, E1])
        tot = p.sb("tot", [P, E1, NT])
        keep = p.sb("keep", [P, E1, NT])
        inc = p.sb("inc", [P, E1, NT])
        n_e = p.sb("n_e", [P, E1])
        ni = p.sb("ni", [P, 2, E1], I32)
        ovt = p.sb("ovt", [P, E1])
        ovi = p.sb("ovi", [P, E1])
        ovx = p.sb("ovx", [P, E1])
        zero = p.sb("zero", [P, E1])
        pos = p.sb("pos", [P, NT, TOP])
        ovb = p.sb("ovb", [P, NT, TOP])
        qi = p.sb("qi", [P, 3, NT, TOP], I32)
        qf = p.sb("qf", [P, 2, NT, TOP])
        far = p.sb("far", [P, NT, TOP])
        item = p.sb("item", [P, NT, TOP])
        valid = p.sb("valid", [P, NT, TOP])
        tmp = p.sb("tmp", [P, NT, TOP])
        oq = p.sb("oq", [P, 1])
        pv = p.sb("pv", [P, 1])
        tri = p.sb("tri", [P, P])
        tio = p.sb("tio", [P, NT, TOP])
        oa = p.sb("oa", [P, 2, NI1], BF16)
        ob = p.sb("ob", [P, 2, 2, P], BF16)
        idf = p.sb("idf", [NI1, P])
        ps = [p.ps(f"ps{u}", [P, D]) for u in range(4)]
        psI = p.ps("psI", [P, D])
        psT = p.ps("psT", [P, D])
        g1 = p.sem("g1"); vch = p.sem("vch"); tv = p.sem("tv"); vt = p.sem("vt"); od = p.sem("od"); om = p.sem("om")
        oc = p.sem("oc")
        b = p.block(K.counted)

        @b.gpsimd
        def _(g):
            nc.gpsimd.affine_select(out=tri[:], in_=K.ones[:], compare_op=ALU.is_gt, fill=0.0, base=0,
                                    pattern=[[1, P]], channel_multiplier=-1).then_inc(g1, 1)
            nc.gpsimd.iota(tio[:], [[1, NT], [0, TOP]], base=0, channel_multiplier=0,
                           allow_small_or_imprecise_dtypes=True).then_inc(g1, 1)

        @b.tensor
        def _(t):
            tens = nc.tensor
            t.wait_ge(g1, 2)
            for c in range(CH):
                t.wait_ge(tv, 1 + c)
                cols = both[:, c * TC:(c + 1) * TC, :].rearrange("p t e -> p (t e)")
                tens.matmul(ps[0][:, 0:TC * E1], tri[:], cols, start=True, stop=True)
                tens.matmul(ps[1][:, 0:TC * E1], K.ones[:], cols, start=True, stop=True).then_inc(vt, 1)
            t.wait_ge(tv, CH + 2)
            tens.matmul(ps[2][0:1, 0:P], oq[:], K.ident[:], start=True, stop=True).then_inc(vt, 1)

            def pairm(n, k, u):
                t.wait_ge(od, n + 1)
                ins = tens.matmul(psI[0:NI1, 0:2 * P], oa[:, u, :], ob[:, u].rearrange("p w b -> p (w b)"),
                                  start=isinstance(n, int) and n == 0, stop=isinstance(n, int) and n == NT * TOP - 1,
                                  skip_group_check=True)
                ins.then_inc(om, 1)
            for u in range(2):
                pairm(u, 0, u)
            with t.Fori(1, NT - 1) as k:
                for u in range(2):
                    pairm(k * 2 + u, k, u)
            for u in range(2):
                pairm(NT * TOP - 2 + u, NT - 1, u)
            t.wait_ge(oc, 1)
            tens.transpose(psT[:, 0:NI1], idf[:], K.ident[0:NI1, 0:NI1]).then_inc(vt, 1)

        @b.vector
        def _(v):
            vv = nc.vector
            ch = Chain(v, vch)
            v.wait_ge(g1, 2)
            for n in range(NT):
                ins = vv.max(top[:, n, :], sc[:, n, :])
            ch(ins)
            for n in range(NT):
                ins = vv.max_index(tix[:, n, :], top[:, n, :], sc[:, n, :])
            ch(ins)
            ch(vv.tensor_copy(exf[:], tix[:, :, 0:TOP]))
            ch(vv.tensor_tensor(den[:], top[:, :, 0:1], top[:, :, 1:2], ALU.add))
            ch(vv.tensor_scalar(den[:], den[:], 1e-20, None, ALU.add))
            ch(vv.reciprocal(den[:], den[:]))
            ch(vv.tensor_tensor(ok[:], top[:, :, 0:TOP], den[:].to_broadcast([P, NT, TOP]), ALU.mult))
            ch(vv.tensor_reduce(pv[:], K.ident[:, 0:TAIL], AX.X, ALU.add))
            ch(vv.tensor_scalar(pv[:], pv[:], -1000.0, 1000.0, ALU.mult, ALU.add))
            ch(vv.tensor_scalar(exf[:, NT - 1, :], exf[:, NT - 1, :], pv[:], None, ALU.add))
            io = K.iota[:, 0:E1].unsqueeze(1).to_broadcast([P, NT, E1])
            for k in range(TOP):
                ins = vv.tensor_tensor(oh[:, k], io, exf[:, :, k:k + 1].to_broadcast([P, NT, E1]), ALU.is_equal)
            ch(ins)
            vv.memset(zero[:], 0.0)
            ch(vv.memset(keep[:], 1.0))
            ch(vv.memset(keep[:, :, 0:1], 0.0))
            vv.tensor_tensor(both[:], oh[:, 0], oh[:, 1], ALU.add).then_inc(tv, 1)
            for c in range(CH):
                v.wait_ge(vt, 1 + c)
                vv.tensor_copy(within[:, c * TC:(c + 1) * TC, :].rearrange("p t e -> p (t e)"), ps[0][:, 0:TC * E1])
                vv.tensor_copy(tot[:, :, c * TC:(c + 1) * TC],
                               ps[1][:, 0:TC * E1].rearrange("p (t e) -> p e t", e=E1)).then_inc(tv, 1)
            v.wait_ge(tv, CH + 1)
            fl = lambda t: t[:].rearrange("p e t -> p (e t)")
            ch(vv.tensor_tensor_scan(fl(inc), fl(keep), fl(tot), 0.0, ALU.mult, ALU.add))
            ch(vv.tensor_scalar(n_e[:], inc[:, :, NT - 1], float(CAP1), None, ALU.min))
            ch(vv.tensor_tensor(inc[:], inc[:], tot[:], ALU.subtract))
            ch(vv.tensor_tensor(within[:], within[:], inc[:].rearrange("p e t -> p t e"), ALU.add))
            ch(vv.tensor_scalar(n_e[:], n_e[:], -1.0, None, ALU.add))
            ch(vv.tensor_copy(ni[:, 0], n_e[:]))
            ch(vv.tensor_single_scalar(ni[:, 1], ni[:, 0], 7, ALU.arith_shift_right))
            ch(vv.tensor_copy(ovt[:], ni[:, 1]))
            ch(vv.tensor_scalar(ovt[:], ovt[:], 0.0, None, ALU.max))
            ch(vv.tensor_tensor_scan(ovi[:], ovt[:], zero[:], 0.0, ALU.add, ALU.add))
            ch(vv.tensor_tensor(ovx[:], ovi[:], ovt[:], ALU.subtract))
            ch(vv.tensor_copy(K.nov[:], ovi[0:1, E1 - 1:E1]))
            ch(vv.tensor_scalar(zero[:], ovi[:], K.part[:], None, ALU.is_le))
            ch(vv.tensor_reduce(oq[:], zero[:], AX.X, ALU.add))
            vv.tensor_scalar(oq[:], oq[:], float(E1 - 1), None, ALU.min).then_inc(tv, 1)
            v.wait_ge(vt, CH + 1)
            ch(vv.tensor_copy(K.ovf[:], ps[2][0:1, 0:P]))
            for k in range(TOP):
                ch(vv.tensor_tensor(both[:], oh[:, k], within[:], ALU.mult))
                ch(vv.tensor_reduce(pos[:, :, k], both[:], AX.X, ALU.add))
                ch(vv.tensor_tensor(both[:], oh[:, k], ovx[:].unsqueeze(1).to_broadcast([P, NT, E1]), ALU.mult))
                ch(vv.tensor_reduce(ovb[:, :, k], both[:], AX.X, ALU.add))
            ch(vv.tensor_copy(qi[:, 0], pos[:]))
            ch(vv.tensor_single_scalar(qi[:, 1], qi[:, 0], 7, ALU.arith_shift_right))
            ch(vv.tensor_single_scalar(qi[:, 2], qi[:, 0], P - 1, ALU.bitwise_and))
            ch(vv.tensor_copy(qf[:], qi[:, 1:3]))
            ch(vv.tensor_scalar(far[:], qf[:, 0], 0.5, None, ALU.is_gt))
            ch(vv.tensor_tensor(tmp[:], qf[:, 0], ovb[:], ALU.add))
            ch(vv.tensor_scalar(tmp[:], tmp[:], float(E1 - 1), None, ALU.add))
            ch(vv.tensor_tensor(tmp[:], tmp[:], exf[:], ALU.subtract))
            ch(vv.tensor_tensor(tmp[:], tmp[:], far[:], ALU.mult))
            ch(vv.tensor_tensor(item[:], tmp[:], exf[:], ALU.add))
            ch(vv.tensor_scalar(valid[:], pos[:], float(CAP1), None, ALU.is_lt))
            ch(vv.tensor_scalar(tmp[:], item[:], float(P), None, ALU.mult))
            ch(vv.tensor_tensor(tmp[:], tmp[:], qf[:, 1], ALU.add))
            ch(vv.tensor_tensor(tmp[:], tmp[:], valid[:], ALU.mult))
            ch(vv.tensor_scalar(tmp[:], tmp[:], float(NI1 * P - 1), None, ALU.min))
            ch(vv.tensor_copy(K.pair[:], tmp[:]))
            ch(vv.tensor_scalar(ok[:], ok[:], ROUTE_SCALE, None, ALU.mult))
            ch(vv.tensor_tensor(K.gate[:], ok[:], valid[:], ALU.mult))
            ch(vv.tensor_scalar(valid[:], valid[:], -1000.0, 1000.0, ALU.mult, ALU.add))
            ch(vv.tensor_tensor(item[:], item[:], valid[:], ALU.add))
            fi = item[:].rearrange("p t k -> p (t k)")
            lo = qf[:, 1].rearrange("p t k -> p (t k)")
            ti = tio[:].rearrange("p t k -> p (t k)")

            def pairo(n, k, u):
                wait(v, om, n - 1)
                vv.tensor_scalar(oa[:, u, :], K.iota[:, 0:NI1], fi[:, ds(n, 1)], None, ALU.is_equal)
                vv.tensor_scalar(ob[:, u, 0, :], K.iota[:], lo[:, ds(n, 1)], K.part[:], ALU.is_equal, ALU.mult)
                vv.tensor_scalar(ob[:, u, 1, :], K.iota[:], lo[:, ds(n, 1)], ti[:, ds(n, 1)], ALU.is_equal,
                                 ALU.mult).then_inc(od, 1)
            pairs(v, NT * TOP, pairo)
            v.wait_ge(om, NT * TOP)
            ch(vv.tensor_scalar(idf[:], psI[0:NI1, P:2 * P], float(P), None, ALU.mult))
            vv.tensor_tensor(idf[:], idf[:], psI[0:NI1, 0:P], ALU.add).then_inc(oc, 1)
            v.wait_ge(vt, CH + 2)
            ch(vv.tensor_copy(K.slot[:], psT[:, 0:NI1]))


def phase_experts1(nc, K, a, tab3, ys):
    with Phase(nc, "e1") as p:
        NG, NW = 4, 2
        g = p.sb("g", [P, NG, D])
        w13 = p.sb("w13", [P, NW, KT, 2 * F1])
        w2 = p.sb("w2", [P, NW, F1 // P, D])
        xT = p.sb("xT", [P, 2, KT, P])
        sg = p.sb("sg", [P, 2, F1])
        hh = p.sb("hh", [P, 2, F1])
        hT = p.sb("hT", [P, 2, F1 // P, P])
        y = p.sb("y", [P, 2, D])
        psX = p.ps("psX", [P, D])
        psH = [p.ps(f"psH{u}", [P, D]) for u in range(2)]
        psU = p.ps("psU", [P, D])
        psY = [p.ps(f"psY{u}", [P, D]) for u in range(2)]
        got = [p.gather_sem(f"got{q}") for q in range(NG)]
        wl = [p.sem(f"wl{q}") for q in range(NW)]
        st = [p.sem(f"st{u}") for u in range(2)]
        turned = p.sem("turned"); cop = p.sem("cop"); up = p.sem("up"); sgd = p.sem("sgd"); hd = p.sem("hd")
        ht = p.sem("ht"); hc = p.sem("hc"); yd = p.sem("yd"); yc = p.sem("yc"); vch = p.sem("vch")
        b = p.block(K.counted)

        def load(s, n, u, e):
            wait(s, yd, n - 1)
            for j, nm in enumerate(("L1_ffn_w1", "L1_ffn_w3")):
                s.dma_start(w13[:, u, :, j * F1:(j + 1) * F1],
                            a[nm][ds(e, 1)].rearrange("o (k p) f -> p (o k) f", p=P)).then_inc(wl[u], 16)
            s.dma_start(w2[:, u], a["L1_ffn_w2"][ds(e, 1)].rearrange("o (k p) d -> p (o k) d", p=P)).then_inc(wl[u], 16)

        @b.sync
        def _(s):
            pairs(s, E1, lambda n, k, u: load(s, n, u, n))
            with s.Fori(E1 // 2, NI1 // 2) as k:
                for u in range(2):
                    e = s.value_load(K.ovf[0:1, ds(k * 2 + (u - E1), 1)], min_val=0, max_val=E1 - 1)
                    load(s, k * 2 + u, u, e)

        @b.gpsimd
        def _(q):
            for n in range(NI1):
                wait(q, turned, n - NG + 1)
                q.indirect_dma_start(g[:, n % NG, :], None, tab3,
                                     bass.IndirectOffsetOnAxis(K.slot[:, n:n + 1], 0)).then_inc(got[n % NG], 16)

        def quads(body):
            def run(eng):
                for q in range(4):
                    body(eng, q, 0, q)
                with eng.Fori(1, NI1 // 4) as k:
                    for q in range(4):
                        body(eng, k * 4 + q, k, q)
            return run

        @b.tensor
        def _(t):
            tens = nc.tensor

            def item(t, n, k, q):
                u = q % 2
                t.wait_ge(got[q], k * 16 + 16)
                for kt in range(KT):
                    ins = tens.transpose(psX[:, kt * P:(kt + 1) * P], g[:, q, kt * P:(kt + 1) * P], K.ident[:])
                ins.then_inc(turned, 1)
                t.wait_ge(cop, n + 1)
                t.wait_ge(wl[u], k * 96 + (48 if q < 2 else 96))
                wait(t, hd, n - 1)
                for kt in range(KT):
                    ins = tens.matmul(psH[u][:], xT[:, u, kt, :], w13[:, u, kt, :], start=(kt == 0), stop=(kt == KT - 1))
                ins.then_inc(up, 1)
                t.wait_ge(hd, n + 1)
                for c in range(F1 // P):
                    ins = tens.transpose(psU[:, c * P:(c + 1) * P], hh[:, u, c * P:(c + 1) * P], K.ident[:])
                ins.then_inc(ht, 1)
                t.wait_ge(hc, n + 1)
                wait(t, yc, n - 1)
                for c in range(F1 // P):
                    ins = tens.matmul(psY[u][:], hT[:, u, c, :], w2[:, u, c, :], start=(c == 0), stop=(c == F1 // P - 1))
                ins.then_inc(yd, 1)
            quads(item)(t)

        @b.scalar
        def _(c):
            def item(c, n, k, q):
                u = q % 2
                c.wait_ge(turned, n + 1)
                nc.scalar.activation(xT[:, u], psX[:].rearrange("p (k t) -> p k t", k=KT), ACT.Copy).then_inc(cop, 1)
                c.wait_ge(up, n + 1)
                nc.scalar.activation(sg[:, u, :], psH[u][:, 0:F1], ACT.Sigmoid).then_inc(sgd, 1)
                c.wait_ge(ht, n + 1)
                nc.scalar.activation(hT[:, u], psU[:, 0:F1].rearrange("p (c t) -> p c t", t=P), ACT.Copy).then_inc(hc, 1)
                c.wait_ge(yd, n + 1)
                if isinstance(n, int):
                    wait(c, st[u], 16 * (n // 2))
                else:
                    c.wait_ge(st[u], k * 32 + 16 * (q // 2))
                nc.scalar.activation(y[:, u, :], psY[u][:], ACT.Copy).then_inc(yc, 1)
                c.wait_ge(yc, n + 1)
                c.dma_start(ys[ds(n * P, P), :], y[:, u, :]).then_inc(st[u], 16)
            quads(item)(c)
            for u in range(2):
                c.wait_ge(st[u], 16 * (NI1 // 2))

        @b.vector
        def _(v):
            vv = nc.vector

            def item(v, n, k, q):
                u = q % 2
                v.wait_ge(sgd, n + 1)
                ch = Chain(v, vch, n)
                ch(vv.tensor_tensor(sg[:, u, :], sg[:, u, :], psH[u][:, 0:F1], ALU.mult))
                wait(v, ht, n - 1)
                vv.tensor_tensor(hh[:, u, :], sg[:, u, :], psH[u][:, F1:2 * F1], ALU.mult).then_inc(hd, 1)
            quads(item)(v)


def phase_combine(nc, K, xsh, ys, out):
    with Phase(nc, "cb") as p:
        z = p.sb("z", [P, 2, D])
        g = p.sb("g", [P, 2, TOP, D])
        o = p.sb("o", [P, 2, D])
        zl = [p.sem(f"zl{u}") for u in range(2)]
        got = [p.gather_sem(f"got{u}") for u in range(2)]
        st = [p.sem(f"st{u}") for u in range(2)]
        half = p.sem("half"); od = p.sem("od")
        b = p.block(K.counted)

        @b.sync
        def _(s):
            def load(n, k, u):
                wait(s, od, n - 1)
                s.dma_start(z[:, u, :], xsh[ds(n * P, P), :]).then_inc(zl[u], 16)
            pairs(s, NT, load)

        @b.gpsimd
        def _(q):
            for n in range(NT):
                wait(q, od, n - 1)
                for k in range(TOP):
                    q.indirect_dma_start(g[:, n % 2, k, :], None, ys,
                                         bass.IndirectOffsetOnAxis(K.pair[:, n, k:k + 1], 0)).then_inc(got[n % 2], 16)

        @b.scalar
        def _(c):
            def store(n, k, u):
                c.wait_ge(od, n + 1)
                c.dma_start(tile_rows(out, n), o[0:rows_of(n), u, :]).then_inc(st[u], 16)
            pairs(c, NT, store)
            for u in range(2):
                c.wait_ge(st[u], 16 * ((NT + 1 - u) // 2))

        @b.vector
        def _(v):
            def step(n, k, u):
                v.wait_ge(zl[u], k * 16 + 16)
                v.wait_ge(got[u], k * 32 + 32)
                wait(v, st[u], k * 16)
                w = lambda j: K.gate[:, ds(n, 1), j:j + 1].rearrange("p o d -> p (o d)")
                nc.vector.scalar_tensor_tensor(o[:, u, :], g[:, u, 0, :], w(0), z[:, u, :], ALU.mult, ALU.add).then_inc(half, 1)
                v.wait_ge(half, n + 1)
                nc.vector.scalar_tensor_tensor(o[:, u, :], g[:, u, 1, :], w(1), o[:, u, :], ALU.mult, ALU.add).then_inc(od, 1)
            pairs(v, NT, step)


def kernel(**inputs):
    import concourse.bacc as bacc
    from concourse.bass_utils import run_bass_kernel_spmd as run

    nc = bacc.Bacc("TRN2", target_bir_lowering=False, num_devices=1)
    arrays, aps = {}, {}
    for name, value in inputs.items():
        v = np.ascontiguousarray(value)
        arrays[f"in_{name}"] = v
        aps[name] = nc.dram_tensor(f"in_{name}", v.shape, mybir.dt.from_np(v.dtype), kind="ExternalInput").ap()
    out = nc.dram_tensor("out_x", (N, D), F32, kind="ExternalOutput").ap()
    build(nc, aps, out, 9)
    return run(nc, [arrays], core_ids=[0]).results[0]["out_x"]
```

```python
from contextlib import ExitStack

import numpy as np

import concourse.bass as bass
from concourse import mybir

ALU = mybir.AluOpType
ACT = mybir.ActivationFunctionType
AX = mybir.AxisListType
F32 = mybir.dt.float32
BF16 = mybir.dt.bfloat16
I32 = mybir.dt.int32
U32 = mybir.dt.uint32
ds = bass.ds

P = 128
N = 3125
D = 512
KT = D // P
NT = -(-N // P)
NP = NT * P
TAIL = N - (NT - 1) * P
E = 50000
H0 = 8
HD = D // H0
SUP = 2
NSUP = -(-E // (P * SUP))
NET = NSUP * SUP
ESLOT = NET * P
NX = NT - 1
NIT = NSUP + NX
EC = 4
ER = NET // EC
BIG = 1.0e30
FAR = 1 << 20
ROW = D + 2 * H0
EXW = H0 + 1
EPS = 1e-5
E0, F0, CAP0 = 8, 128, 256
E1, F1, TOP, CAP1 = 64, 256, 2, 1024
ROUTE_SCALE = 2.5
NOV = (N * TOP) // P
NI1 = E1 + NOV
assert NI1 <= P and NET % EC == 0 and ER <= P and NET * P >= E


def pairs(eng, count, body):
    for u in range(2):
        body(u, 0, u)
    with eng.Fori(1, count // 2) as k:
        for u in range(2):
            body(k * 2 + u, k, u)
    if count % 2:
        body(count - 1, count // 2, 0)


def skewed(eng, count, skew, body, unroll=2, total=None):
    first = -(-(skew + 2) // unroll)
    for n in range(first * unroll):
        body(n, n // unroll, n % unroll)
    turns = count // unroll if total is None else total
    with eng.Fori(first, turns) as k:
        for u in range(unroll):
            body(k * unroll + u, k, u)
    if total is None:
        for n in range(turns * unroll, count + skew):
            body(n, n // unroll, n % unroll)
    else:
        for u in range(skew):
            body(total * unroll + u, total, u)


def back(n, k, u, j, unroll=2):
    return n - j, k + (u - j) // unroll, (u - j) % unroll


def within(n, count):
    return not isinstance(n, int) or 0 <= n < count


def wait(eng, sem, value):
    if not isinstance(value, int) or value > 0:
        eng.wait_ge(sem, value)


def last(n):
    return isinstance(n, int) and n == NT - 1


class Chain:

    def __init__(self, eng, sem, base=0):
        self.eng, self.sem, self.base, self.n = eng, sem, base, 0

    def __call__(self, ins):
        self.n += 1
        ins.then_inc(self.sem, 1)
        self.eng.wait_ge(self.sem, self.base + self.n)


class Phase:

    def __init__(self, nc, name):
        self.nc, self.name, self.ctx, self.sems = nc, name, ExitStack(), []

    def __enter__(self):
        self.ctx.__enter__()
        return self

    def __exit__(self, *a):
        return self.ctx.__exit__(*a)

    def sb(self, name, shape, dt=F32):
        return self.ctx.enter_context(self.nc.sbuf_tensor(f"{self.name}_{name}", shape, dt))

    def ps(self, name, shape, dt=F32):
        return self.ctx.enter_context(self.nc.psum_tensor(f"{self.name}_{name}", shape, dt))

    def sem(self, name):
        s = self.ctx.enter_context(self.nc.semaphore(f"{self.name}_{name}"))
        self.sems.append(s.num)
        return s

    def gather_sem(self, name):
        return self.nc.alloc_semaphore(f"{self.name}_{name}")

    def block(self, counted):
        if counted & set(self.sems):
            with self.nc.Block() as b:
                @b.gpsimd
                def _(g):
                    for n in sorted(counted):
                        if n - 1 not in counted:
                            end = n
                            while end in counted:
                                end += 1
                            g.sem_clear(range(n, end))
            counted.clear()
        counted |= set(self.sems)
        return self.ctx.enter_context(self.nc.Block())


class Shared:

    def __init__(self):
        self.counted = set()


class Norm:

    def __init__(self, p, nc):
        self.nc = nc
        self.st = p.sb("ln_st", [P, 6])
        self.mv = p.sb("ln_mv", [P, 2])
        self.sd = p.sb("ln_sd", [P, 2])
        self.junk = p.sb("ln_junk", [P, 1])
        self.chain = p.sem("ln_chain")
        self.var = p.sem("ln_var")
        self.root = p.sem("ln_root")

    def vector(self, v, n, x, out, done):
        ch, vv = Chain(v, self.chain, n * 3), self.nc.vector
        ch(vv.bn_stats(self.st[:], x))
        vv.tensor_scalar(self.junk[:], self.st[:, 0:1], 1.0, None, ALU.mult)
        ch(vv.bn_aggr(self.mv[:], self.st[:]))
        vv.tensor_scalar(self.sd[:, 0:1], self.mv[:, 1:2], EPS, None, ALU.add).then_inc(self.var, 1)
        v.wait_ge(self.root, n + 1)
        ch(vv.reciprocal(self.sd[:, 1:2], self.sd[:, 1:2]))
        vv.tensor_scalar(out, x, self.mv[:, 0:1], self.sd[:, 1:2], ALU.subtract, ALU.mult).then_inc(done, 1)

    def scalar(self, c, n):
        c.wait_ge(self.var, n + 1)
        self.nc.scalar.activation(self.sd[:, 1:2], self.sd[:, 0:1], ACT.Sqrt).then_inc(self.root, 1)


def build(nc, a, out, stop):
    dram = lambda name, shape, dt=F32: nc.dram_tensor(name, shape, dt, kind="Internal").ap()
    tab0 = dram("tab0", [NP, ROW])
    tabs = dram("tabs", [NP, H0])
    esrc = dram("esrc", [NSUP, SUP * P], I32)
    edst = dram("edst", [NSUP + 2, SUP * P], I32)
    xmid = dram("xmid", [NP, D])
    tab1 = dram("tab1", [NP, D + E0])
    sid = dram("sid", [E0, CAP0], I32)
    tab2 = dram("tab2", [NP, D])
    tab3 = dram("tab3", [NP, D])
    xsh = dram("xsh", [NP, D])
    ys = dram("ys", [NI1 * P, D])

    with ExitStack() as top:
        sb = lambda name, shape, dt=F32: top.enter_context(nc.sbuf_tensor(name, shape, dt))
        K = Shared()
        K.ident = sb("ident", [P, P])
        K.iota = sb("iota", [P, P])
        K.ones = sb("ones", [P, P])
        K.part = sb("part", [P, 1])
        K.src = sb("src_of_item", [P, NIT * SUP], I32)
        K.rel = sb("rel_of_item", [P, NIT * SUP])
        K.blk = sb("blk_of_item", [1, NIT], I32)
        K.junk = sb("junk", [P, D])
        K.xsup = sb("xsup", [1, NX], I32)
        phase_project(nc, K, a, tab0, tabs, esrc, edst)
        phase_tables(nc, K, esrc, edst)
        with nc.sbuf_tensor("acc", [P, NT, D + EXW], F32) as acc:
            with nc.sbuf_tensor("ex", [P, NIT * SUP, EXW], F32) as ex:
                phase_scores(nc, K, tab0, tabs, edst, ex)
                phase_aggregate(nc, K, "g0", tab0, ROW, ex, acc)
            with nc.sbuf_tensor("logits0", [P, NT, E0], F32) as lg:
                phase_attend(nc, K, a, acc, xmid, tab1, lg)
                phase_route0(nc, K, lg, tab1, sid)
        phase_experts0(nc, K, a, tab1, sid, xmid)
        if stop == 2:
            return phase_copy(nc, K, xmid, out)
        phase_norm2(nc, K, xmid, tab2)
        K.mv = sb("ln_mv3", [P, NT, 2])
        with nc.sbuf_tensor("acc1", [P, NT, D + 1], F32) as acc:
            phase_aggregate(nc, K, "g1", tab2, D, None, acc)
            phase_sage(nc, K, a, acc, tab2, xmid, K.mv, ys)
        if stop == 3:
            return phase_copy(nc, K, xmid, out)
        K.slot = sb("slot_of_item", [P, NI1], I32)
        K.ovf = sb("ovf", [1, P], I32)
        K.nov = sb("nov", [1, 1], I32)
        K.pair = sb("pair_slot", [P, NT, TOP], I32)
        K.gate = sb("pair_gate", [P, NT, TOP])
        with nc.sbuf_tensor("scores1", [P, NT, E1], F32) as sc:
            phase_shared(nc, K, a, xmid, tab3, xsh, sc)
            phase_route1(nc, K, sc)
        phase_experts1(nc, K, a, tab3, ys)
        phase_combine(nc, K, xsh, ys, out)


def phase_project(nc, K, a, tab0, tabs, esrc, edst):
    with Phase(nc, "pj") as p:
        w = p.sb("w", [P, KT, D + 2 * H0])
        aw = p.sb("aw", [P, H0, 2 * HD])
        prod = p.sb("prod", [P, D])
        wb = p.sb("wb", [P, D])
        ab = p.sb("ab", [P, H0])
        cst = p.sb("cst", [P, 2 * H0])
        ctmp = p.sb("ctmp", [P, 2 * H0])
        xt = p.sb("xt", [P, 2, D])
        xn = p.sb("xn", [P, 2, D])
        xnT = p.sb("xnT", [P, 2, D])
        ln = Norm(p, nc)
        row = p.sb("row", [P, 2, ROW])
        pad = p.sb("pad", [1, 3, SUP * P], I32)
        psT = [p.ps(f"psT{u}", [P, D]) for u in range(2)]
        psW = [p.ps(f"psW{u}", [P, D]) for u in range(2)]
        psS = [p.ps(f"psS{u}", [P, D]) for u in range(2)]
        consts = p.sem("consts")
        idz = p.sem("idz")
        wl = p.sem("wl")
        padr = p.sem("padr")
        edge = p.sem("edge")
        wready = p.sem("wready")
        xl = [p.sem(f"xl{u}") for u in range(2)]
        normed = p.sem("normed")
        turned = p.sem("turned")
        turned_sb = p.sem("turned_sb")
        prodn = p.sem("prodn")
        evac = p.sem("evac")
        st_row = [p.sem(f"st_row{u}") for u in range(2)]
        vch = p.sem("vch")
        wch = p.sem("wch")
        b = p.block(K.counted)

        @b.gpsimd
        def _(g):
            nc.gpsimd.memset(K.ident[:], 0.0).then_inc(idz, 1)
            nc.gpsimd.iota(K.iota[:], [[1, P]], base=0, channel_multiplier=0,
                           allow_small_or_imprecise_dtypes=True).then_inc(consts, 1)
            nc.gpsimd.iota(K.part[:], [[0, 1]], base=0, channel_multiplier=1,
                           allow_small_or_imprecise_dtypes=True).then_inc(consts, 1)
            g.wait_ge(idz, 1)
            nc.gpsimd.affine_select(out=K.ident[:], in_=K.ident[:], compare_op=ALU.not_equal, fill=1.0,
                                    base=0, pattern=[[-1, P]], channel_multiplier=1).then_inc(consts, 1)
            nc.gpsimd.memset(pad[:, 0, :], 0).then_inc(padr, 1)
            nc.gpsimd.memset(pad[:, 1, :], FAR).then_inc(padr, 1)
            nc.gpsimd.memset(pad[:, 2, :], 2 * FAR).then_inc(padr, 1)

        @b.sync
        def _(s):
            for kt in range(KT):
                s.dma_start(w[:, kt, 0:D].rearrange("p (h d) -> p h d", h=H0),
                            a["L0_gnn_Ws"][:, kt * P:(kt + 1) * P, :].rearrange("h p d -> p h d")).then_inc(wl, 16)
            s.dma_start(aw[:].rearrange("p h d -> p (h d)"),
                        a["L0_gnn_a_w"].rearrange("h d -> (h d)").partition_broadcast(P)).then_inc(wl, 16)
            s.dma_start(wb[:], a["L0_gnn_Wb"].rearrange("h d -> (h d)").partition_broadcast(P)).then_inc(wl, 16)
            s.dma_start(ab[:], a["L0_gnn_a_b"].partition_broadcast(P)).then_inc(wl, 16)

            def load(n, k, u):
                wait(s, normed, n - 1)
                rows = TAIL if last(n) else P
                src = a["x"][n * P:N, :] if last(n) else a["x"][ds(n * P, P), :]
                s.dma_start(xt[0:rows, u, :], src).then_inc(xl[u], 16)
            pairs(s, NT, load)

        @b.scalar
        def _(c):
            flat = lambda t: t.rearrange("s e -> (s e)")
            c.dma_start(flat(esrc)[0:E], a["src"]).then_inc(edge, 16)
            c.dma_start(flat(edst)[SUP * P:SUP * P + E], a["dst"]).then_inc(edge, 16)
            c.wait_ge(padr, 3)
            c.dma_start(flat(esrc)[E:ESLOT].unsqueeze(0), pad[:, 0, 0:ESLOT - E]).then_inc(edge, 16)
            c.dma_start(flat(edst)[0:SUP * P].unsqueeze(0), pad[:, 2, :]).then_inc(edge, 16)
            c.dma_start(flat(edst)[SUP * P + E:SUP * P + ESLOT].unsqueeze(0),
                        pad[:, 1, 0:ESLOT - E]).then_inc(edge, 16)
            c.dma_start(flat(edst)[SUP * P + ESLOT:].unsqueeze(0), pad[:, 2, :]).then_inc(edge, 16)

            def store(n, k, u):
                c.wait_ge(evac, n + 1)
                c.dma_start(tab0[ds(n * P, P), :], row[:, u, :]).then_inc(st_row[u], 16)
                c.dma_start(tabs[ds(n * P, P), :], row[:, u, D:D + H0]).then_inc(st_row[u], 16)

            def step(n, k, u):
                if not last(n):
                    ln.scalar(c, n + 1)
                c.wait_ge(turned, n + 1)
                nc.scalar.activation(xnT[:, u, :], psT[u][:], ACT.Copy).then_inc(turned_sb, 1)
                if not (isinstance(n, int) and n == 0):
                    store(n - 1, k + u - 1, 1 - u)
            ln.scalar(c, 0)
            pairs(c, NT, step)
            store(NT - 1, NT // 2, 0)
            c.wait_ge(edge, 6 * 16)
            for u in range(2):
                c.wait_ge(st_row[u], 32 * ((NT + 1 - u) // 2))

        @b.tensor
        def _(t):
            t.wait_ge(consts, 4)

            def tile(n, k, u):
                t.wait_ge(normed, n + 1)
                for kt in range(KT):
                    ins = nc.tensor.transpose(psT[u][:, kt * P:(kt + 1) * P], xn[:, u, kt * P:(kt + 1) * P], K.ident[:])
                ins.then_inc(turned, 1)
                t.wait_ge(turned_sb, n + 1)
                wait(t, evac, n - 1)
                if isinstance(n, int) and n == 0:
                    t.wait_ge(wready, 1)
                for kt in range(KT):
                    nc.tensor.matmul(psW[u][:], xnT[:, u, kt * P:(kt + 1) * P], w[:, kt, 0:D],
                                     start=(kt == 0), stop=(kt == KT - 1))
                    ins = nc.tensor.matmul(psS[u][:, 0:2 * H0], xnT[:, u, kt * P:(kt + 1) * P], w[:, kt, D:ROW],
                                           start=(kt == 0), stop=(kt == KT - 1))
                ins.then_inc(prodn, 1)
            pairs(t, NT, tile)

        @b.vector
        def _(v):
            nc.vector.memset(K.ones[:], 1.0).then_inc(consts, 1)
            wc = Chain(v, wch)
            v.wait_ge(wl, 16 * (KT + 3))
            for kt in range(KT + 1):
                src = w[:, kt, 0:D] if kt < KT else wb[:]
                dst = w[:, kt, D:ROW] if kt < KT else ctmp[:]
                for half, col in ((1, 0), (0, H0)):
                    wc(nc.vector.tensor_tensor(prod[:].rearrange("p (h d) -> p h d", h=H0),
                                               src.rearrange("p (h d) -> p h d", h=H0),
                                               aw[:, :, half * HD:(half + 1) * HD], ALU.mult))
                    wc(nc.vector.tensor_reduce(dst[:, col:col + H0], prod[:].rearrange("p (h d) -> p h d", h=H0),
                                               AX.X, ALU.add))
            wc(nc.vector.memset(cst[:, 0:H0], 0.0))
            wc(nc.vector.tensor_tensor(ctmp[:, 0:H0], ctmp[:, 0:H0], ctmp[:, H0:2 * H0], ALU.add))
            nc.vector.tensor_tensor(cst[:, H0:2 * H0], ctmp[:, 0:H0], ab[:], ALU.add).then_inc(wready, 1)
            v.wait_ge(wready, 1)

            def norm(n, k, u):
                v.wait_ge(xl[u], k * 16 + 16)
                ln.vector(v, n, xt[:, u, :], xn[:, u, :], normed)

            def evacuate(n, k, u):
                v.wait_ge(prodn, n + 1)
                wait(v, st_row[u], k * 32)
                nc.vector.tensor_tensor(row[:, u, 0:D], psW[u][:], wb[:], ALU.add)
                nc.vector.tensor_tensor(row[:, u, D:ROW], psS[u][:, 0:2 * H0], cst[:], ALU.add).then_inc(evac, 1)

            def step(n, k, u):
                if not last(n):
                    norm(n + 1, k + u, 1 - u)
                evacuate(n, k, u)
            norm(0, 0, 0)
            pairs(v, NT, step)


def phase_tables(nc, K, esrc, edst):
    with Phase(nc, "tb") as p:
        rowi = p.sb("rowi", [ER, 2, EC, P], I32)
        rowf = p.sb("rowf", [ER, 2, EC, P])
        cnt = p.sb("cnt", [ER, NX])
        xst = p.sb("xst", [NX, 1])
        xsti = p.sb("xsti", [NX, 4], I32)
        xsupf = p.sb("xsupf", [NX, 1])
        xi = p.sb("xi", [NX, 2, SUP * P], I32)
        xf = p.sb("xf", [NX, 2, SUP * P])
        xlow = p.sb("xlow", [NX, 1])
        xbad = p.sb("xbad", [NX, 1])
        xrel = p.sb("xrel", [NX, SUP * P])
        b0i = p.sb("b0i", [1, NSUP], I32)
        b0f = p.sb("b0f", [1, NSUP])
        xsf = p.sb("xsf", [1, NX])
        dstT = p.sb("dstT", [P, NET])
        psA = [p.ps(f"psA{u}", [P, D]) for u in range(2)]
        psC = p.ps("psC", [P, D])
        psR = p.ps("psR", [P, D])
        psX = p.ps("psX", [P, D])
        psY = p.ps("psY", [P, D])
        ld = p.sem("ld")
        fx = p.sem("fx")
        lowr = p.sem("lowr")
        cntd = p.sem("cntd")
        turned = p.sem("turned")
        gat = p.gather_sem("gat")
        xin = p.sem("xin")
        vch = p.sem("vch")
        vall = p.sem("vall")
        bcast = p.sem("bcast")
        flat = lambda t: t.rearrange("s e -> (s e)")
        tiles = lambda t: t.rearrange("(c r e) -> r c e", c=EC, e=P)
        b = p.block(K.counted)

        @b.sync
        def _(s):
            s.dma_start(rowi[:, 0], tiles(flat(esrc))).then_inc(ld, 16)
            s.dma_start(rowi[:, 1], tiles(flat(edst)[SUP * P:SUP * P + ESLOT])).then_inc(ld, 16)
            with nc.allow_non_contiguous_dma(reason="one word per super tile"):
                s.dma_start(b0i[:], edst[1:1 + NSUP, 0:1].rearrange("s o -> o s")).then_inc(ld, 16)

        @b.gpsimd
        def _(g):
            nc.gpsimd.iota(xlow[:], [[0, 1]], base=P, channel_multiplier=P,
                           allow_small_or_imprecise_dtypes=True).then_inc(lowr, 1)
            g.wait_ge(xin, 1)
            g.indirect_dma_start(xi[:, 0, :], None, esrc, bass.IndirectOffsetOnAxis(xsti[:, 2:3], 0)).then_inc(gat, 16)
            g.indirect_dma_start(xi[:, 1, :], None, edst, bass.IndirectOffsetOnAxis(xsti[:, 3:4], 0)).then_inc(gat, 16)
            g.wait_ge(gat, 32)

        @b.tensor
        def _(t):
            t.wait_ge(fx, 2)
            for c in range(EC):
                for w in range(2):
                    ins = nc.tensor.transpose(psA[w][:, c * P:c * P + ER], rowf[:, w, c, :], K.ident[0:ER, 0:ER])
            ins.then_inc(turned, 1)
            t.wait_ge(cntd, 1)
            nc.tensor.matmul(psC[0:NX, 0:1], cnt[:], K.ones[0:ER, 0:1], start=True, stop=True).then_inc(turned, 1)
            nc.tensor.matmul(psR[0:1, 0:NX], K.ones[0:ER, 0:1], cnt[:], start=True, stop=True).then_inc(turned, 1)
            t.wait_ge(fx, 3)
            nc.tensor.matmul(psY[:, 0:NSUP], K.ones[0:1, :], b0f[:], start=True, stop=True).then_inc(turned, 1)
            t.wait_ge(fx, 4)
            for h in range(SUP):
                nc.tensor.transpose(psX[:, h * NX:(h + 1) * NX], xf[:, 0, h * P:(h + 1) * P], K.ident[0:NX, 0:NX])
                ins = nc.tensor.transpose(psX[:, 128 + h * NX:128 + (h + 1) * NX], xrel[:, h * P:(h + 1) * P],
                                          K.ident[0:NX, 0:NX])
            ins.then_inc(turned, 1)

        @b.vector
        def _(v):
            ch = Chain(v, vch)
            vv = nc.vector
            v.wait_ge(ld, 48)
            vv.tensor_copy(rowf[:, 0], rowi[:, 0]).then_inc(fx, 1)
            vv.tensor_copy(rowf[:, 1], rowi[:, 1]).then_inc(fx, 1)
            v.wait_ge(fx, 2)
            for x in range(NX):
                ins = vv.tensor_scalar(K.junk[0:ER, :], rowf[:, 1].rearrange("p c e -> p (c e)"), float((x + 1) * P), 0.0,
                                       ALU.is_lt, ALU.add, accum_out=cnt[:, x:x + 1])
                if x < NX - 1:
                    ch(ins)
            ins.then_inc(cntd, 1)
            ch(vv.tensor_single_scalar(K.blk[0:1, 0:NSUP], b0i[:], 7, ALU.arith_shift_right))
            ch(vv.tensor_copy(b0f[:], K.blk[0:1, 0:NSUP]))
            vv.tensor_scalar(b0f[:], b0f[:], float(P), None, ALU.mult).then_inc(fx, 1)
            for x in range(NX):
                vv.memset(K.blk[0:1, NSUP + x:NSUP + x + 1], x + 1)
            v.wait_ge(turned, 1)
            for c in range(EC):
                vv.tensor_copy(K.src[:, c * ER:(c + 1) * ER], psA[0][:, c * P:c * P + ER])
                ch(vv.tensor_copy(dstT[:, c * ER:(c + 1) * ER], psA[1][:, c * P:c * P + ER]))
            v.wait_ge(turned, 3)
            ch(vv.tensor_copy(xsti[:, 0:1], psC[0:NX, 0:1]))
            ch(vv.tensor_single_scalar(xsti[:, 2:3], xsti[:, 0:1], 8, ALU.arith_shift_right))
            ch(vv.tensor_copy(xst[:], xsti[:, 2:3]))
            ch(vv.tensor_scalar(xst[:], xst[:], 1.0, None, ALU.add))
            vv.tensor_copy(xsti[:, 3:4], xst[:]).then_inc(xin, 1)
            ch(vv.tensor_copy(K.xsup[:], psR[0:1, 0:NX]))
            ch(vv.tensor_single_scalar(K.xsup[:], K.xsup[:], 8, ALU.arith_shift_right))
            v.wait_ge(turned, 4)
            vv.tensor_tensor(K.rel[:, 0:NET].rearrange("p (s h) -> p s h", h=SUP),
                             dstT[:].rearrange("p (s h) -> p s h", h=SUP),
                             psY[:, 0:NSUP].unsqueeze(2).to_broadcast([P, NSUP, SUP]), ALU.subtract)
            v.wait_ge(gat, 32)
            v.wait_ge(lowr, 1)
            ch(vv.tensor_copy(xf[:], xi[:]))
            ch(vv.tensor_scalar(xbad[:], xf[:, 1, 0:1], xlow[:], float(FAR), ALU.is_ge, ALU.mult))
            ch(vv.tensor_tensor(xbad[:], xbad[:], xlow[:], ALU.subtract))
            vv.tensor_scalar(xrel[:], xf[:, 1, :], xbad[:], None, ALU.add).then_inc(fx, 1)
            v.wait_ge(turned, 5)
            for h in range(SUP):
                vv.tensor_copy(K.src[:, NET + h::SUP], psX[:, h * NX:(h + 1) * NX])
                ch(vv.tensor_copy(K.rel[:, NET + h::SUP], psX[:, 128 + h * NX:128 + (h + 1) * NX]))


def phase_scores(nc, K, tab0, tabs, edst, ex):
    NI = NIT * SUP
    with Phase(nc, "sc") as p:
        S = p.sb("S", [P, NI, H0])
        M = p.sb("M", [P, NI, H0])
        T = p.sb("T", [P, NI, H0])
        tT = p.sb("tT", [P, NT, H0])
        oh = p.sb("oh", [P, 2, SUP, P])
        ohT = p.sb("ohT", [P, 2, SUP, P])
        SR = p.sb("SR", [ER, EC, H0, P])
        FR = p.sb("FR", [ER, EC, H0, P])
        BR = p.sb("BR", [ER, EC, H0, P])
        di = p.sb("di", [ER, 3, EC, P], I32)
        dn = p.sb("dn", [ER, 3, EC, P])
        pen = p.sb("pen", [ER, 2, EC, P])
        pent = p.sb("pent", [ER, 2, EC, H0])
        carry = p.sb("carry", [H0, 2, NET + 2])
        seq = p.sb("seq", [H0, 2, NET])
        pq = p.sb("pq", [H0, 2, NET])
        cin = p.sb("cin", [ER, 2, EC, H0])
        last_ = p.sb("last_", [ER, 2, EC, H0])
        psO = [p.ps(f"psO{u}", [P, D]) for u in range(2)]
        psT = [p.ps(f"psT{u}", [P, D]) for u in range(2)]
        psS = [p.ps(f"psS{u}", [P, D]) for u in range(4)]
        ld = p.sem("ld"); got = p.gather_sem("got"); ohd = p.sem("ohd"); oht = p.sem("oht"); ohc = p.sem("ohc")
        tdone = p.sem("tdone"); tcop = p.sem("tcop"); vch = p.sem("vch"); st = p.sem("st"); sc = p.sem("sc")
        mt = p.sem("mt"); mc = p.sem("mc"); sx = p.sem("sx"); sy = p.sem("sy"); zr = p.sem("zr"); er = p.sem("er")
        xch = p.sem("xch")
        flat = lambda t: t.rearrange("s e -> (s e)")
        tiles = lambda t: t.rearrange("(c r e) -> r c e", c=EC, e=P)
        b = p.block(K.counted)

        @b.sync
        def _(s):
            s.dma_start(tT[:], tab0[:, D + H0:ROW].rearrange("(t p) h -> p t h", p=P)).then_inc(ld, 16)
            for j in range(3):
                s.dma_start(di[:, j], tiles(flat(edst)[SUP * P - 1 + j:SUP * P - 1 + j + ESLOT])).then_inc(ld, 16)

        @b.gpsimd
        def _(g):
            for j in range(NET):
                g.indirect_dma_start(S[:, j, :], None, tabs,
                                     bass.IndirectOffsetOnAxis(K.src[:, j:j + 1], 0)).then_inc(got, 16)
            g.wait_ge(got, 16 * NET)

        @b.tensor
        def _(t):
            tens = nc.tensor
            t.wait_ge(ld, 64)

            def tscore(n, k, u):
                t.wait_ge(ohd, n + 1)
                blk = t.value_load(K.blk[0:1, ds(n, 1)], min_val=0, max_val=NT - 1)
                for h in range(SUP):
                    ins = tens.transpose(psO[u][:, h * P:(h + 1) * P], oh[:, u, h, :], K.ident[:])
                ins.then_inc(oht, 1)
                t.wait_ge(ohc, n + 1)
                wait(t, tcop, n - 1)
                for h in range(SUP):
                    ins = tens.matmul(psT[u][:, h * H0:(h + 1) * H0], ohT[:, u, h, :],
                                      tT[:, ds(blk, 1), :], start=True, stop=True)
                ins.then_inc(tdone, 1)
            pairs(t, NIT, tscore)
            t.wait_ge(got, 16 * NET)
            for h in range(H0):
                q = h % 4
                wait(t, sc, h - 3)
                for c in range(EC):
                    ins = tens.transpose(psS[q][0:ER, c * P:(c + 1) * P], S[:, c * ER:(c + 1) * ER, h], K.ident[:])
                ins.then_inc(st, 1)
            t.wait_ge(sx, 1)
            for d in range(2):
                for c in range(EC):
                    tens.transpose(psO[d][0:H0, c * ER:(c + 1) * ER], last_[:, d, c, :], K.ident[0:ER, 0:ER])
                    ins = tens.transpose(psT[d][0:H0, c * ER:(c + 1) * ER], pent[:, d, c, :], K.ident[0:ER, 0:ER])
            ins.then_inc(sy, 1)
            t.wait_ge(sx, 2)
            for d in range(2):
                for c in range(EC):
                    ins = tens.transpose(psS[0][0:ER, (d * EC + c) * H0:(d * EC + c + 1) * H0],
                                         carry[:, d, 2 * d + c * ER:2 * d + (c + 1) * ER], K.ident[0:H0, 0:H0])
            ins.then_inc(sy, 1)
            for h in range(H0):
                q = h % 4
                t.wait_ge(sx, 3 + h)
                wait(t, mc, h - 3)
                for c in range(EC):
                    ins = tens.transpose(psS[q][:, c * P:c * P + ER], FR[:, c, h, :], K.ident[0:ER, 0:ER])
                ins.then_inc(mt, 1)

        @b.scalar
        def _(c_):
            sc_ = nc.scalar

            def copy(n, k, u):
                c_.wait_ge(oht, n + 1)
                wait(c_, tdone, n - 1)
                sc_.activation(ohT[:, u], psO[u][:, 0:SUP * P].rearrange("p (h e) -> p h e", h=SUP),
                               ACT.Copy).then_inc(ohc, 1)
            pairs(c_, NIT, copy)
            for h in range(H0):
                c_.wait_ge(st, h + 1)
                sc_.activation(SR[:, :, h, :], psS[h % 4][0:ER, :].rearrange("p (c e) -> p c e", c=EC),
                               ACT.Copy).then_inc(sc, 1)
            for h in range(H0):
                c_.wait_ge(mt, h + 1)
                sc_.activation(M[:, 0:NET, h].rearrange("p (c r) -> p c r", c=EC),
                               psS[h % 4][:, :].rearrange("p (c e) -> p c e", c=EC)[:, :, 0:ER],
                               ACT.Copy).then_inc(mc, 1)
            c_.wait_ge(zr, 1)
            sc_.activation(ex[:, :, 0:H0], S[:], ACT.Exp).then_inc(er, 1)
            c_.wait_ge(er, 1)

        @b.vector
        def _(v):
            vv = nc.vector
            ch = Chain(v, vch)
            v.wait_ge(ld, 64)
            ch(vv.tensor_copy(dn[:], di[:]))
            for d in range(2):
                vv.tensor_tensor(pen[:, d], dn[:, 1], dn[:, 2 * d], ALU.not_equal)
            ch(vv.memset(ex[:, :, H0:EXW], 1.0))
            ch(vv.tensor_scalar(pen[:], pen[:], -BIG, None, ALU.mult))
            for d in range(2):
                ch(vv.tensor_reduce(cin[:, d, :, 0:1], pen[:, d], AX.X, ALU.min))
            ch(vv.tensor_copy(pent[:], cin[:, :, :, 0:1].to_broadcast([ER, 2, EC, H0])))

            def onehot(n, k, u):
                wait(v, oht, n - 1)
                for h in range(SUP):
                    ins = vv.tensor_scalar(oh[:, u, h, :], K.iota[:], K.rel[:, ds(n * SUP + h, 1)], None, ALU.is_equal)
                ins.then_inc(ohd, 1)

            def tcopy(n, k, u):
                v.wait_ge(tdone, n + 1)
                vv.tensor_scalar(T[:, ds(n * SUP, SUP), :], psT[u][:, 0:SUP * H0].rearrange("p (h e) -> p h e", h=SUP),
                                 0.0, None, ALU.add).then_inc(tcop, 1)

            def step(n, k, u):
                if not isinstance(n, int) or n < NIT - 1:
                    onehot(n + 1, k, 1 - u)
                tcopy(n, k, u)
            onehot(0, 0, 0)
            for u in range(2):
                step(u, 0, u)
            with v.Fori(1, NIT // 2 - 1) as k:
                for u in range(2):
                    step(k * 2 + u, k, u)
            for u in range(2):
                step(NIT - 2 + u, 0, u)
            v.wait_ge(tcop, NIT)

            v.wait_ge(sc, H0)
            out2 = (FR, BR)
            rev = lambda t, d: t if d == 0 else t[:, ::-1]

            def scans(first):
                for h in range(H0):
                    for c in range(EC):
                        for d in range(2):
                            init = -BIG if first else cin[:, d, c, h:h + 1]
                            ins = vv.tensor_tensor_scan(rev(out2[d][:, c, h, :], d), rev(pen[:, d, c, :], d),
                                                        rev(SR[:, c, h, :], d), init, ALU.add, ALU.max)
                    ch(ins)
                    if not first:
                        vv.tensor_tensor(FR[:, :, h, :], FR[:, :, h, :], BR[:, :, h, :], ALU.max).then_inc(sx, 1)
            scans(True)
            vv.tensor_copy(last_[:, 0], FR[:, :, :, P - 1])
            vv.tensor_copy(last_[:, 1], BR[:, :, :, 0]).then_inc(sx, 1)
            v.wait_ge(sy, 1)
            ch(vv.memset(carry[:], -BIG))
            for d in range(2):
                vv.tensor_copy(seq[:, d, :], psO[d][0:H0, 0:NET])
                ch(vv.tensor_copy(pq[:, d, :], psT[d][0:H0, 0:NET]))
            for d in range(2):
                ins = vv.tensor_tensor_scan(rev(carry[:, d, 1:1 + NET], d), rev(pq[:, d, :], d),
                                            rev(seq[:, d, :], d), -BIG, ALU.add, ALU.max)
            ins.then_inc(sx, 1)
            v.wait_ge(sy, 2)
            ch(vv.tensor_copy(cin[:], psS[0][0:ER, 0:2 * EC * H0].rearrange("p (d c h) -> p d c h", d=2, c=EC)))
            scans(False)
            v.wait_ge(mc, H0)

            def repeat(x, k, u):
                r = v.value_load(K.xsup[0:1, ds(x, 1)], min_val=0, max_val=NSUP - 1)
                for t in (S, M):
                    ins = vv.tensor_scalar(t[:, ds(x * SUP + NET, SUP), :], t[:, ds(r * SUP, SUP), :], 0.0, None, ALU.add)
                ins.then_inc(xch, 1)
            pairs(v, NX, repeat)
            v.wait_ge(xch, NX)
            for t in (S, M):
                ins = vv.tensor_tensor(t[:], t[:], T[:], ALU.add)
            ch(ins)
            for t in (S, M):
                ins = vv.scalar_tensor_tensor(t[:], t[:], 0.2, t[:], ALU.mult, ALU.max)
            ch(ins)
            vv.tensor_tensor(S[:], S[:], M[:], ALU.subtract).then_inc(zr, 1)


GQ = 4


def phase_aggregate(nc, K, name, table, row, ex, acc):
    with Phase(nc, name) as p:
        nw = EXW if ex is not None else 1
        G = p.sb("G", [P, GQ, SUP, row])
        oh = p.sb("oh", [P, 2, SUP, P])
        psA = [p.ps(f"psA{u}", [P, D]) for u in range(2)]
        psB = [p.ps(f"psB{u}", [P, D]) for u in range(2)]
        got = [p.gather_sem(f"got{q}") for q in range(GQ)]
        ready = p.sem("ready")
        summed = p.sem("summed")
        added = p.sem("added")
        zero = p.sem("zero")
        one = p.sem("one")
        b = p.block(K.counted)

        def quads(eng, body):
            for q in range(GQ):
                body(q, 0, q)
            with eng.Fori(1, NIT // GQ - 1) as k:
                for q in range(GQ):
                    body(k * GQ + q, k, q)
            for q in range(GQ):
                body(NIT - GQ + q, NIT // GQ - 1, q)
        assert NIT % GQ == 0

        @b.gpsimd
        def _(g):
            for n in range(NIT):
                q = n % GQ
                wait(g, summed, n - GQ + 1)
                for h in range(SUP):
                    j = n * SUP + h
                    g.indirect_dma_start(G[:, q, h, :], None, table,
                                         bass.IndirectOffsetOnAxis(K.src[:, j:j + 1], 0)).then_inc(got[q], 16)

        @b.tensor
        def _(t):
            def item(n, k, q):
                u = q % 2
                t.wait_ge(ready, n + 1)
                if ex is None:
                    t.wait_ge(got[q], k * 32 + 32)
                wait(t, added, n - 1)
                for h in range(SUP):
                    nc.tensor.matmul(psA[u][:], oh[:, u, h, :], G[:, q, h, 0:D], start=(h == 0), stop=(h == SUP - 1))
                for h in range(SUP):
                    w = K.ones[:, 0:1] if ex is None else ex[:, ds(n * SUP + h, 1), :]
                    ins = nc.tensor.matmul(psB[u][:, 0:nw], oh[:, u, h, :], w, start=(h == 0), stop=(h == SUP - 1))
                ins.then_inc(summed, 1)
            quads(t, item)

        @b.vector
        def _(v):
            vv = nc.vector
            vv.memset(acc[:, :, 0:D + nw], 0.0).then_inc(zero, 1)
            v.wait_ge(zero, 1)

            def prep(n, k, q):
                u = q % 2
                wait(v, summed, n - 1)
                for h in range(SUP):
                    ins = vv.tensor_scalar(oh[:, u, h, :], K.iota[:], K.rel[:, ds(n * SUP + h, 1)], None, ALU.is_equal)
                if ex is not None:
                    v.wait_ge(got[q], k * 32 + 32)
                    for h in range(SUP):
                        rows = G[:, q, h, 0:D].rearrange("p (h d) -> p h d", h=H0)
                        w = ex[:, ds(n * SUP + h, 1), 0:H0].rearrange("p o h -> p (o h)").unsqueeze(2)
                        ins = vv.tensor_tensor(rows, rows, w.to_broadcast([P, H0, HD]), ALU.mult)
                ins.then_inc(ready, 1)

            def add(n, k, q):
                u = q % 2
                blk = v.value_load(K.blk[0:1, ds(n, 1)], min_val=0, max_val=NT - 1)
                v.wait_ge(summed, n + 1)
                wait(v, added, n)
                a1 = acc[:, ds(blk, 1), 0:D].rearrange("p o d -> p (o d)")
                a2 = acc[:, ds(blk, 1), D:D + nw].rearrange("p o d -> p (o d)")
                vv.tensor_tensor(a1, a1, psA[u][:], ALU.add)
                vv.tensor_tensor(a2, a2, psB[u][:, 0:nw], ALU.add).then_inc(added, 1)

            def step(n, k, q):
                if not isinstance(n, int) or n < NIT - 1:
                    prep(n + 1, k + (q + 1) // GQ, (q + 1) % GQ)
                add(n, k, q)
            prep(0, 0, 0)
            quads(v, step)
            v.wait_ge(added, NIT)


def phase_copy(nc, K, src, out):
    with Phase(nc, "cp") as p:
        d = p.sem("d")
        b = p.block(K.counted)

        @b.sync
        def _(s):
            s.dma_start(out, src[0:N]).then_inc(d, 16)
            s.wait_ge(d, 16)


def rows_of(n):
    return TAIL if last(n) else P


def tile_rows(t, n):
    return t[n * P:N, :] if last(n) else t[ds(n * P, P), :]


def phase_attend(nc, K, a, acc, xmid, tab1, lg):
    with Phase(nc, "at") as p:
        wr = p.sb("wr", [P, KT, E0])
        xt = p.sb("xt", [P, 2, D])
        x1 = p.sb("x1", [P, 2, D])
        den = p.sb("den", [P, NT, H0])
        xn = p.sb("xn", [P, 2, D])
        xnT = p.sb("xnT", [P, 2, D])
        psT = [p.ps(f"psT{u}", [P, D]) for u in range(2)]
        psL = [p.ps(f"psL{u}", [P, D]) for u in range(2)]
        ln = Norm(p, nc)
        wl = p.sem("wl"); normed = p.sem("normed"); turned = p.sem("turned"); copied = p.sem("copied")
        prod = p.sem("prod"); read = p.sem("read"); vch = p.sem("vch"); dch = p.sem("dch")
        xl = [p.sem(f"xl{u}") for u in range(2)]
        st = [p.sem(f"st{u}") for u in range(2)]
        b = p.block(K.counted)

        @b.sync
        def _(s):
            s.dma_start(wr[:], a["L0_ffn_Wr"].rearrange("(kt p) e -> p kt e", p=P)).then_inc(wl, 16)

            def load(n, k, u):
                wait(s, normed, n - 1)
                s.dma_start(xt[0:rows_of(n), u, :], tile_rows(a["x"], n)).then_inc(xl[u], 16)
            pairs(s, NT, load)

        @b.scalar
        def _(c):
            def step(n, k, u):
                ln.scalar(c, n)
                c.wait_ge(normed, n + 1)
                c.dma_start(xmid[ds(n * P, P), :], x1[:, u, :]).then_inc(st[u], 16)
                c.dma_start(tab1[ds(n * P, P), 0:D], xn[:, u, :]).then_inc(st[u], 16)
                c.wait_ge(turned, n + 1)
                nc.scalar.activation(xnT[:, u, :], psT[u][:], ACT.Copy).then_inc(copied, 1)
            pairs(c, NT, step)
            for u in range(2):
                c.wait_ge(st[u], 32 * ((NT + 1 - u) // 2))

        @b.tensor
        def _(t):
            t.wait_ge(wl, 16)

            def tile(n, k, u):
                t.wait_ge(normed, n + 1)
                for kt in range(KT):
                    ins = nc.tensor.transpose(psT[u][:, kt * P:(kt + 1) * P], xn[:, u, kt * P:(kt + 1) * P], K.ident[:])
                ins.then_inc(turned, 1)
                t.wait_ge(copied, n + 1)
                wait(t, read, n - 1)
                for kt in range(KT):
                    ins = nc.tensor.matmul(psL[u][:, 0:E0], xnT[:, u, kt * P:(kt + 1) * P], wr[:, kt, :],
                                           start=(kt == 0), stop=(kt == KT - 1))
                ins.then_inc(prod, 1)
            pairs(t, NT, tile)

        @b.vector
        def _(v):
            vv = nc.vector
            d = Chain(v, dch)
            d(vv.tensor_scalar(den[:], acc[:, :, D:D + H0], 1e-30, None, ALU.max))
            d(vv.reciprocal(den[:], den[:]))

            def norm(n, k, u):
                v.wait_ge(xl[u], k * 16 + 16)
                wait(v, st[u], k * 32)
                ch = Chain(v, vch, n * 2)
                o = x1[:, u, :]
                ch(vv.tensor_tensor(o.rearrange("p (h d) -> p h d", h=H0),
                                    acc[:, ds(n, 1), 0:D].rearrange("p o (h d) -> p (o h) d", h=H0),
                                    den[:, ds(n, 1), :].rearrange("p o h -> p (o h)").unsqueeze(2)
                                    .to_broadcast([P, H0, HD]), ALU.mult))
                ch(vv.tensor_tensor(o, o, xt[:, u, :], ALU.add))
                ln.vector(v, n, o, xn[:, u, :], normed)

            def step(n, k, u):
                if not last(n):
                    norm(n + 1, k + u, 1 - u)
                v.wait_ge(prod, n + 1)
                vv.tensor_scalar(lg[:, ds(n, 1), :].rearrange("p o e -> p (o e)"), psL[u][:, 0:E0], 0.0, None,
                                 ALU.add).then_inc(read, 1)
            norm(0, 0, 0)
            pairs(v, NT, step)
            v.wait_ge(read, NT)


def phase_route0(nc, K, lg, tab1, sid):
    BITS = 30
    W = NT * E0
    S = 16
    with Phase(nc, "r0") as p:
        pv = p.sb("pv", [P, 1])
        v_ = p.sb("v", [P, NT, E0])
        m8 = p.sb("m8", [P, E0])
        m1 = p.sb("m1", [E0, 1])
        dg = p.sb("dg", [E0, E0])
        rs = p.sb("rs", [P, E0])
        thr = p.sb("thr", [P, E0], I32)
        cand = p.sb("cand", [P, E0], I32)
        bit = p.sb("bit", [P, 1], I32)
        msk = p.sb("msk", [P, E0], I32)
        hit = p.sb("hit", [P, NT, E0])
        gt = p.sb("gt", [P, NT, E0])
        need = p.sb("need", [P, E0])
        tot = p.sb("tot", [P, NT, E0])
        inc = p.sb("inc", [P, NT, E0])
        rank = p.sb("rank", [P, NT, E0])
        zero = p.sb("zero", [P, NT])
        tri = p.sb("tri", [P, P])
        ri = p.sb("ri", [P, 3, NT, E0], I32)
        rf = p.sb("rf", [P, 2, NT, E0])
        tio = p.sb("tio", [P, NT])
        oa = p.sb("oa", [P, W, S], BF16)
        ob = p.sb("ob", [P, W, 2, S], BF16)
        obm = p.sb("obm", [P, W, S], BF16)
        idf = p.sb("idf", [S, E0, S])
        idi = p.sb("idi", [S, E0, S], I32)
        ps = [p.ps(f"ps{u}", [P, D]) for u in range(4)]
        psC = [p.ps(f"psC{u}", [P, D]) for u in range(2)]
        g1 = p.sem("g1"); vch = p.sem("vch"); tv = p.sem("tv"); vt = p.sem("vt"); ex = p.sem("ex"); xe = p.sem("xe")
        lc = p.sem("lc"); cs = p.sem("cs"); cd = p.sem("cd"); dd = p.sem("dd"); st = p.sem("st")
        b = p.block(K.counted)

        @b.gpsimd
        def _(g):
            nc.gpsimd.affine_select(out=tri[:], in_=K.ones[:], compare_op=ALU.is_gt, fill=0.0, base=0,
                                    pattern=[[1, P]], channel_multiplier=-1).then_inc(g1, 1)
            nc.gpsimd.iota(tio[:], [[1, NT]], base=0, channel_multiplier=0,
                           allow_small_or_imprecise_dtypes=True).then_inc(g1, 1)

        @b.sync
        def _(s):
            s.wait_ge(dd, 1)
            s.dma_start(tab1[:, D:D + E0].rearrange("(t p) e -> p t e", p=P), v_[:]).then_inc(st, 16)
            s.wait_ge(dd, 2)
            s.dma_start(sid.rearrange("e (a b) -> a e b", b=S), idi[:]).then_inc(st, 16)
            s.wait_ge(st, 32)

        @b.scalar
        def _(c):
            c.wait_ge(ex, 1)
            nc.scalar.activation(v_[:], v_[:], ACT.Exp).then_inc(xe, 1)

        flat = lambda t: t[:].rearrange("p t e -> p (t e)")

        @b.tensor
        def _(t):
            tens = nc.tensor
            t.wait_ge(tv, 1)
            tens.transpose(ps[0][0:E0, 0:P], m8[:], K.ident[:]).then_inc(vt, 1)
            t.wait_ge(tv, 2)
            tens.matmul(ps[1][:, 0:E0], K.ones[0:E0, :], dg[:], start=True, stop=True).then_inc(vt, 1)
            t.wait_ge(tv, 3)
            tens.matmul(ps[2][:, 0:E0], K.ones[:], rs[:], start=True, stop=True).then_inc(vt, 1)

            def count(n, k, u):
                t.wait_ge(cs, n + 1)
                tens.matmul(psC[u][:, 0:E0], K.ones[:], m8[:], start=True, stop=True).then_inc(cd, 1)
            pairs(t, BITS, count)
            t.wait_ge(tv, 4)
            t.wait_ge(g1, 2)
            tens.matmul(ps[0][:, 0:E0], K.ones[:], m8[:], start=True, stop=True)
            tens.matmul(ps[1][:, 0:W], tri[:], flat(hit), start=True, stop=True)
            tens.matmul(ps[2][:, 0:W], K.ones[:], flat(hit), start=True, stop=True).then_inc(vt, 1)
            t.wait_ge(tv, 5)
            tens.matmul(ps[1][:, 0:W], tri[:], flat(hit), start=True, stop=True)
            tens.matmul(ps[2][:, 0:W], K.ones[:], flat(hit), start=True, stop=True).then_inc(vt, 1)
            t.wait_ge(tv, 6)
            for e in range(E0):
                for k in range(NT):
                    ins = tens.matmul(ps[3][0:S, e * 2 * S:(e + 1) * 2 * S], oa[:, k * E0 + e, :],
                                      ob[:, k * E0 + e, :, :].rearrange("p a b -> p (a b)"),
                                      start=(k == 0), stop=(k == NT - 1))
            ins.then_inc(vt, 1)

        @b.vector
        def _(v):
            vv = nc.vector
            ch = Chain(v, vch)
            eh = lambda t: t[:].rearrange("p t e -> p e t")
            bc = lambda t: t.unsqueeze(1).to_broadcast([P, NT, E0])
            v.wait_ge(g1, 2)
            ch(vv.tensor_reduce(pv[:], K.ident[:, 0:TAIL], AX.X, ALU.add))
            ch(vv.memset(zero[:], 0.0))
            lastl = lg[:, NT - 1, :]
            ch(vv.tensor_scalar(lastl, lastl, pv[:], None, ALU.mult))
            ch(vv.tensor_scalar(rank[:, 0, 0:1], pv[:], BIG, -BIG, ALU.mult, ALU.add))
            ch(vv.tensor_scalar(lastl, lastl, rank[:, 0, 0:1], None, ALU.add))
            vv.tensor_reduce(m8[:], eh(lg), AX.X, ALU.max).then_inc(tv, 1)
            v.wait_ge(vt, 1)
            ch(vv.tensor_reduce(m1[:], ps[0][0:E0, 0:P], AX.X, ALU.max))
            vv.tensor_scalar(dg[:], K.ident[0:E0, 0:E0], m1[:], None, ALU.mult).then_inc(tv, 1)
            v.wait_ge(vt, 2)
            vv.tensor_tensor(v_[:], lg[:], bc(ps[1][:, 0:E0]), ALU.subtract).then_inc(ex, 1)
            v.wait_ge(xe, 1)
            vv.tensor_reduce(rs[:], eh(v_), AX.X, ALU.add).then_inc(tv, 1)
            v.wait_ge(vt, 3)
            ch(vv.reciprocal(need[:], ps[2][:, 0:E0]))
            vv.tensor_tensor(v_[:], v_[:], bc(need[:]), ALU.mult).then_inc(dd, 1)
            v.wait_ge(st, 16)
            ch(vv.tensor_scalar(v_[:, NT - 1, :], v_[:, NT - 1, :], pv[:], None, ALU.add))
            ch(vv.tensor_scalar(v_[:, NT - 1, :], v_[:, NT - 1, :], 1.0, None, ALU.subtract))
            ch(vv.memset(thr[:], 0))
            ch(vv.memset(bit[:], 1 << (BITS - 1)))

            def step(n, k, u):
                c = Chain(v, lc, n * 5)
                c(vv.tensor_tensor(cand[:], thr[:], bit[:].to_broadcast([P, E0]), ALU.bitwise_or))
                c(vv.tensor_tensor(hit[:], v_[:], bc(cand[:].bitcast(F32)), ALU.is_ge))
                vv.tensor_reduce(m8[:], eh(hit), AX.X, ALU.add).then_inc(cs, 1)
                v.wait_ge(cd, n + 1)
                c(vv.tensor_scalar(msk[:], psC[u][:, 0:E0], CAP0 - 0.5, -1.0, ALU.is_gt, ALU.mult))
                c(vv.scalar_tensor_tensor(thr[:], msk[:], bit[:], thr[:], ALU.bitwise_and, ALU.bitwise_or))
                c(vv.tensor_single_scalar(bit[:], bit[:], 1, ALU.logical_shift_right))
            pairs(v, BITS, step)
            tf = bc(thr[:].bitcast(F32))
            ch(vv.tensor_tensor(gt[:], v_[:], tf, ALU.is_gt))
            ch(vv.tensor_tensor(hit[:], v_[:], tf, ALU.is_equal))
            vv.tensor_reduce(m8[:], eh(gt), AX.X, ALU.add).then_inc(tv, 1)

            def ranks():
                ch(vv.tensor_copy(flat(tot), ps[2][:, 0:W]))
                for e in range(E0):
                    ins = vv.tensor_tensor_scan(inc[:, :, e], tot[:, :, e], zero[:], 0.0, ALU.add, ALU.add)
                ch(ins)
                ch(vv.tensor_tensor(inc[:], inc[:], tot[:], ALU.subtract))
                ch(vv.tensor_tensor(flat(rank), flat(inc), ps[1][:, 0:W], ALU.add))
            v.wait_ge(vt, 4)
            ch(vv.tensor_scalar(need[:], ps[0][:, 0:E0], -1.0, float(CAP0), ALU.mult, ALU.add))
            ranks()
            ch(vv.tensor_tensor(rank[:], rank[:], bc(need[:]), ALU.is_lt))
            ch(vv.tensor_tensor(hit[:], hit[:], rank[:], ALU.mult))
            vv.tensor_tensor(hit[:], hit[:], gt[:], ALU.add).then_inc(tv, 1)
            v.wait_ge(vt, 5)
            ranks()
            ch(vv.tensor_copy(ri[:, 0], rank[:]))
            ch(vv.tensor_single_scalar(ri[:, 1], ri[:, 0], 4, ALU.arith_shift_right))
            ch(vv.tensor_single_scalar(ri[:, 2], ri[:, 0], S - 1, ALU.bitwise_and))
            ch(vv.tensor_copy(rf[:], ri[:, 1:3]))
            ch(vv.tensor_scalar(gt[:], hit[:], -1000.0, 1000.0, ALU.mult, ALU.add))
            ch(vv.tensor_tensor(rf[:, 0], rf[:, 0], gt[:], ALU.add))
            io = K.iota[:, 0:S].unsqueeze(1).to_broadcast([P, W, S])
            for j, o in ((0, oa), (1, obm)):
                ch(vv.tensor_tensor(o[:], io, rf[:, j].rearrange("p t e -> p (t e)").unsqueeze(2).to_broadcast([P, W, S]),
                                    ALU.is_equal))
            ch(vv.tensor_scalar(ob[:, :, 0, :], obm[:], K.part[:], None, ALU.mult))
            vv.tensor_tensor(ob[:, :, 1, :].rearrange("p (t e) s -> p t e s", e=E0),
                             obm[:].rearrange("p (t e) s -> p t e s", e=E0),
                             tio[:].unsqueeze(2).unsqueeze(3).to_broadcast([P, NT, E0, S]), ALU.mult).then_inc(tv, 1)
            v.wait_ge(vt, 6)
            r = ps[3][0:S, 0:E0 * 2 * S].rearrange("a (e w b) -> a e w b", w=2, b=S)
            ch(vv.tensor_scalar(idf[:], r[:, :, 1, :], float(P), None, ALU.mult))
            ch(vv.tensor_tensor(idf[:], idf[:], r[:, :, 0, :], ALU.add))
            vv.tensor_copy(idi[:], idf[:]).then_inc(dd, 1)


def phase_experts0(nc, K, a, tab1, sid, xmid):
    HC = CAP0 // P
    NJ = E0 * HC
    R = D + E0
    with Phase(nc, "e0") as p:
        ix = p.sb("ix", [P, NJ], I32)
        g = p.sb("g", [P, NJ, R])
        w1 = p.sb("w1", [P, E0, KT, F0])
        w2 = p.sb("w2", [F0, E0, D])
        b1 = p.sb("b1", [F0, E0])
        b2 = p.sb("b2", [P, E0, D])
        xT = p.sb("xT", [P, 2, KT, CAP0])
        hT = p.sb("hT", [F0, 2, CAP0])
        y = p.sb("y", [P, 2, HC, D])
        psT = [p.ps(f"psT{u}", [P, D]) for u in range(4)]
        psH = [p.ps(f"psH{u}", [P, D]) for u in range(2)]
        psY = [p.ps(f"psY{u}", [P, D]) for u in range(2)]
        il = p.sem("il"); wl = p.sem("wl"); got = p.gather_sem("got"); turned = p.sem("turned"); cop = p.sem("cop")
        hd = p.sem("hd"); act = p.sem("act"); yd = p.sem("yd"); yb = p.sem("yb"); yr = p.sem("yr"); sca = p.gather_sem("sca")
        b = p.block(K.counted)

        @b.sync
        def _(s):
            with nc.allow_non_contiguous_dma(reason="slot tokens to one per partition"):
                s.dma_start(ix[:], sid.rearrange("e (c p) -> p (e c)", p=P)).then_inc(il, 16)
            for e in range(E0):
                s.dma_start(w1[:, e], a["L0_ffn_W1"][e].rearrange("(kt p) f -> p kt f", p=P)).then_inc(wl, 16)
            s.dma_start(w2[:], a["L0_ffn_W2"].rearrange("e f d -> f e d")).then_inc(wl, 16)
            with nc.allow_non_contiguous_dma(reason="biases to one per partition"):
                s.dma_start(b1[:], a["L0_ffn_b1"].rearrange("e f -> f e")).then_inc(wl, 16)
            s.dma_start(b2[:].rearrange("p e d -> p (e d)"),
                        a["L0_ffn_b2"].rearrange("e d -> (e d)").partition_broadcast(P)).then_inc(wl, 16)

        @b.gpsimd
        def _(q):
            q.wait_ge(il, 16)
            for j in range(NJ):
                q.indirect_dma_start(g[:, j, :], None, tab1,
                                     bass.IndirectOffsetOnAxis(ix[:, j:j + 1], 0)).then_inc(got, 16)
            for e in range(E0):
                q.wait_ge(yr, HC * (e + 1))
                if e:
                    q.wait_ge(sca, 16 * HC * e)
                for c in range(HC):
                    j = e * HC + c
                    q.indirect_dma_start(xmid, bass.IndirectOffsetOnAxis(ix[:, j:j + 1], 0), y[:, e % 2, c, :], None,
                                         bounds_check=NP - 1, compute_op=ALU.add).then_inc(sca, 16)
            q.wait_ge(sca, 16 * HC * E0)

        @b.tensor
        def _(t):
            tens = nc.tensor
            t.wait_ge(got, 16 * NJ)
            t.wait_ge(wl, 16 * (E0 + 3))
            for e in range(E0):
                u = e % 2
                for c in range(HC):
                    wait(t, cop, 2 * e - 1 + c)
                    for kt in range(KT):
                        ins = tens.transpose(psT[2 * u + c][:, kt * P:(kt + 1) * P],
                                             g[:, e * HC + c, kt * P:(kt + 1) * P], K.ident[:])
                    ins.then_inc(turned, 1)
                t.wait_ge(cop, HC * (e + 1))
                wait(t, act, e - 1)
                for kt in range(KT):
                    ins = tens.matmul(psH[u][:, 0:CAP0], w1[:, e, kt, :], xT[:, u, kt, :],
                                      start=(kt == 0), stop=(kt == KT - 1))
                ins.then_inc(hd, 1)
                t.wait_ge(act, e + 1)
                for c in range(HC):
                    wait(t, yb, HC * e + c - 1)
                    tens.matmul(psY[c][:], hT[:, u, c * P:(c + 1) * P], w2[:, e, :],
                                start=True, stop=True).then_inc(yd, 1)

        @b.scalar
        def _(c_):
            for e in range(E0):
                u = e % 2
                for c in range(HC):
                    c_.wait_ge(turned, HC * e + c + 1)
                    wait(c_, hd, e - 1)
                    nc.scalar.activation(xT[:, u, :, c * P:(c + 1) * P],
                                         psT[2 * u + c][:].rearrange("p (k t) -> p k t", k=KT), ACT.Copy).then_inc(cop, 1)
                c_.wait_ge(hd, e + 1)
                wait(c_, yd, HC * (e - 1))
                nc.scalar.activation(hT[:, u, :], psH[u][:, 0:CAP0], ACT.Gelu, bias=b1[:, e:e + 1]).then_inc(act, 1)
                for c in range(HC):
                    c_.wait_ge(yb, HC * e + c + 1)
                    j = e * HC + c
                    nc.scalar.activation(y[:, u, c, :], y[:, u, c, :], ACT.Copy,
                                         scale=g[:, j, D + e:D + e + 1]).then_inc(yr, 1)

        @b.vector
        def _(v):
            for e in range(E0):
                for c in range(HC):
                    v.wait_ge(yd, HC * e + c + 1)
                    wait(v, sca, 16 * HC * (e - 1))
                    nc.vector.tensor_tensor(y[:, e % 2, c, :], psY[c][:], b2[:, e, :], ALU.add).then_inc(yb, 1)


def phase_norm2(nc, K, xmid, tab2):
    with Phase(nc, "n2") as p:
        xt = p.sb("xt", [P, 2, D])
        xn = p.sb("xn", [P, 2, D])
        ln = Norm(p, nc)
        normed = p.sem("normed")
        xl = [p.sem(f"xl{u}") for u in range(2)]
        st = [p.sem(f"st{u}") for u in range(2)]
        b = p.block(K.counted)

        @b.sync
        def _(s):
            def load(n, k, u):
                wait(s, normed, n - 1)
                s.dma_start(xt[:, u, :], xmid[ds(n * P, P), :]).then_inc(xl[u], 16)
            pairs(s, NT, load)

        @b.scalar
        def _(c):
            def step(n, k, u):
                ln.scalar(c, n)
                c.wait_ge(normed, n + 1)
                c.dma_start(tab2[ds(n * P, P), :], xn[:, u, :]).then_inc(st[u], 16)
            pairs(c, NT, step)
            for u in range(2):
                c.wait_ge(st[u], 16 * ((NT + 1 - u) // 2))

        @b.vector
        def _(v):
            def step(n, k, u):
                v.wait_ge(xl[u], k * 16 + 16)
                wait(v, st[u], k * 16)
                ln.vector(v, n, xt[:, u, :], xn[:, u, :], normed)
            pairs(v, NT, step)


def phase_sage(nc, K, a, acc, tab2, xmid, mv, ys):
    ZT = NOV // (NT - 1)
    assert ZT * (NT - 1) == NOV
    XB = 4
    with Phase(nc, "sg") as p:
        w = p.sb("w", [P, 2 * KT, D])
        bb = p.sb("bb", [P, D])
        deg = p.sb("deg", [P, NT, 1])
        xt = p.sb("xt", [P, XB, D])
        xn = p.sb("xn", [P, 2, 2, D])
        xT = p.sb("xT", [P, 2, 2 * KT, P])
        h = p.sb("h", [P, 2, D])
        sg = p.sb("sg", [P, 2, D])
        x3 = p.sb("x3", [P, 2, D])
        zeros = p.sb("zeros", [P, ZT, D])
        bst = p.sb("bst", [P, 6])
        junk = p.sb("junk", [P, 1])
        bmv = p.sb("bmv", [P, 2])
        psT = [p.ps(f"psT{u}", [P, D]) for u in range(4)]
        psH = [p.ps(f"psH{u}", [P, D]) for u in range(2)]
        wl = p.sem("wl"); md = p.sem("md"); turned = p.sem("turned"); cop = p.sem("cop"); prod = p.sem("prod")
        hs = p.sem("hs"); sgd = p.sem("sgd"); xd = p.sem("xd"); vch = p.sem("vch"); dch = p.sem("dch"); fin = p.sem("fin")
        vf = p.sem("vf"); zr = p.sem("zr"); zs = p.sem("zs")
        xl = [p.sem(f"xl{q}") for q in range(XB)]
        nl = [p.sem(f"nl{u}") for u in range(2)]
        st = [p.sem(f"st{u}") for u in range(2)]
        b = p.block(K.counted)

        @b.sync
        def _(s):
            s.dma_start(w[:, 0:KT], a["L1_gnn_W_l"].rearrange("(k p) d -> p k d", p=P)).then_inc(wl, 16)
            s.dma_start(w[:, KT:], a["L1_gnn_W_r"].rearrange("(k p) d -> p k d", p=P)).then_inc(wl, 16)
            s.dma_start(bb[:], a["L1_gnn_b"].partition_broadcast(P)).then_inc(wl, 16)

            def load(n, k, q):
                if within(n, NT):
                    u = q % 2
                    wait(s, turned, n - 1)
                    s.dma_start(xn[:, u, 1, :], tab2[ds(n * P, P), :]).then_inc(nl[u], 16)
                    wait(s, xd, n - XB + 1)
                    s.dma_start(xt[:, q, :], xmid[ds(n * P, P), :]).then_inc(xl[q], 16)
                    if not last(n):
                        s.dma_start(ys[ds(n * (ZT * P) + E1 * P, ZT * P), :].rearrange("(j p) d -> p j d", p=P),
                                    zeros[:]).then_inc(zs, 16)
            s.wait_ge(zr, 1)
            skewed(s, NT, 0, load, XB)
            s.wait_ge(zs, 16 * (NT - 1))

        @b.gpsimd
        def _(g):
            nc.gpsimd.memset(zeros[:], 0.0).then_inc(zr, 1)

        @b.scalar
        def _(c):
            def step(n, k, q):
                u = q % 2
                if within(n, NT):
                    c.wait_ge(turned, n + 1)
                    wait(c, prod, n - 1)
                    for j in range(2):
                        ins = nc.scalar.activation(xT[:, u, j * KT:(j + 1) * KT, :],
                                                   psT[2 * u + j][:].rearrange("p (k t) -> p k t", k=KT), ACT.Copy)
                    ins.then_inc(cop, 1)
                m = n - 2
                if within(m, NT):
                    c.wait_ge(hs, m + 1)
                    wait(c, xd, m - 1)
                    nc.scalar.activation(sg[:, u, :], h[:, u, :], ACT.Sigmoid).then_inc(sgd, 1)
                m, u = n - 4, q % 2
                if within(m, NT):
                    c.wait_ge(xd, m + 1)
                    c.dma_start(xmid[ds(m * P, P), :], x3[:, u, :]).then_inc(st[u], 16)
            skewed(c, NT, 4, step, XB)
            c.wait_ge(vf, 1)
            nc.scalar.activation(mv[:, :, 1:2], mv[:, :, 1:2], ACT.Sqrt).then_inc(fin, 1)
            for u in range(2):
                c.wait_ge(st[u], 16 * ((NT + 1 - u) // 2))

        @b.tensor
        def _(t):
            t.wait_ge(wl, 48)

            def step(n, k, q):
                u = q % 2
                if within(n, NT):
                    t.wait_ge(md, n + 1)
                    t.wait_ge(nl[u], k * 32 + 16 * (q // 2) + 16)
                    wait(t, cop, n - 1)
                    for j in range(2):
                        for kt in range(KT):
                            ins = nc.tensor.transpose(psT[2 * u + j][:, kt * P:(kt + 1) * P],
                                                      xn[:, u, j, kt * P:(kt + 1) * P], K.ident[:])
                    ins.then_inc(turned, 1)
                m, um = n - 1, 1 - u
                if within(m, NT):
                    t.wait_ge(cop, m + 1)
                    wait(t, hs, m - 1)
                    for kt in range(2 * KT):
                        ins = nc.tensor.matmul(psH[um][:], xT[:, um, kt, :], w[:, kt, :],
                                               start=(kt == 0), stop=(kt == 2 * KT - 1))
                    ins.then_inc(prod, 1)
            skewed(t, NT, 1, step, XB)

        @b.vector
        def _(v):
            vv = nc.vector
            d = Chain(v, dch)
            d(vv.tensor_scalar(deg[:], acc[:, :, D:D + 1], 1.0, None, ALU.max))
            d(vv.reciprocal(deg[:], deg[:]))
            v.wait_ge(wl, 48)

            def step(n, k, q):
                u = q % 2
                if within(n, NT):
                    wait(v, turned, n - 1)
                    vv.tensor_scalar(xn[:, u, 0, :], acc[:, ds(n, 1), 0:D].rearrange("p o d -> p (o d)"),
                                     deg[:, ds(n, 1), :].rearrange("p o d -> p (o d)"), None, ALU.mult).then_inc(md, 1)
                m, um = n - 2, u
                if within(m, NT):
                    v.wait_ge(prod, m + 1)
                    wait(v, sgd, m - 1)
                    vv.tensor_tensor(h[:, um, :], psH[um][:], bb[:], ALU.add).then_inc(hs, 1)
                m, km, qm = back(n, k, q, 3, XB)
                um = qm % 2
                if within(m, NT):
                    v.wait_ge(sgd, m + 1)
                    ch = Chain(v, vch, m * 4)
                    ch(vv.tensor_tensor(sg[:, um, :], sg[:, um, :], h[:, um, :], ALU.mult))
                    v.wait_ge(xl[qm], km * 16 + 16)
                    wait(v, st[um], km * 32 + 16 * (qm // 2))
                    vv.tensor_tensor(x3[:, um, :], sg[:, um, :], xt[:, qm, :], ALU.add).then_inc(xd, 1)
                    v.wait_ge(xd, m + 1)
                    ch(vv.bn_stats(bst[:], x3[:, um, :]))
                    vv.tensor_scalar(junk[:], bst[:, 0:1], 1.0, None, ALU.mult)
                    ch(vv.bn_aggr(bmv[:], bst[:]))
                    ch(vv.tensor_scalar(mv[:, ds(m, 1), :].rearrange("p o d -> p (o d)"), bmv[:], 0.0, None, ALU.add))
            skewed(v, NT, 3, step, XB)
            vv.tensor_scalar(mv[:, :, 1:2], mv[:, :, 1:2], EPS, None, ALU.add).then_inc(vf, 1)
            v.wait_ge(fin, 1)
            d(vv.reciprocal(mv[:, :, 1:2], mv[:, :, 1:2]))


def phase_shared(nc, K, a, xmid, tab3, xsh, sc):
    XB = 4
    with Phase(nc, "sh") as p:
        w13 = p.sb("w13", [P, 2, KT, D])
        w2 = p.sb("w2", [P, KT, D])
        gw = p.sb("gw", [E1, D])
        gT = p.sb("gT", [P, KT, E1])
        xt = p.sb("xt", [P, XB, D])
        xn = p.sb("xn", [P, 2, D])
        xT = p.sb("xT", [P, 2, KT, P])
        sg = p.sb("sg", [P, 2, D])
        hh = p.sb("hh", [P, 2, D])
        hT = p.sb("hT", [P, 2, KT, P])
        z = p.sb("z", [P, 2, D])
        psT = p.ps("psT", [P, D])
        psU = p.ps("psU", [P, D])
        psA = [p.ps(f"psA{u}", [P, D]) for u in range(2)]
        psB = [p.ps(f"psB{u}", [P, D]) for u in range(2)]
        psG = p.ps("psG", [P, D])
        psY = p.ps("psY", [P, D])
        wl = p.sem("wl"); nd = p.sem("nd"); turned = p.sem("turned"); cop = p.sem("cop"); ab = p.sem("ab")
        sgd = p.sem("sgd"); hd = p.sem("hd"); ht = p.sem("ht"); hc = p.sem("hc"); yd = p.sem("yd"); zd = p.sem("zd")
        scd = p.sem("scd"); gt = p.sem("gt"); gc = p.sem("gc"); vch = p.sem("vch")
        xl = [p.sem(f"xl{q}") for q in range(XB)]
        sn = [p.sem(f"sn{u}") for u in range(2)]
        sz = [p.sem(f"sz{u}") for u in range(2)]
        b = p.block(K.counted)

        @b.sync
        def _(s):
            s.dma_start(gw[:], a["L1_ffn_gate_w"]).then_inc(wl, 16)
            for j, nm in enumerate(("L1_ffn_sw1", "L1_ffn_sw3")):
                s.dma_start(w13[:, j], a[nm].rearrange("(k p) d -> p k d", p=P)).then_inc(wl, 16)
            s.dma_start(w2[:], a["L1_ffn_sw2"].rearrange("(k p) d -> p k d", p=P)).then_inc(wl, 16)

            def load(n, k, q):
                if within(n, NT):
                    wait(s, zd, n - XB + 1)
                    s.dma_start(xt[:, q, :], xmid[ds(n * P, P), :]).then_inc(xl[q], 16)
            skewed(s, NT, 0, load, XB)

        @b.scalar
        def _(c):
            c.wait_ge(gt, 1)
            nc.scalar.activation(gT[:], psG[:, 0:KT * E1].rearrange("p (k e) -> p k e", k=KT), ACT.Copy).then_inc(gc, 1)

            def step(n, k, q):
                m, u = n - 1, (q - 1) % 2
                if within(m, NT):
                    c.wait_ge(ab, m + 1)
                    wait(c, hd, m - 1)
                    nc.scalar.activation(sg[:, u, :], psA[u][:], ACT.Sigmoid)
                    nc.scalar.activation(sc[:, ds(m, 1), :].rearrange("p o e -> p (o e)"), psG[:, 0:E1],
                                         ACT.Sigmoid).then_inc(sgd, 1)
                m, u = n - 2, q % 2
                if within(m, NT):
                    c.wait_ge(ht, m + 1)
                    wait(c, yd, m - 1)
                    nc.scalar.activation(hT[:, u], psU[:].rearrange("p (k t) -> p k t", k=KT), ACT.Copy).then_inc(hc, 1)
                if within(n, NT):
                    c.wait_ge(turned, n + 1)
                    wait(c, ab, n - 1)
                    nc.scalar.activation(xT[:, u], psT[:].rearrange("p (k t) -> p k t", k=KT), ACT.Copy).then_inc(cop, 1)
                    c.wait_ge(nd, n + 1)
                    c.dma_start(tab3[ds(n * P, P), :], xn[:, u, :]).then_inc(sn[u], 16)
                m, u = n - 3, (q - 3) % 2
                if within(m, NT):
                    c.wait_ge(zd, m + 1)
                    c.dma_start(xsh[ds(m * P, P), :], z[:, u, :]).then_inc(sz[u], 16)
            skewed(c, NT, 3, step, XB)
            c.wait_ge(sgd, NT)
            for u in range(2):
                c.wait_ge(sn[u], 16 * ((NT + 1 - u) // 2))
                c.wait_ge(sz[u], 16 * ((NT + 1 - u) // 2))

        @b.tensor
        def _(t):
            tens = nc.tensor
            t.wait_ge(wl, 64)
            for kt in range(KT):
                ins = tens.transpose(psG[:, kt * E1:(kt + 1) * E1], gw[:, kt * P:(kt + 1) * P], K.ident[0:E1, 0:E1])
            ins.then_inc(gt, 1)
            t.wait_ge(gc, 1)

            def step(n, k, q):
                m, u = n - 1, (q - 1) % 2
                if within(m, NT):
                    t.wait_ge(cop, m + 1)
                    wait(t, hd, m - 1)
                    wait(t, sgd, m)
                    for kt in range(KT):
                        tens.matmul(psA[u][:], xT[:, u, kt, :], w13[:, 0, kt, :], start=(kt == 0), stop=(kt == KT - 1))
                        tens.matmul(psB[u][:], xT[:, u, kt, :], w13[:, 1, kt, :], start=(kt == 0), stop=(kt == KT - 1))
                        ins = tens.matmul(psG[:, 0:E1], xT[:, u, kt, :], gT[:, kt, :], start=(kt == 0), stop=(kt == KT - 1))
                    ins.then_inc(ab, 1)
                m, u = n - 2, q % 2
                if within(m, NT):
                    t.wait_ge(hd, m + 1)
                    wait(t, hc, m)
                    for kt in range(KT):
                        ins = tens.transpose(psU[:, kt * P:(kt + 1) * P], hh[:, u, kt * P:(kt + 1) * P], K.ident[:])
                    ins.then_inc(ht, 1)
                if within(n, NT):
                    t.wait_ge(nd, n + 1)
                    wait(t, cop, n)
                    for kt in range(KT):
                        ins = tens.transpose(psT[:, kt * P:(kt + 1) * P], xn[:, u, kt * P:(kt + 1) * P], K.ident[:])
                    ins.then_inc(turned, 1)
                if within(m, NT):
                    t.wait_ge(hc, m + 1)
                    wait(t, zd, m)
                    for kt in range(KT):
                        ins = tens.matmul(psY[:], hT[:, u, kt, :], w2[:, kt, :], start=(kt == 0), stop=(kt == KT - 1))
                    ins.then_inc(yd, 1)
            skewed(t, NT, 2, step, XB)

        @b.vector
        def _(v):
            vv = nc.vector

            def step(n, k, q):
                if within(n, NT):
                    u = q % 2
                    v.wait_ge(xl[q], k * 16 + 16)
                    wait(v, turned, n - 1)
                    wait(v, sn[u], k * 32 + 16 * (q // 2))
                    mean = K.mv[:, ds(n, 1), 0:1].rearrange("p o d -> p (o d)")
                    rstd = K.mv[:, ds(n, 1), 1:2].rearrange("p o d -> p (o d)")
                    vv.tensor_scalar(xn[:, u, :], xt[:, q, :], mean, rstd, ALU.subtract, ALU.mult).then_inc(nd, 1)
                m, km, qm = back(n, k, q, 2, XB)
                if within(m, NT):
                    u = qm % 2
                    v.wait_ge(sgd, m + 1)
                    ch = Chain(v, vch, m)
                    ch(vv.tensor_tensor(sg[:, u, :], sg[:, u, :], psA[u][:], ALU.mult))
                    wait(v, ht, m - 1)
                    vv.tensor_tensor(hh[:, u, :], sg[:, u, :], psB[u][:], ALU.mult).then_inc(hd, 1)
                m, km, qm = back(n, k, q, 3, XB)
                if within(m, NT):
                    u = qm % 2
                    v.wait_ge(yd, m + 1)
                    wait(v, sz[u], km * 32 + 16 * (qm // 2))
                    vv.tensor_tensor(z[:, u, :], psY[:], xt[:, qm, :], ALU.add).then_inc(zd, 1)
            skewed(v, NT, 3, step, XB)


def phase_route1(nc, K, sc):
    W = NT * E1
    CH = 5
    TC = NT // CH
    with Phase(nc, "r1") as p:
        top = p.sb("top", [P, NT, 8])
        tix = p.sb("tix", [P, NT, 8], U32)
        exf = p.sb("exf", [P, NT, TOP])
        den = p.sb("den", [P, NT, 1])
        ok = p.sb("ok", [P, NT, TOP])
        oh = p.sb("oh", [P, TOP, NT, E1])
        both = p.sb("both", [P, NT, E1])
        within = p.sb("within", [P, NT, E1])
        tot = p.sb("tot", [P, E1, NT])
        keep = p.sb("keep", [P, E1, NT])
        inc = p.sb("inc", [P, E1, NT])
        n_e = p.sb("n_e", [P, E1])
        ni = p.sb("ni", [P, 2, E1], I32)
        ovt = p.sb("ovt", [P, E1])
        ovi = p.sb("ovi", [P, E1])
        ovx = p.sb("ovx", [P, E1])
        zero = p.sb("zero", [P, E1])
        pos = p.sb("pos", [P, NT, TOP])
        ovb = p.sb("ovb", [P, NT, TOP])
        qi = p.sb("qi", [P, 3, NT, TOP], I32)
        qf = p.sb("qf", [P, 2, NT, TOP])
        far = p.sb("far", [P, NT, TOP])
        item = p.sb("item", [P, NT, TOP])
        valid = p.sb("valid", [P, NT, TOP])
        tmp = p.sb("tmp", [P, NT, TOP])
        oq = p.sb("oq", [P, 1])
        pv = p.sb("pv", [P, 1])
        tri = p.sb("tri", [P, P])
        tio = p.sb("tio", [P, NT, TOP])
        oa = p.sb("oa", [P, 2, NI1], BF16)
        ob = p.sb("ob", [P, 2, 2, P], BF16)
        idf = p.sb("idf", [NI1, P])
        ps = [p.ps(f"ps{u}", [P, D]) for u in range(4)]
        psI = p.ps("psI", [P, D])
        psT = p.ps("psT", [P, D])
        g1 = p.sem("g1"); vch = p.sem("vch"); tv = p.sem("tv"); vt = p.sem("vt"); od = p.sem("od"); om = p.sem("om")
        oc = p.sem("oc")
        b = p.block(K.counted)

        @b.gpsimd
        def _(g):
            nc.gpsimd.affine_select(out=tri[:], in_=K.ones[:], compare_op=ALU.is_gt, fill=0.0, base=0,
                                    pattern=[[1, P]], channel_multiplier=-1).then_inc(g1, 1)
            nc.gpsimd.iota(tio[:], [[1, NT], [0, TOP]], base=0, channel_multiplier=0,
                           allow_small_or_imprecise_dtypes=True).then_inc(g1, 1)

        @b.tensor
        def _(t):
            tens = nc.tensor
            t.wait_ge(g1, 2)
            for c in range(CH):
                t.wait_ge(tv, 1 + c)
                cols = both[:, c * TC:(c + 1) * TC, :].rearrange("p t e -> p (t e)")
                tens.matmul(ps[0][:, 0:TC * E1], tri[:], cols, start=True, stop=True)
                tens.matmul(ps[1][:, 0:TC * E1], K.ones[:], cols, start=True, stop=True).then_inc(vt, 1)
            t.wait_ge(tv, CH + 2)
            tens.matmul(ps[2][0:1, 0:P], oq[:], K.ident[:], start=True, stop=True).then_inc(vt, 1)

            def pairm(n, k, u):
                t.wait_ge(od, n + 1)
                ins = tens.matmul(psI[0:NI1, 0:2 * P], oa[:, u, :], ob[:, u].rearrange("p w b -> p (w b)"),
                                  start=isinstance(n, int) and n == 0, stop=isinstance(n, int) and n == NT * TOP - 1,
                                  skip_group_check=True)
                ins.then_inc(om, 1)
            for u in range(2):
                pairm(u, 0, u)
            with t.Fori(1, NT - 1) as k:
                for u in range(2):
                    pairm(k * 2 + u, k, u)
            for u in range(2):
                pairm(NT * TOP - 2 + u, NT - 1, u)
            t.wait_ge(oc, 1)
            tens.transpose(psT[:, 0:NI1], idf[:], K.ident[0:NI1, 0:NI1]).then_inc(vt, 1)

        @b.vector
        def _(v):
            vv = nc.vector
            ch = Chain(v, vch)
            v.wait_ge(g1, 2)
            for n in range(NT):
                ins = vv.max(top[:, n, :], sc[:, n, :])
            ch(ins)
            for n in range(NT):
                ins = vv.max_index(tix[:, n, :], top[:, n, :], sc[:, n, :])
            ch(ins)
            ch(vv.tensor_copy(exf[:], tix[:, :, 0:TOP]))
            ch(vv.tensor_tensor(den[:], top[:, :, 0:1], top[:, :, 1:2], ALU.add))
            ch(vv.tensor_scalar(den[:], den[:], 1e-20, None, ALU.add))
            ch(vv.reciprocal(den[:], den[:]))
            ch(vv.tensor_tensor(ok[:], top[:, :, 0:TOP], den[:].to_broadcast([P, NT, TOP]), ALU.mult))
            ch(vv.tensor_reduce(pv[:], K.ident[:, 0:TAIL], AX.X, ALU.add))
            ch(vv.tensor_scalar(pv[:], pv[:], -1000.0, 1000.0, ALU.mult, ALU.add))
            ch(vv.tensor_scalar(exf[:, NT - 1, :], exf[:, NT - 1, :], pv[:], None, ALU.add))
            io = K.iota[:, 0:E1].unsqueeze(1).to_broadcast([P, NT, E1])
            for k in range(TOP):
                ins = vv.tensor_tensor(oh[:, k], io, exf[:, :, k:k + 1].to_broadcast([P, NT, E1]), ALU.is_equal)
            ch(ins)
            vv.memset(zero[:], 0.0)
            ch(vv.memset(keep[:], 1.0))
            ch(vv.memset(keep[:, :, 0:1], 0.0))
            vv.tensor_tensor(both[:], oh[:, 0], oh[:, 1], ALU.add).then_inc(tv, 1)
            for c in range(CH):
                v.wait_ge(vt, 1 + c)
                vv.tensor_copy(within[:, c * TC:(c + 1) * TC, :].rearrange("p t e -> p (t e)"), ps[0][:, 0:TC * E1])
                vv.tensor_copy(tot[:, :, c * TC:(c + 1) * TC],
                               ps[1][:, 0:TC * E1].rearrange("p (t e) -> p e t", e=E1)).then_inc(tv, 1)
            v.wait_ge(tv, CH + 1)
            fl = lambda t: t[:].rearrange("p e t -> p (e t)")
            ch(vv.tensor_tensor_scan(fl(inc), fl(keep), fl(tot), 0.0, ALU.mult, ALU.add))
            ch(vv.tensor_scalar(n_e[:], inc[:, :, NT - 1], float(CAP1), None, ALU.min))
            ch(vv.tensor_tensor(inc[:], inc[:], tot[:], ALU.subtract))
            ch(vv.tensor_tensor(within[:], within[:], inc[:].rearrange("p e t -> p t e"), ALU.add))
            ch(vv.tensor_scalar(n_e[:], n_e[:], -1.0, None, ALU.add))
            ch(vv.tensor_copy(ni[:, 0], n_e[:]))
            ch(vv.tensor_single_scalar(ni[:, 1], ni[:, 0], 7, ALU.arith_shift_right))
            ch(vv.tensor_copy(ovt[:], ni[:, 1]))
            ch(vv.tensor_scalar(ovt[:], ovt[:], 0.0, None, ALU.max))
            ch(vv.tensor_tensor_scan(ovi[:], ovt[:], zero[:], 0.0, ALU.add, ALU.add))
            ch(vv.tensor_scalar(ovx[0:1, 0:1], ovi[0:1, E1 - 1:E1], float(E1 - 1), None, ALU.add))
            ch(vv.tensor_copy(K.nov[:], ovx[0:1, 0:1]))
            ch(vv.tensor_single_scalar(K.nov[:], K.nov[:], 2, ALU.arith_shift_right))
            ch(vv.tensor_tensor(ovx[:], ovi[:], ovt[:], ALU.subtract))
            ch(vv.tensor_scalar(zero[:], ovi[:], K.part[:], None, ALU.is_le))
            ch(vv.tensor_reduce(oq[:], zero[:], AX.X, ALU.add))
            vv.tensor_scalar(oq[:], oq[:], float(E1 - 1), None, ALU.min).then_inc(tv, 1)
            v.wait_ge(vt, CH + 1)
            ch(vv.tensor_copy(K.ovf[:], ps[2][0:1, 0:P]))
            for k in range(TOP):
                ch(vv.tensor_tensor(both[:], oh[:, k], within[:], ALU.mult))
                ch(vv.tensor_reduce(pos[:, :, k], both[:], AX.X, ALU.add))
                ch(vv.tensor_tensor(both[:], oh[:, k], ovx[:].unsqueeze(1).to_broadcast([P, NT, E1]), ALU.mult))
                ch(vv.tensor_reduce(ovb[:, :, k], both[:], AX.X, ALU.add))
            ch(vv.tensor_copy(qi[:, 0], pos[:]))
            ch(vv.tensor_single_scalar(qi[:, 1], qi[:, 0], 7, ALU.arith_shift_right))
            ch(vv.tensor_single_scalar(qi[:, 2], qi[:, 0], P - 1, ALU.bitwise_and))
            ch(vv.tensor_copy(qf[:], qi[:, 1:3]))
            ch(vv.tensor_scalar(far[:], qf[:, 0], 0.5, None, ALU.is_gt))
            ch(vv.tensor_tensor(tmp[:], qf[:, 0], ovb[:], ALU.add))
            ch(vv.tensor_scalar(tmp[:], tmp[:], float(E1 - 1), None, ALU.add))
            ch(vv.tensor_tensor(tmp[:], tmp[:], exf[:], ALU.subtract))
            ch(vv.tensor_tensor(tmp[:], tmp[:], far[:], ALU.mult))
            ch(vv.tensor_tensor(item[:], tmp[:], exf[:], ALU.add))
            ch(vv.tensor_scalar(valid[:], pos[:], float(CAP1), None, ALU.is_lt))
            ch(vv.tensor_scalar(tmp[:], item[:], float(P), None, ALU.mult))
            ch(vv.tensor_tensor(tmp[:], tmp[:], qf[:, 1], ALU.add))
            ch(vv.tensor_tensor(tmp[:], tmp[:], valid[:], ALU.mult))
            ch(vv.tensor_scalar(tmp[:], tmp[:], float(NI1 * P - 1), None, ALU.min))
            ch(vv.tensor_copy(K.pair[:], tmp[:]))
            ch(vv.tensor_scalar(ok[:], ok[:], ROUTE_SCALE, None, ALU.mult))
            ch(vv.tensor_tensor(K.gate[:], ok[:], valid[:], ALU.mult))
            ch(vv.tensor_scalar(valid[:], valid[:], -1000.0, 1000.0, ALU.mult, ALU.add))
            ch(vv.tensor_tensor(item[:], item[:], valid[:], ALU.add))
            fi = item[:].rearrange("p t k -> p (t k)")
            lo = qf[:, 1].rearrange("p t k -> p (t k)")
            ti = tio[:].rearrange("p t k -> p (t k)")

            def pairo(n, k, u):
                wait(v, om, n - 1)
                vv.tensor_scalar(oa[:, u, :], K.iota[:, 0:NI1], fi[:, ds(n, 1)], None, ALU.is_equal)
                vv.tensor_scalar(ob[:, u, 0, :], K.iota[:], lo[:, ds(n, 1)], K.part[:], ALU.is_equal, ALU.mult)
                vv.tensor_scalar(ob[:, u, 1, :], K.iota[:], lo[:, ds(n, 1)], ti[:, ds(n, 1)], ALU.is_equal,
                                 ALU.mult).then_inc(od, 1)
            pairs(v, NT * TOP, pairo)
            v.wait_ge(om, NT * TOP)
            ch(vv.tensor_scalar(idf[:], psI[0:NI1, P:2 * P], float(P), None, ALU.mult))
            vv.tensor_tensor(idf[:], idf[:], psI[0:NI1, 0:P], ALU.add).then_inc(oc, 1)
            v.wait_ge(vt, CH + 2)
            ch(vv.tensor_copy(K.slot[:], psT[:, 0:NI1]))


def phase_experts1(nc, K, a, tab3, ys):
    NW = 4
    FT = F1 // P
    with Phase(nc, "e1") as p:
        g = p.sb("g", [P, NW, D])
        w13 = p.sb("w13", [P, NW, KT, 2 * F1])
        w2 = p.sb("w2", [P, NW, FT, D])
        xT = p.sb("xT", [P, 2, KT, P])
        sg = p.sb("sg", [P, 2, F1])
        hh = p.sb("hh", [P, 2, F1])
        hT = p.sb("hT", [P, 2, FT, P])
        y = p.sb("y", [P, NW, D])
        fin = p.sb("fin", [1, 1])
        psX = [p.ps(f"psX{u}", [P, D]) for u in range(2)]
        psH = [p.ps(f"psH{u}", [P, D]) for u in range(2)]
        psU = [p.ps(f"psU{u}", [P, D]) for u in range(2)]
        psY = [p.ps(f"psY{u}", [P, D]) for u in range(2)]
        got = [p.gather_sem(f"got{q}") for q in range(NW)]
        wl = [p.sem(f"wl{q}") for q in range(NW)]
        vl = [p.sem(f"vl{q}") for q in range(NW)]
        st = [p.sem(f"st{q}") for q in range(NW)]
        turned = p.sem("turned")
        cop = p.sem("cop")
        up = p.sem("up")
        sgd = p.sem("sgd")
        hd = p.sem("hd")
        ht = p.sem("ht")
        hc = p.sem("hc")
        yd = p.sem("yd")
        yc = p.sem("yc")
        vch = p.sem("vch")
        b = p.block(K.counted)

        def turns(eng):
            return eng.value_load(K.nov[0:1, 0:1], min_val=E1 // NW - 1, max_val=NI1 // NW - 1)

        def prev(n, k, q, j):
            return n - j, k + (q - j) // NW, (q - j) % NW

        def n_ok(n, q, j):
            if ended[0]:
                return q < j
            return not isinstance(n, int) or n >= j

        ended = [False]

        def run(eng, skew, step):
            nt = turns(eng)
            first = 2
            for n in range(first * NW):
                step(n, n // NW, n % NW)
            with eng.Fori(first, nt + 1) as k:
                for q in range(NW):
                    step(k * NW + q, k, q)
            ended[0] = True
            for q in range(skew):
                step(nt * NW + (NW + q), nt + 1, q)
            ended[0] = False
            return nt

        def load(s, n, k, q, e):
            wait(s, up, n - NW + 1)
            for j, nm in enumerate(("L1_ffn_w1", "L1_ffn_w3")):
                s.dma_start(w13[:, q, :, j * F1:(j + 1) * F1],
                            a[nm][ds(e, 1)].rearrange("o (k p) f -> p (o k) f", p=P)).then_inc(wl[q], 16)
            wait(s, yd, n - NW + 1)
            s.dma_start(w2[:, q], a["L1_ffn_w2"][ds(e, 1)].rearrange("o (k p) d -> p (o k) d", p=P)).then_inc(vl[q], 16)

        @b.sync
        def _(s):
            for q in range(NW):
                load(s, q, 0, q, q)
            with s.Fori(1, E1 // NW) as k:
                for q in range(NW):
                    load(s, k * NW + q, k, q, k * NW + q)
            with s.Fori(E1 // NW, turns(s) + 1) as k:
                for q in range(NW):
                    e = s.value_load(K.ovf[0:1, ds(k * NW + (q - E1), 1)], min_val=0, max_val=E1 - 1)
                    load(s, k * NW + q, k, q, e)

        @b.gpsimd
        def _(g_):
            def gather(n):
                wait(g_, turned, n - NW + 1)
                g_.indirect_dma_start(g[:, n % NW, :], None, tab3,
                                      bass.IndirectOffsetOnAxis(K.slot[:, n:n + 1], 0)).then_inc(got[n % NW], 16)
            for n in range(E1):
                gather(n)
            nt = turns(g_)
            for k in range(E1 // NW, NI1 // NW):
                with g_.If(nt > k - 1):
                    for q in range(NW):
                        gather(k * NW + q)

        @b.tensor
        def _(t):
            tens = nc.tensor

            def step(n, k, q):
                u = q % 2
                m, km, qm = prev(n, k, q, 1)
                if n_ok(n, q, 1):
                    um = qm % 2
                    t.wait_ge(cop, m + 1)
                    t.wait_ge(wl[qm], km * 32 + 32)
                    wait(t, hd, m - 1)
                    for kt in range(KT):
                        ins = tens.matmul(psH[um][:], xT[:, um, kt, :], w13[:, qm, kt, :],
                                          start=(kt == 0), stop=(kt == KT - 1))
                    ins.then_inc(up, 1)
                m, km, qm = prev(n, k, q, 2)
                um = qm % 2
                if n_ok(n, q, 2):
                    t.wait_ge(hd, m + 1)
                    wait(t, hc, m - 1)
                    for c in range(FT):
                        ins = tens.transpose(psU[um][:, c * P:(c + 1) * P], hh[:, um, c * P:(c + 1) * P], K.ident[:])
                    ins.then_inc(ht, 1)
                if n_ok(n, q, 0):
                    t.wait_ge(got[q], k * 16 + 16)
                    wait(t, cop, n - 1)
                    for kt in range(KT):
                        ins = tens.transpose(psX[u][:, kt * P:(kt + 1) * P], g[:, q, kt * P:(kt + 1) * P], K.ident[:])
                    ins.then_inc(turned, 1)
                if n_ok(n, q, 2):
                    t.wait_ge(hc, m + 1)
                    t.wait_ge(vl[qm], km * 16 + 16)
                    wait(t, yc, m - 1)
                    for c in range(FT):
                        ins = tens.matmul(psY[um][:], hT[:, um, c, :], w2[:, qm, c, :], start=(c == 0), stop=(c == FT - 1))
                    ins.then_inc(yd, 1)
            run(t, 2, step)

        @b.scalar
        def _(c):
            def step(n, k, q):
                m, km, qm = prev(n, k, q, 1)
                um = qm % 2
                if n_ok(n, q, 1):
                    c.wait_ge(up, m + 1)
                    nc.scalar.activation(sg[:, um, :], psH[um][:, 0:F1], ACT.Sigmoid).then_inc(sgd, 1)
                m, km, qm = prev(n, k, q, 2)
                um = qm % 2
                if n_ok(n, q, 2):
                    c.wait_ge(ht, m + 1)
                    wait(c, yd, m - 1)
                    nc.scalar.activation(hT[:, um], psU[um][:, 0:F1].rearrange("p (c t) -> p c t", t=P),
                                         ACT.Copy).then_inc(hc, 1)
                if n_ok(n, q, 0):
                    u = q % 2
                    c.wait_ge(turned, n + 1)
                    wait(c, up, n - 1)
                    nc.scalar.activation(xT[:, u], psX[u][:].rearrange("p (k t) -> p k t", k=KT), ACT.Copy).then_inc(cop, 1)
                m, km, qm = prev(n, k, q, 3)
                if n_ok(n, q, 3):
                    c.wait_ge(yc, m + 1)
                    c.dma_start(ys[ds(m * P, P), :], y[:, qm, :]).then_inc(st[qm], 16)
            nt = run(c, 3, step)
            for q in range(NW):
                c.wait_ge(st[q], nt * 16 + 16)
            nc.scalar.activation(fin[:], K.part[0:1, :], ACT.Copy)

        @b.vector
        def _(v):
            vv = nc.vector

            def step(n, k, q):
                m, km, qm = prev(n, k, q, 1)
                um = qm % 2
                if n_ok(n, q, 1):
                    v.wait_ge(sgd, m + 1)
                    ch = Chain(v, vch, m)
                    ch(vv.tensor_tensor(sg[:, um, :], sg[:, um, :], psH[um][:, 0:F1], ALU.mult))
                    wait(v, ht, m - 1)
                    vv.tensor_tensor(hh[:, um, :], sg[:, um, :], psH[um][:, F1:2 * F1], ALU.mult).then_inc(hd, 1)
                m, km, qm = prev(n, k, q, 2)
                um = qm % 2
                if n_ok(n, q, 2):
                    v.wait_ge(yd, m + 1)
                    wait(v, st[qm], km * 16)
                    vv.tensor_copy(y[:, qm, :], psY[um][:]).then_inc(yc, 1)
            run(v, 2, step)


def phase_combine(nc, K, xsh, ys, out):
    with Phase(nc, "cb") as p:
        z = p.sb("z", [P, 2, D])
        g = p.sb("g", [P, 2, TOP, D])
        o = p.sb("o", [P, 2, D])
        zl = [p.sem(f"zl{u}") for u in range(2)]
        got = [p.gather_sem(f"got{u}") for u in range(2)]
        st = [p.sem(f"st{u}") for u in range(2)]
        half = p.sem("half"); od = p.sem("od")
        b = p.block(K.counted)

        @b.sync
        def _(s):
            def load(n, k, u):
                wait(s, od, n - 1)
                s.dma_start(z[:, u, :], xsh[ds(n * P, P), :]).then_inc(zl[u], 16)
            pairs(s, NT, load)

        @b.gpsimd
        def _(q):
            for n in range(NT):
                wait(q, od, n - 1)
                for k in range(TOP):
                    q.indirect_dma_start(g[:, n % 2, k, :], None, ys,
                                         bass.IndirectOffsetOnAxis(K.pair[:, n, k:k + 1], 0)).then_inc(got[n % 2], 16)

        @b.scalar
        def _(c):
            def store(n, k, u):
                c.wait_ge(od, n + 1)
                c.dma_start(tile_rows(out, n), o[0:rows_of(n), u, :]).then_inc(st[u], 16)
            pairs(c, NT, store)
            for u in range(2):
                c.wait_ge(st[u], 16 * ((NT + 1 - u) // 2))

        @b.vector
        def _(v):
            def step(n, k, u):
                v.wait_ge(zl[u], k * 16 + 16)
                v.wait_ge(got[u], k * 32 + 32)
                wait(v, st[u], k * 16)
                w = lambda j: K.gate[:, ds(n, 1), j:j + 1].rearrange("p o d -> p (o d)")
                nc.vector.scalar_tensor_tensor(o[:, u, :], g[:, u, 0, :], w(0), z[:, u, :], ALU.mult, ALU.add).then_inc(half, 1)
                v.wait_ge(half, n + 1)
                nc.vector.scalar_tensor_tensor(o[:, u, :], g[:, u, 1, :], w(1), o[:, u, :], ALU.mult, ALU.add).then_inc(od, 1)
            pairs(v, NT, step)


def kernel(**inputs):
    import concourse.bacc as bacc
    from concourse.bass_utils import run_bass_kernel_spmd as run

    nc = bacc.Bacc("TRN2", target_bir_lowering=False, num_devices=1)
    arrays, aps = {}, {}
    for name, value in inputs.items():
        v = np.ascontiguousarray(value)
        arrays[f"in_{name}"] = v
        aps[name] = nc.dram_tensor(f"in_{name}", v.shape, mybir.dt.from_np(v.dtype), kind="ExternalInput").ap()
    out = nc.dram_tensor("out_x", (N, D), F32, kind="ExternalOutput").ap()
    build(nc, aps, out, 9)
    return run(nc, [arrays], core_ids=[0]).results[0]["out_x"]
```

```python
from contextlib import ExitStack

import numpy as np

import concourse.bass as bass
from concourse import mybir

ALU = mybir.AluOpType
ACT = mybir.ActivationFunctionType
AX = mybir.AxisListType
F32 = mybir.dt.float32
BF16 = mybir.dt.bfloat16
I32 = mybir.dt.int32
U32 = mybir.dt.uint32
ds = bass.ds

P = 128
N = 3125
D = 512
KT = D // P
NT = -(-N // P)
NP = NT * P
TAIL = N - (NT - 1) * P
E = 50000
H0 = 8
HD = D // H0
SUP = 2
NSUP = -(-E // (P * SUP))
NET = NSUP * SUP
ESLOT = NET * P
NX = NT - 1
NIT = NSUP + NX
EC = 4
ER = NET // EC
BIG = 1.0e30
FAR = 1 << 20
EXW = H0 + 1
EPS = 1e-5
E0, F0, CAP0 = 8, 128, 256
E1, F1, TOP, CAP1 = 64, 256, 2, 1024
ROUTE_SCALE = 2.5
NOV = (N * TOP) // P
NI1 = E1 + NOV
assert NI1 <= P and NET % EC == 0 and ER <= P and NET * P >= E


def pairs(eng, count, body):
    for u in range(2):
        body(u, 0, u)
    with eng.Fori(1, count // 2) as k:
        for u in range(2):
            body(k * 2 + u, k, u)
    if count % 2:
        body(count - 1, count // 2, 0)


def skewed(eng, count, skew, body, unroll=2, total=None):
    first = -(-(skew + 2) // unroll)
    for n in range(first * unroll):
        body(n, n // unroll, n % unroll)
    turns = count // unroll if total is None else total
    with eng.Fori(first, turns) as k:
        for u in range(unroll):
            body(k * unroll + u, k, u)
    if total is None:
        for n in range(turns * unroll, count + skew):
            body(n, n // unroll, n % unroll)
    else:
        for u in range(skew):
            body(total * unroll + u, total, u)


def back(n, k, u, j, unroll=2):
    return n - j, k + (u - j) // unroll, (u - j) % unroll


def within(n, count):
    return not isinstance(n, int) or 0 <= n < count


def wait(eng, sem, value):
    if not isinstance(value, int) or value > 0:
        eng.wait_ge(sem, value)


def last(n):
    return isinstance(n, int) and n == NT - 1


class Chain:

    def __init__(self, eng, sem, base=0):
        self.eng, self.sem, self.base, self.n = eng, sem, base, 0

    def __call__(self, ins):
        self.n += 1
        ins.then_inc(self.sem, 1)
        self.eng.wait_ge(self.sem, self.base + self.n)


class Phase:

    def __init__(self, nc, name):
        self.nc, self.name, self.ctx, self.sems = nc, name, ExitStack(), []

    def __enter__(self):
        self.ctx.__enter__()
        return self

    def __exit__(self, *a):
        return self.ctx.__exit__(*a)

    def sb(self, name, shape, dt=F32):
        return self.ctx.enter_context(self.nc.sbuf_tensor(f"{self.name}_{name}", shape, dt))

    def ps(self, name, shape, dt=F32):
        return self.ctx.enter_context(self.nc.psum_tensor(f"{self.name}_{name}", shape, dt))

    def sem(self, name):
        s = self.ctx.enter_context(self.nc.semaphore(f"{self.name}_{name}"))
        self.sems.append(s.num)
        return s

    def gather_sem(self, name):
        return self.nc.alloc_semaphore(f"{self.name}_{name}")

    def block(self, counted):
        if counted & set(self.sems):
            with self.nc.Block() as b:
                @b.gpsimd
                def _(g):
                    for n in sorted(counted):
                        if n - 1 not in counted:
                            end = n
                            while end in counted:
                                end += 1
                            g.sem_clear(range(n, end))
            counted.clear()
        counted |= set(self.sems)
        return self.ctx.enter_context(self.nc.Block())


class Shared:

    def __init__(self):
        self.counted = set()


class Norm:

    def __init__(self, p, nc):
        self.nc = nc
        self.st = p.sb("ln_st", [P, 2, 6])
        self.mv = p.sb("ln_mv", [P, 2, 2])
        self.sd = p.sb("ln_sd", [P, 2, 2])
        self.fo = p.sb("ln_fo", [P, 2, 2])
        self.junk = p.sb("ln_junk", [P, 1])
        self.stat = p.sem("ln_stat")
        self.inv = p.sem("ln_inv")
        self.var = p.sem("ln_var")
        self.root = p.sem("ln_root")
        self.ready = p.sem("ln_ready")

    def scale(self, u):
        return self.fo[:, u, 0:1]

    def offset(self, u):
        return self.fo[:, u, 1:2]

    def stats(self, v, n, u, x):
        ch, vv = Chain(v, self.stat, n * 2), self.nc.vector
        ch(vv.bn_stats(self.st[:, u], x))
        vv.tensor_scalar(self.junk[:], self.st[:, u, 0:1], 1.0, None, ALU.mult)
        ch(vv.bn_aggr(self.mv[:, u], self.st[:, u]))
        vv.tensor_scalar(self.sd[:, u, 0:1], self.mv[:, u, 1:2], EPS, None, ALU.add).then_inc(self.var, 1)

    def finish(self, v, n, u, applied):
        ch, vv = Chain(v, self.inv, n), self.nc.vector
        wait(v, applied, n - 1)
        v.wait_ge(self.root, n + 1)
        ch(vv.reciprocal(self.fo[:, u, 0:1], self.sd[:, u, 1:2]))
        vv.scalar_tensor_tensor(self.fo[:, u, 1:2], self.mv[:, u, 0:1], -1.0, self.fo[:, u, 0:1],
                                ALU.mult, ALU.mult).then_inc(self.ready, 1)

    def scalar(self, c, n, u):
        c.wait_ge(self.var, n + 1)
        self.nc.scalar.activation(self.sd[:, u, 1:2], self.sd[:, u, 0:1], ACT.Sqrt).then_inc(self.root, 1)


def build(nc, a, out, stop):
    dram = lambda name, shape, dt=F32: nc.dram_tensor(name, shape, dt, kind="Internal").ap()
    tab0 = dram("tab0", [NP, D])
    tabs = dram("tabs", [NP, H0])
    esrc = dram("esrc", [NSUP, SUP * P], I32)
    edst = dram("edst", [NSUP + 2, SUP * P], I32)
    xmid = dram("xmid", [NP, D])
    tab1 = dram("tab1", [NP, D + E0])
    sid = dram("sid", [E0, CAP0], I32)
    tab2 = dram("tab2", [NP, D])
    tab3 = dram("tab3", [NP, D])
    xsh = dram("xsh", [NP, D])
    ys = dram("ys", [NI1 * P, D])

    with ExitStack() as top:
        sb = lambda name, shape, dt=F32: top.enter_context(nc.sbuf_tensor(name, shape, dt))
        K = Shared()
        K.ident = sb("ident", [P, P])
        K.iota = sb("iota", [P, P])
        K.ones = sb("ones", [P, P])
        K.part = sb("part", [P, 1])
        K.src = sb("src_of_item", [P, NIT * SUP], I32)
        K.rel = sb("rel_of_item", [P, NIT * SUP])
        K.blk = sb("blk_of_item", [1, NIT], I32)
        K.junk = sb("junk", [P, D])
        K.xsup = sb("xsup", [1, NX], I32)
        K.rdeg = sb("rdeg", [P, NT, 1])
        K.score = sb("score", [P, NT, 2 * H0])
        with nc.sbuf_tensor("ex", [P, NIT * SUP, EXW], F32) as ex:
            with nc.sbuf_tensor("ws", [P, KT, D + 2 * H0], F32) as w, nc.sbuf_tensor("wb", [P, D], F32) as wb, \
                    nc.sbuf_tensor("xnT", [P, NT, D], F32) as xnT:
                phase_first(nc, K, a, tabs, esrc, edst, w, wb, xnT)
                phase_scores(nc, K, tab0, tabs, edst, w, wb, xnT, ex)
            with nc.sbuf_tensor("acc", [P, NT, D + EXW], F32) as acc:
                phase_aggregate(nc, K, "g0", tab0, ex, acc)
                with nc.sbuf_tensor("logits0", [P, NT, E0], F32) as lg:
                    phase_attend(nc, K, a, acc, xmid, tab1, lg)
                    phase_route0(nc, K, lg, tab1, sid)
        phase_experts0(nc, K, a, tab1, sid, xmid)
        if stop == 2:
            return phase_copy(nc, K, xmid, out)
        phase_norm2(nc, K, xmid, tab2)
        K.mv = sb("ln_mv3", [P, NT, 2])
        with nc.sbuf_tensor("acc1", [P, NT, D], F32) as acc, nc.sbuf_tensor("own", [P, NT, D], F32) as own:
            phase_aggregate(nc, K, "g1", tab2, None, acc, a, own)
            phase_sage(nc, K, a, acc, own, xmid, K.mv, ys)
        if stop == 3:
            return phase_copy(nc, K, xmid, out)
        K.slot = sb("slot_of_item", [P, NI1], I32)
        K.ovf = sb("ovf", [1, P], I32)
        K.nov = sb("nov", [1, 1], I32)
        K.pair = sb("pair_slot", [P, NT, TOP], I32)
        K.gate = sb("pair_gate", [P, NT, TOP])
        with nc.sbuf_tensor("scores1", [P, NT, E1], F32) as sc:
            phase_shared(nc, K, a, xmid, tab3, xsh, sc)
            phase_route1(nc, K, sc)
        phase_experts1(nc, K, a, tab3, ys)
        phase_combine(nc, K, xsh, ys, out)


XB = 4


def phase_first(nc, K, a, tabs, esrc, edst, w, wb, xnT):
    with Phase(nc, "fi") as p:
        aw = p.sb("aw", [P, H0, 2 * HD])
        prod = p.sb("prod", [P, 2, 2, H0, HD])
        ab = p.sb("ab", [P, H0])
        cst = p.sb("cst", [P, 2 * H0])
        ctmp = p.sb("ctmp", [P, 2 * H0])
        xt = p.sb("xt", [P, XB, D])
        xn = p.sb("xn", [P, 2, D])
        xnTu = p.sb("xnTu", [P, 2, D])
        ln = Norm(p, nc)
        pad = p.sb("pad", [1, 3, SUP * P], I32)
        rowi = p.sb("rowi", [ER, 2, EC * P], I32)
        rowf = p.sb("rowf", [ER, 2, EC * P])
        xst = p.sb("xst", [NX, 2])
        xsti = p.sb("xsti", [NX, 4], I32)
        xi = p.sb("xi", [NX, 2, SUP * P], I32)
        xf = p.sb("xf", [NX, 2, SUP * P])
        xlow = p.sb("xlow", [NX, 1])
        xbad = p.sb("xbad", [NX, 1])
        xrel = p.sb("xrel", [NX, SUP * P])
        b0i = p.sb("b0i", [1, 2, NSUP], I32)
        b0f = p.sb("b0f", [1, 2, NSUP])
        dstT = p.sb("dstT", [P, NET])
        psT = [p.ps(f"psT{u}", [P, D]) for u in range(2)]
        psS = [p.ps(f"psS{u}", [P, D]) for u in range(2)]
        psA = [p.ps(f"psA{u}", [P, D]) for u in range(2)]
        psE = p.ps("psE", [P, D])
        psX = p.ps("psX", [P, D])
        psR, psY, psL = psX[0:1, 0:NX], psE[:, 32:32 + NSUP], psE[0:NX, 256:256 + NSUP]
        consts = p.sem("consts")
        idz = p.sem("idz")
        wl = p.sem("wl")
        padr = p.sem("padr")
        edge = p.sem("edge")
        wready = p.sem("wready")
        xl = [p.sem(f"xl{q}") for q in range(XB)]
        normed = p.sem("normed")
        turned = p.sem("turned")
        turned_sb = p.sem("turned_sb")
        scored = p.sem("scored")
        kept = p.sem("kept")
        stored = p.sem("stored")
        saved = p.sem("saved")
        wch = p.sem("wch")
        rows_in = p.sem("rows_in")
        conv = p.sem("conv")
        lowr = p.sem("lowr")
        tdone = p.sem("tdone")
        xidx = p.sem("xidx")
        got = p.gather_sem("got")
        ech = p.sem("ech")
        flat = lambda t: t.rearrange("s e -> (s e)")
        rows = lambda t: t.rearrange("(r e) -> r e", e=EC * P)
        b = p.block(K.counted)

        @b.gpsimd
        def _(g):
            nc.gpsimd.memset(pad[:, 0, :], 0).then_inc(padr, 1)
            nc.gpsimd.memset(pad[:, 1, :], FAR).then_inc(padr, 1)
            nc.gpsimd.memset(pad[:, 2, :], 2 * FAR).then_inc(padr, 1)
            nc.gpsimd.memset(K.ident[:], 0.0).then_inc(idz, 1)
            nc.gpsimd.iota(K.iota[:], [[1, P]], base=0, channel_multiplier=0,
                           allow_small_or_imprecise_dtypes=True).then_inc(consts, 1)
            nc.gpsimd.iota(K.part[:], [[0, 1]], base=0, channel_multiplier=1,
                           allow_small_or_imprecise_dtypes=True).then_inc(consts, 1)
            g.wait_ge(idz, 1)
            nc.gpsimd.affine_select(out=K.ident[:], in_=K.ident[:], compare_op=ALU.not_equal, fill=1.0,
                                    base=0, pattern=[[-1, P]], channel_multiplier=1).then_inc(consts, 1)
            nc.gpsimd.iota(xlow[:], [[0, 1]], base=P, channel_multiplier=P,
                           allow_small_or_imprecise_dtypes=True).then_inc(lowr, 1)
            g.wait_ge(xidx, 1)
            g.indirect_dma_start(xi[:, 0, :], None, esrc, bass.IndirectOffsetOnAxis(xsti[:, 2:3], 0)).then_inc(got, 16)
            g.indirect_dma_start(xi[:, 1, :], None, edst, bass.IndirectOffsetOnAxis(xsti[:, 3:4], 0)).then_inc(got, 16)
            g.wait_ge(got, 32)

            def save(n, k, u):
                g.wait_ge(turned_sb, n + 1)
                nc.gpsimd.tensor_copy(xnT[:, ds(n, 1), :].rearrange("p o d -> p (o d)"), xnTu[:, u, :]).then_inc(saved, 1)
            pairs(g, NT, save)
            g.wait_ge(saved, NT)

        @b.sync
        def _(s):
            s.dma_start(aw[:].rearrange("p h d -> p (h d)"),
                        a["L0_gnn_a_w"].rearrange("h d -> (h d)").partition_broadcast(P)).then_inc(wl, 16)
            s.dma_start(wb[:], a["L0_gnn_Wb"].rearrange("h d -> (h d)").partition_broadcast(P)).then_inc(wl, 16)
            s.dma_start(ab[:], a["L0_gnn_a_b"].partition_broadcast(P)).then_inc(wl, 16)
            for kt in range(KT):
                s.dma_start(w[:, kt, 0:D].rearrange("p (h d) -> p h d", h=H0),
                            a["L0_gnn_Ws"][:, kt * P:(kt + 1) * P, :].rearrange("h p d -> p h d")).then_inc(wl, 16)

            def load(n, k, q):
                if within(n, NT):
                    wait(s, normed, n - XB + 1)
                    s.dma_start(xt[0:rows_of(n), q, :], tile_rows(a["x"], n)).then_inc(xl[q], 16)
            skewed(s, NT, 0, load, XB)
            s.wait_ge(kept, NT)
            s.dma_start(tabs.rearrange("(t p) h -> p t h", p=P), K.score[:, :, 0:H0]).then_inc(stored, 16)
            s.wait_ge(stored, 16)

        @b.scalar
        def _(c):
            c.dma_start(flat(esrc)[0:E], a["src"]).then_inc(edge, 16)
            c.dma_start(flat(edst)[SUP * P:SUP * P + E], a["dst"]).then_inc(edge, 16)
            c.wait_ge(padr, 3)
            c.dma_start(flat(esrc)[E:ESLOT].unsqueeze(0), pad[:, 0, 0:ESLOT - E]).then_inc(edge, 16)
            c.dma_start(flat(edst)[0:SUP * P].unsqueeze(0), pad[:, 2, :]).then_inc(edge, 16)
            c.dma_start(flat(edst)[SUP * P + E:SUP * P + ESLOT].unsqueeze(0),
                        pad[:, 1, 0:ESLOT - E]).then_inc(edge, 16)
            c.dma_start(flat(edst)[SUP * P + ESLOT:].unsqueeze(0), pad[:, 2, :]).then_inc(edge, 16)
            c.wait_ge(edge, 6 * 16)
            c.dma_start(rowi[:, 0], rows(flat(esrc))).then_inc(rows_in, 16)
            c.dma_start(rowi[:, 1], rows(flat(edst)[SUP * P:SUP * P + ESLOT])).then_inc(rows_in, 16)
            with nc.allow_non_contiguous_dma(reason="one word per super tile"):
                c.dma_start(b0i[:, 0], edst[1:1 + NSUP, 0:1].rearrange("s o -> o s")).then_inc(rows_in, 16)
                c.dma_start(b0i[:, 1], edst[1:1 + NSUP, SUP * P - 1:SUP * P].rearrange("s o -> o s")).then_inc(rows_in, 16)

            def step(n, k, q):
                u = q % 2
                if within(n, NT):
                    ln.scalar(c, n, u)
                m, km, qm = back(n, k, q, 1, XB)
                um = qm % 2
                if within(m, NT):
                    c.wait_ge(ln.ready, m + 1)
                    wait(c, turned, m - 1)
                    nc.scalar.activation(xn[:, um, :], xt[:, qm, :], ACT.Identity, bias=ln.offset(um),
                                         scale=ln.scale(um)).then_inc(normed, 1)
                m = n - 2
                if within(m, NT):
                    c.wait_ge(turned, m + 1)
                    wait(c, scored, m - 1)
                    wait(c, saved, m - 1)
                    nc.scalar.activation(xnTu[:, u, :], psT[u][:], ACT.Copy).then_inc(turned_sb, 1)
            skewed(c, NT, 2, step, XB)

        @b.tensor
        def _(t):
            tens = nc.tensor
            t.wait_ge(consts, 4)
            t.wait_ge(conv, 2)
            for c in range(EC):
                for j in range(2):
                    ins = tens.transpose(psA[j][:, c * P:c * P + ER], rowf[:, j, c * P:(c + 1) * P], K.ident[0:ER, 0:ER])
            ins.then_inc(tdone, 1)
            t.wait_ge(conv, 3)
            tens.matmul(psY, K.ones[0:1, :], b0f[:, 0], start=True, stop=True)
            tens.matmul(psL, K.ones[0:1, 0:NX], b0f[:, 1], start=True, stop=True).then_inc(tdone, 1)
            t.wait_ge(conv, 4)
            tens.matmul(psR, xst[:, 0:1], K.ident[0:NX, 0:NX], start=True, stop=True).then_inc(tdone, 1)
            t.wait_ge(wready, 1)

            def step(n, k, u):
                if within(n, NT):
                    t.wait_ge(normed, n + 1)
                    wait(t, turned_sb, n - 1)
                    for kt in range(KT):
                        ins = tens.transpose(psT[u][:, kt * P:(kt + 1) * P], xn[:, u, kt * P:(kt + 1) * P], K.ident[:])
                    ins.then_inc(turned, 1)
                m, um = n - 1, 1 - u
                if within(m, NT):
                    t.wait_ge(turned_sb, m + 1)
                    wait(t, kept, m - 1)
                    for kt in range(KT):
                        ins = tens.matmul(psS[um][:, 0:2 * H0], xnTu[:, um, kt * P:(kt + 1) * P],
                                          w[:, kt, D:D + 2 * H0], start=(kt == 0), stop=(kt == KT - 1))
                    ins.then_inc(scored, 1)
            skewed(t, NT, 1, step)
            t.wait_ge(conv, 5)
            for h in range(SUP):
                tens.transpose(psX[:, h * NX:(h + 1) * NX], xf[:, 0, h * P:(h + 1) * P], K.ident[0:NX, 0:NX])
                ins = tens.transpose(psX[:, 128 + h * NX:128 + (h + 1) * NX], xrel[:, h * P:(h + 1) * P],
                                     K.ident[0:NX, 0:NX])
            ins.then_inc(tdone, 1)

        @b.vector
        def _(v):
            vv = nc.vector
            nc.vector.memset(K.ones[:], 1.0).then_inc(consts, 1)
            ch = Chain(v, ech)
            wc = Chain(v, wch)
            v.wait_ge(wl, 16 * (KT + 3))
            halves = aw[:].rearrange("p h (t d) -> p t h d", t=2)[:, ::-1]
            for kt in range(KT + 1):
                src = w[:, kt, 0:D] if kt < KT else wb[:]
                dst = w[:, kt, D:D + 2 * H0] if kt < KT else ctmp[:]
                wc(vv.tensor_tensor(prod[:, kt % 2], src.rearrange("p (h d) -> p h d", h=H0).unsqueeze(1)
                                    .to_broadcast([P, 2, H0, HD]), halves, ALU.mult))
                wc(vv.tensor_reduce(dst, prod[:, kt % 2].rearrange("p t h d -> p (t h) d"), AX.X, ALU.add))
            wc(vv.memset(cst[:, 0:H0], 0.0))
            wc(vv.tensor_tensor(ctmp[:, 0:H0], ctmp[:, 0:H0], ctmp[:, H0:2 * H0], ALU.add))
            vv.tensor_tensor(cst[:, H0:2 * H0], ctmp[:, 0:H0], ab[:], ALU.add).then_inc(wready, 1)
            v.wait_ge(wready, 1)
            v.wait_ge(rows_in, 64)
            vv.tensor_copy(rowf[:, 0], rowi[:, 0]).then_inc(conv, 1)
            vv.tensor_copy(rowf[:, 1], rowi[:, 1]).then_inc(conv, 1)
            ch(vv.tensor_single_scalar(K.blk[0:1, 0:NSUP], b0i[:, 0], 7, ALU.arith_shift_right))
            vv.tensor_copy(b0f[:, 1], b0i[:, 1])
            ch(vv.tensor_copy(b0f[:, 0], K.blk[0:1, 0:NSUP]))
            vv.tensor_scalar(b0f[:, 0], b0f[:, 0], float(P), None, ALU.mult).then_inc(conv, 1)
            for x in range(NX):
                vv.memset(K.blk[0:1, NSUP + x:NSUP + x + 1], x + 1)
            v.wait_ge(tdone, 1)
            by_row = lambda t: t.rearrange("p (r c) -> p c r", c=EC)
            from_ps = lambda t: t[:].rearrange("p (c e) -> p c e", c=EC)[:, :, 0:ER]
            vv.tensor_copy(by_row(K.src[:, 0:NET]), from_ps(psA[0]))
            ch(vv.tensor_copy(by_row(dstT[:]), from_ps(psA[1])))
            v.wait_ge(tdone, 2)
            v.wait_ge(lowr, 1)
            ch(vv.tensor_scalar(K.junk[0:NX, 0:NSUP], psL, xlow[:], 0.0, ALU.is_lt, ALU.add, accum_out=xst[:, 0:1]))
            vv.tensor_scalar(xst[:, 1:2], xst[:, 0:1], 1.0, None, ALU.add).then_inc(conv, 1)
            v.wait_ge(conv, 4)
            vv.tensor_copy(xsti[:, 2:4], xst[:]).then_inc(xidx, 1)
            vv.tensor_tensor(K.rel[:, 0:NET].rearrange("p (s h) -> p s h", h=SUP),
                             dstT[:].rearrange("p (s h) -> p s h", h=SUP),
                             psY.unsqueeze(2).to_broadcast([P, NSUP, SUP]), ALU.subtract)
            v.wait_ge(tdone, 3)
            vv.tensor_copy(K.xsup[:], psR)

            def step(n, k, q):
                u = q % 2
                if within(n, NT):
                    v.wait_ge(xl[q], k * 16 + 16)
                    ln.stats(v, n, u, xt[:, q, :])
                m = n - 1
                if within(m, NT):
                    ln.finish(v, m, 1 - u, normed)
                m, um = n - 3, 1 - u
                if within(m, NT):
                    v.wait_ge(scored, m + 1)
                    vv.tensor_tensor(K.score[:, ds(m, 1), :].rearrange("p o h -> p (o h)"),
                                     psS[um][:, 0:2 * H0], cst[:], ALU.add).then_inc(kept, 1)
            skewed(v, NT, 3, step, XB)
            v.wait_ge(got, 32)
            ch(vv.tensor_copy(xf[:], xi[:]))
            ch(vv.tensor_scalar(xbad[:], xf[:, 1, 0:1], xlow[:], float(FAR), ALU.is_ge, ALU.mult))
            ch(vv.tensor_tensor(xbad[:], xbad[:], xlow[:], ALU.subtract))
            vv.tensor_scalar(xrel[:], xf[:, 1, :], xbad[:], None, ALU.add).then_inc(conv, 1)
            v.wait_ge(tdone, 4)
            for h in range(SUP):
                vv.tensor_copy(K.src[:, NET + h::SUP], psX[:, h * NX:(h + 1) * NX])
                vv.tensor_copy(K.rel[:, NET + h::SUP], psX[:, 128 + h * NX:128 + (h + 1) * NX])


def phase_scores(nc, K, tab0, tabs, edst, w, wb, xnT, ex):
    LW = EC * P
    with Phase(nc, "sc") as p:
        S = p.sb("S", [P, NET, H0])
        T = p.sb("T", [P, NIT * SUP, H0])
        row = p.sb("row", [P, 2, D])
        xu = p.sb("xu", [P, 2, D])
        oh = p.sb("oh", [P, 2, SUP, P])
        ohT = p.sb("ohT", [P, 2, SUP, P])
        FR = p.sb("FR", [ER, H0, LW])
        BR = p.sb("BR", [ER, H0, LW])
        di = p.sb("di", [ER, 3, LW], I32)
        dn = p.sb("dn", [ER, 3, LW])
        pen = p.sb("pen", [ER, 2, LW])
        cum = p.sb("cum", [ER, 2, LW])
        pent = p.sb("pent", [ER, 2, H0])
        pq = p.sb("pq", [H0, 2, ER])
        seq = p.sb("seq", [H0, 2, ER])
        carry = p.sb("carry", [H0, 2, ER + 2])
        cin = p.sb("cin", [ER, 2, H0])
        psO = [p.ps(f"psO{u}", [P, D]) for u in range(2)]
        psT = [p.ps(f"psT{u}", [P, D]) for u in range(2)]
        psS = [p.ps(f"psS{u}", [P, D]) for u in range(4)]
        ld = p.sem("ld")
        got = [p.gather_sem(f"got{c}") for c in range(EC)]
        fetched = p.sem("fetched")
        prj = p.sem("prj")
        kept = p.sem("kept")
        st = [p.sem(f"st{u}") for u in range(2)]
        ohd = p.sem("ohd")
        oht = p.sem("oht")
        ohc = p.sem("ohc")
        tdone = p.sem("tdone")
        tcop = p.sem("tcop")
        xch = p.sem("xch")
        vch = p.sem("vch")
        zready = p.sem("zready")
        zt = p.sem("zt")
        fsc = p.sem("fsc")
        bsc = p.sem("bsc")
        penr = p.sem("penr")
        cart = p.sem("cart")
        cars = p.sem("cars")
        m1 = p.sem("m1"); m2 = p.sem("m2")
        mt = p.sem("mt")
        dif = p.sem("dif")
        exd = p.sem("exd")
        flat = lambda t: t.rearrange("s e -> (s e)")
        b = p.block(K.counted)

        @b.sync
        def _(s):
            for j in range(3):
                s.dma_start(di[:, j], flat(edst)[SUP * P - 1 + j:SUP * P - 1 + j + ESLOT]
                            .rearrange("(r e) -> r e", e=LW)).then_inc(ld, 16)

            def store(n, k, u):
                s.wait_ge(kept, n + 1)
                s.dma_start(tab0[ds(n * P, P), :], row[:, u, :]).then_inc(st[u], 16)
            pairs(s, NT, store)
            for u in range(2):
                s.wait_ge(st[u], 16 * ((NT + 1 - u) // 2))

        @b.gpsimd
        def _(g):
            for j in range(NET):
                g.indirect_dma_start(S[:, j, :], None, tabs,
                                     bass.IndirectOffsetOnAxis(K.src[:, j:j + 1], 0)).then_inc(got[j // ER], 16)
            for c in range(EC):
                g.wait_ge(got[c], 16 * ER)

        @b.tensor
        def _(t):
            tens = nc.tensor

            def tscore(n, k, u):
                if within(n, NIT):
                    t.wait_ge(ohd, n + 1)
                    wait(t, ohc, n - 1)
                    for h in range(SUP):
                        ins = tens.transpose(psO[u][:, h * P:(h + 1) * P], oh[:, u, h, :], K.ident[:])
                    ins.then_inc(oht, 1)
                m, um = n - 1, 1 - u
                if within(m, NIT):
                    blk = t.value_load(K.blk[0:1, ds(m, 1)], min_val=0, max_val=NT - 1)
                    t.wait_ge(ohc, m + 1)
                    wait(t, tcop, m - 1)
                    for h in range(SUP):
                        ins = tens.matmul(psT[um][:, h * H0:(h + 1) * H0], ohT[:, um, h, :],
                                          K.score[:, ds(blk, 1), H0:2 * H0].rearrange("p o h -> p (o h)"),
                                          start=True, stop=True)
                    ins.then_inc(tdone, 1)
            skewed(t, NIT, 1, tscore)
            t.wait_ge(penr, 1)
            t.wait_ge(tcop, NIT)
            for d in range(2):
                ins = tens.transpose(psT[0][0:H0, d * P:d * P + ER], pent[:, d, :], K.ident[0:ER, 0:ER])
            ins.then_inc(cart, 1)

            def project(n, k, u):
                t.wait_ge(fetched, n + 1)
                wait(t, kept, n - 1)
                for kt in range(KT):
                    ins = tens.matmul(psS[u][:], xu[:, u, kt * P:(kt + 1) * P],
                                      w[:, kt, 0:D], start=(kt == 0), stop=(kt == KT - 1))
                ins.then_inc(prj, 1)
            pairs(t, NT, project)
            t.wait_ge(kept, NT)

            t.wait_ge(zready, 1)
            for h in range(H0):
                wait(t, fsc, h - 3)
                zh = S[:, :, h].rearrange("p (r c) -> p c r", c=EC)
                for c in range(EC):
                    ins = tens.transpose(psS[h % 4][0:ER, c * P:(c + 1) * P], zh[:, c, :], K.ident[:])
                ins.then_inc(zt, 1)
            t.wait_ge(bsc, H0)
            for d, src in ((0, FR[:, :, LW - 1]), (1, BR[:, :, 0])):
                ins = tens.transpose(psO[0][0:H0, d * P:d * P + ER], src, K.ident[0:ER, 0:ER])
            ins.then_inc(cart, 1)
            t.wait_ge(cars, 1)
            for d in range(2):
                ins = tens.transpose(psO[1][0:ER, d * H0:(d + 1) * H0], carry[:, d, 2 * d:2 * d + ER], K.ident[0:H0, 0:H0])
            ins.then_inc(cart, 1)
            for h in range(H0):
                t.wait_ge(m2, h + 1)
                wait(t, dif, h - 3)
                for c in range(EC):
                    ins = tens.transpose(psS[h % 4][:, c * P:c * P + ER], BR[:, h, c * P:(c + 1) * P],
                                         K.ident[0:ER, 0:ER])
                ins.then_inc(mt, 1)

        @b.scalar
        def _(c_):
            sc_ = nc.scalar

            def copy(n, k, u):
                c_.wait_ge(oht, n + 1)
                wait(c_, tdone, n - 1)
                sc_.activation(ohT[:, u], psO[u][:, 0:SUP * P].rearrange("p (h e) -> p h e", h=SUP),
                               ACT.Copy).then_inc(ohc, 1)
            pairs(c_, NIT, copy)

            def fetch(n, k, u):
                wait(c_, prj, n - 1)
                sc_.activation(xu[:, u, :], xnT[:, ds(n, 1), :].rearrange("p o d -> p (o d)"),
                               ACT.Copy).then_inc(fetched, 1)
            pairs(c_, NT, fetch)
            for h in range(H0):
                c_.wait_ge(dif, h + 1)
                sc_.activation(ex[:, 0:NET, h], S[:, :, h], ACT.Exp).then_inc(exd, 1)
            c_.wait_ge(exd, H0)

        @b.vector
        def _(v):
            vv = nc.vector
            ch = Chain(v, vch)
            rev = lambda t, d: t if d == 0 else t[:, ::-1]

            v.wait_ge(ld, 48)
            ch(vv.tensor_copy(dn[:], di[:]))
            for d in range(2):
                ins = vv.tensor_tensor(pen[:, d], dn[:, 1], dn[:, 2 * d], ALU.not_equal)
            ch(ins)
            ch(vv.tensor_scalar(pen[:], pen[:], -BIG, None, ALU.mult))
            for d in range(2):
                vv.tensor_tensor_scan(rev(cum[:, d, :], d), rev(pen[:, d, :], d), rev(pen[:, d, :], d), 0.0,
                                      ALU.add, ALU.min)
                ins = vv.tensor_reduce(cin[:, d, 0:1], pen[:, d], AX.X, ALU.min)
            ch(ins)
            vv.memset(carry[:], -BIG)
            vv.memset(ex[:, :, H0:EXW], 1.0)
            vv.tensor_copy(pent[:], cin[:, :, 0:1].to_broadcast([ER, 2, H0])).then_inc(penr, 1)

            def tscore(n, k, u):
                if within(n, NIT):
                    wait(v, oht, n - 1)
                    for h in range(SUP):
                        ins = vv.tensor_scalar(oh[:, u, h, :], K.iota[:], K.rel[:, ds(n * SUP + h, 1)], None, ALU.is_equal)
                    ins.then_inc(ohd, 1)
                m, um = n - 3, 1 - u
                if within(m, NIT):
                    v.wait_ge(tdone, m + 1)
                    vv.tensor_scalar(T[:, ds(m * SUP, SUP), :], psT[um][:, 0:SUP * H0].rearrange("p (h e) -> p h e", h=SUP),
                                     0.0, None, ALU.add).then_inc(tcop, 1)
            skewed(v, NIT, 3, tscore)
            v.wait_ge(tcop, NIT)

            def keep(n, k, u):
                v.wait_ge(prj, n + 1)
                wait(v, st[u], k * 16)
                vv.tensor_tensor(row[:, u, :], psS[u][:], wb[:], ALU.add).then_inc(kept, 1)
                if last(n):
                    return
                r = v.value_load(K.xsup[0:1, ds(n, 1)], min_val=0, max_val=NSUP - 1)
                wait(v, xch, n)
                t = T[:, ds(r * SUP, SUP), :]
                vv.tensor_tensor(t, t, T[:, ds(n * SUP + NET, SUP), :], ALU.add).then_inc(xch, 1)
            assert NX == NT - 1
            pairs(v, NT, keep)
            v.wait_ge(xch, NX)
            for c in range(EC):
                v.wait_ge(got[c], 16 * ER)
                s_ = S[:, c * ER:(c + 1) * ER, :]
                ch(vv.tensor_tensor(s_, s_, T[:, c * ER:(c + 1) * ER, :], ALU.add))
                ins = vv.scalar_tensor_tensor(s_, s_, 0.2, s_, ALU.mult, ALU.max)
                if c < EC - 1:
                    ch(ins)
            ins.then_inc(zready, 1)
            v.wait_ge(cart, 1)
            vv.tensor_copy(pq[:], psT[0][0:H0, 0:2 * P].rearrange("p (d e) -> p d e", d=2)[:, :, 0:ER])
            for h in range(H0):
                v.wait_ge(zt, h + 1)
                vv.tensor_tensor_scan(FR[:, h, :], pen[:, 0, :], psS[h % 4][0:ER, :], -BIG, ALU.add, ALU.max).then_inc(fsc, 1)
                v.wait_ge(fsc, h + 1)
                vv.tensor_tensor_scan(BR[:, h, ::-1], pen[:, 1, ::-1], FR[:, h, ::-1], -BIG, ALU.add, ALU.max).then_inc(bsc, 1)
            v.wait_ge(cart, 2)
            ch(vv.tensor_copy(seq[:], psO[0][0:H0, 0:2 * P].rearrange("p (d e) -> p d e", d=2)[:, :, 0:ER]))
            for d in range(2):
                ins = vv.tensor_tensor_scan(rev(carry[:, d, 1:1 + ER], d), rev(pq[:, d, :], d), rev(seq[:, d, :], d),
                                            -BIG, ALU.add, ALU.max)
            ins.then_inc(cars, 1)
            v.wait_ge(cart, 3)
            ch(vv.tensor_copy(cin[:], psO[1][0:ER, 0:2 * H0].rearrange("p (d h) -> p d h", d=2)))
            v.wait_ge(bsc, H0)
            for h in range(H0):
                vv.scalar_tensor_tensor(BR[:, h, :], cum[:, 0, :], cin[:, 0, h:h + 1], BR[:, h, :],
                                        ALU.add, ALU.max).then_inc(m1, 1)
            for h in range(H0):
                v.wait_ge(m1, h + 1)
                vv.scalar_tensor_tensor(BR[:, h, :], cum[:, 1, :], cin[:, 1, h:h + 1], BR[:, h, :],
                                        ALU.add, ALU.max).then_inc(m2, 1)
            for h in range(H0):
                v.wait_ge(mt, h + 1)
                zh = S[:, :, h].rearrange("p (r c) -> p c r", c=EC)
                vv.tensor_tensor(zh, zh, psS[h % 4][:].rearrange("p (c e) -> p c e", c=EC)[:, :, 0:ER],
                                 ALU.subtract).then_inc(dif, 1)


GQ = 10
OB = 5
XR = 2
ON_ACT = 2


def phase_aggregate(nc, K, name, table, ex, acc, a=None, own=None):
    with Phase(nc, name) as p:
        nw = EXW if ex is not None else 0
        HV = H0 - ON_ACT
        G = p.sb("G", [P, GQ, SUP, D])
        oh = p.sb("oh", [P, OB, SUP, P])
        psA = [p.ps(f"psA{u}", [P, D]) for u in range(2)]
        if nw:
            psB = [p.ps(f"psB{u}", [P, D]) for u in range(2)]
        got = [p.gather_sem(f"got{q}") for q in range(GQ)]
        ready = p.sem("ready")
        scaled = p.sem("scaled")
        repeated = p.sem("repeated")
        summed = p.sem("summed")
        added = p.sem("added")
        zero = p.sem("zero")
        if own is not None:
            wr = p.sb("wr", [P, KT, D])
            bb = p.sb("bb", [P, D])
            xr = p.sb("xr", [P, 2, D])
            xrT = p.sb("xrT", [P, 2, D])
            psU = [p.ps(f"psU{u}", [P, D]) for u in range(2)]
            psP = [p.ps(f"psP{u}", [P, D]) for u in range(2)]
            wl = p.sem("wl")
            xl = [p.sem(f"xl{u}") for u in range(2)]
            turned = p.sem("turned")
            copied = p.sem("copied")
            prod = p.sem("prod")
            kept = p.sem("kept")
        OWN_TURNS = 1 + (NT - 1) // 2
        b = p.block(K.counted)

        def owns(k):
            if isinstance(k, int):
                return [(0, NT - 1, 0, 0)] if k == 0 else []
            return [(k * 2 - 1, k * 2 - 2, k - 1, 1), (k * 2, k * 2 - 1, k, 0)]

        def quads(eng, body, cuts=(), between=None):
            for q in range(GQ):
                body(q, 0, q)
                if between:
                    between(0, q)
            start = 1
            for turn, act in tuple(cuts) + ((NIT // GQ - 1, None),):
                with eng.Fori(start, turn) as k:
                    for q in range(GQ):
                        body(k * GQ + q, k, q)
                        if between and start == 1:
                            between(k, q)
                if act:
                    act()
                start = turn
            for q in range(GQ):
                body(NIT - GQ + q, NIT // GQ - 1, q)
        assert NIT % GQ == 0 and GQ % 2 == 0 and GQ % OB == 0 and NX // XR + 2 < NSUP // GQ and NX % XR == 0

        @b.gpsimd
        def _(g):
            for n in range(NIT):
                q = n % GQ
                wait(g, summed, n - GQ + 1)
                for h in range(SUP):
                    j = n * SUP + h
                    g.indirect_dma_start(G[:, q, h, :], None, table,
                                         bass.IndirectOffsetOnAxis(K.src[:, j:j + 1], 0)).then_inc(got[q], 16)

        if own is not None:
            @b.sync
            def _(s):
                s.dma_start(wr[:], a["L1_gnn_W_r"].rearrange("(k p) d -> p k d", p=P)).then_inc(wl, 16)
                s.dma_start(bb[:], a["L1_gnn_b"].partition_broadcast(P)).then_inc(wl, 16)

                def turn(k):
                    for i, tile, half, u in owns(k):
                        wait(s, turned, i - 1)
                        s.dma_start(xr[:, u, :], table[ds(tile * P, P), :]).then_inc(xl[u], 16)
                turn(0)
                with s.Fori(1, OWN_TURNS) as k:
                    turn(k)

            @b.scalar
            def _(c):
                def turn(k):
                    for i, tile, half, u in owns(k):
                        c.wait_ge(turned, i + 1)
                        wait(c, prod, i - 1)
                        nc.scalar.activation(xrT[:, u, :], psU[u][:], ACT.Copy).then_inc(copied, 1)
                turn(0)
                with c.Fori(1, OWN_TURNS) as k:
                    turn(k)

        if ex is not None:
            @b.scalar
            def _(c):
                def scale(n, k, q):
                    c.wait_ge(got[q], k * 32 + 32)
                    for h in range(SUP):
                        for hd in range(HV, H0):
                            r = G[:, q, h, hd * HD:(hd + 1) * HD]
                            w = ex[:, ds(n * SUP + h, 1), hd:hd + 1].rearrange("p o h -> p (o h)")
                            ins = nc.scalar.activation(r, r, ACT.Copy, scale=w)
                    ins.then_inc(scaled, 1)

                def turn(k):
                    for q in range(GQ):
                        scale(k * GQ + q, k, q)
                turn(0)
                with c.Fori(1, NX // XR + 1) as k:
                    turn(k)
                    for x in range(XR):
                        r = c.value_load(K.xsup[0:1, ds(k * XR + (x - XR), 1)], min_val=0, max_val=NSUP - 1)
                        nc.scalar.activation(ex[:, ds(k * (XR * SUP) + (NET + (x - XR) * SUP), SUP), :],
                                             ex[:, ds(r * SUP, SUP), :], ACT.Copy).then_inc(repeated, 1)
                with c.Fori(NX // XR + 1, NIT // GQ) as k:
                    turn(k)

        @b.tensor
        def _(t):
            def item(n, k, q):
                u = q % 2
                t.wait_ge(ready, n + 1)
                if ex is None:
                    t.wait_ge(got[q], k * 32 + 32)
                else:
                    t.wait_ge(scaled, n + 1)
                wait(t, added, n - 1)
                for h in range(SUP):
                    ins = nc.tensor.matmul(psA[u][:], oh[:, q % OB, h, :], G[:, q, h, 0:D], start=(h == 0), stop=(h == SUP - 1))
                for h in range(SUP if nw else 0):
                    w = ex[:, ds(n * SUP + h, 1), :]
                    ins = nc.tensor.matmul(psB[u][:, 0:nw], oh[:, q % OB, h, :], w, start=(h == 0), stop=(h == SUP - 1))
                ins.then_inc(summed, 1)

            def between(k, q):
                for i, tile, half, u in owns(k):
                    if q == (5, 1)[u]:
                        t.wait_ge(xl[u], half * 16 + 16)
                        wait(t, copied, i - 1)
                        for kt in range(KT):
                            ins = nc.tensor.transpose(psU[u][:, kt * P:(kt + 1) * P], xr[:, u, kt * P:(kt + 1) * P],
                                                      K.ident[:])
                        ins.then_inc(turned, 1)
                    if q == (7, 3)[u]:
                        t.wait_ge(copied, i + 1)
                        wait(t, kept, i - 1)
                        for kt in range(KT):
                            ins = nc.tensor.matmul(psP[u][:], xrT[:, u, kt * P:(kt + 1) * P], wr[:, kt, :],
                                                   start=(kt == 0), stop=(kt == KT - 1))
                        ins.then_inc(prod, 1)
            if own is None:
                quads(t, item)
            else:
                t.wait_ge(wl, 32)
                quads(t, item, ((OWN_TURNS, None),), between)

        @b.vector
        def _(v):
            vv = nc.vector
            vv.memset(acc[:, :, 0:D + nw], 0.0).then_inc(zero, 1)
            v.wait_ge(zero, 1)

            def prep(n, k, q):
                wait(v, summed, n - OB + 1)
                for h in range(SUP):
                    ins = vv.tensor_scalar(oh[:, q % OB, h, :], K.iota[:], K.rel[:, ds(n * SUP + h, 1)], None, ALU.is_equal)
                if ex is not None:
                    v.wait_ge(got[q], k * 32 + 32)
                    for h in range(SUP):
                        rows = G[:, q, h, 0:HV * HD].rearrange("p (h d) -> p h d", h=HV)
                        w = ex[:, ds(n * SUP + h, 1), 0:HV].rearrange("p o h -> p (o h)").unsqueeze(2)
                        ins = vv.tensor_tensor(rows, rows, w.to_broadcast([P, HV, HD]), ALU.mult)
                ins.then_inc(ready, 1)

            def add(n, k, q):
                u = q % 2
                blk = v.value_load(K.blk[0:1, ds(n, 1)], min_val=0, max_val=NT - 1)
                v.wait_ge(summed, n + 1)
                wait(v, added, n)
                a1 = acc[:, ds(blk, 1), 0:D].rearrange("p o d -> p (o d)")
                ins = vv.tensor_tensor(a1, a1, psA[u][:], ALU.add)
                if nw:
                    a2 = acc[:, ds(blk, 1), D:D + nw].rearrange("p o d -> p (o d)")
                    ins = vv.tensor_tensor(a2, a2, psB[u][:, 0:nw], ALU.add)
                ins.then_inc(added, 1)

            def step(n, k, q):
                if not isinstance(n, int) or n < NIT - 2:
                    prep(n + 2, k + (q + 2) // GQ, (q + 2) % GQ)
                add(n, k, q)

            def between(k, q):
                for i, tile, half, u in owns(k):
                    if q == (9, 5)[u]:
                        v.wait_ge(prod, i + 1)
                        vv.tensor_tensor(own[:, ds(tile, 1), :].rearrange("p o d -> p (o d)"), psP[u][:], bb[:],
                                         ALU.add).then_inc(kept, 1)
            prep(0, 0, 0)
            prep(1, 0, 1)
            if own is not None:
                v.wait_ge(wl, 32)
                quads(v, step, ((OWN_TURNS, None),), between)
                v.wait_ge(added, NIT)
                v.wait_ge(kept, NT)
                return
            quads(v, step, () if ex is None else ((NX // XR + 2, lambda: v.wait_ge(repeated, NX)),))
            v.wait_ge(added, NIT)


def phase_copy(nc, K, src, out):
    with Phase(nc, "cp") as p:
        d = p.sem("d")
        b = p.block(K.counted)

        @b.sync
        def _(s):
            s.dma_start(out, src[0:N]).then_inc(d, 16)
            s.wait_ge(d, 16)


def rows_of(n):
    return TAIL if last(n) else P


def tile_rows(t, n):
    return t[n * P:N, :] if last(n) else t[ds(n * P, P), :]


def phase_attend(nc, K, a, acc, xmid, tab1, lg):
    with Phase(nc, "at") as p:
        wr = p.sb("wr", [P, KT, E0])
        xt = p.sb("xt", [P, XB, D])
        x1 = p.sb("x1", [P, XB, D])
        den = p.sb("den", [P, NT, H0])
        xn = p.sb("xn", [P, XB, D])
        xnT = p.sb("xnT", [P, 2, D])
        psT = [p.ps(f"psT{u}", [P, D]) for u in range(2)]
        psL = [p.ps(f"psL{u}", [P, D]) for u in range(2)]
        ln = Norm(p, nc)
        wl = p.sem("wl")
        mean = p.sem("mean")
        summed = p.sem("summed")
        normed = p.sem("normed")
        turned = p.sem("turned")
        copied = p.sem("copied")
        prod = p.sem("prod")
        read = p.sem("read")
        dch = p.sem("dch")
        xl = [p.sem(f"xl{q}") for q in range(XB)]
        sx = [p.sem(f"sx{q}") for q in range(XB)]
        sn = [p.sem(f"sn{q}") for q in range(XB)]
        b = p.block(K.counted)

        @b.sync
        def _(s):
            s.dma_start(wr[:], a["L0_ffn_Wr"].rearrange("(kt p) e -> p kt e", p=P)).then_inc(wl, 16)

            def step(n, k, q):
                if within(n, NT):
                    wait(s, summed, n - XB + 1)
                    s.dma_start(xt[0:rows_of(n), q, :], tile_rows(a["x"], n)).then_inc(xl[q], 16)
                m, km, qm = back(n, k, q, 3, XB)
                if within(m, NT):
                    s.wait_ge(summed, m + 1)
                    s.dma_start(xmid[ds(m * P, P), :], x1[:, qm, :]).then_inc(sx[qm], 16)
            skewed(s, NT, 3, step, XB)
            for q in range(XB):
                s.wait_ge(sx[q], 16 * ((NT + XB - 1 - q) // XB))

        @b.scalar
        def _(c):
            def step(n, k, q):
                u = q % 2
                if within(n, NT):
                    ln.scalar(c, n, u)
                m, km, qm = back(n, k, q, 1, XB)
                um = qm % 2
                if within(m, NT):
                    c.wait_ge(ln.ready, m + 1)
                    wait(c, turned, m - XB + 1)
                    wait(c, sn[qm], km * 16)
                    nc.scalar.activation(xn[:, qm, :], x1[:, qm, :], ACT.Identity, bias=ln.offset(um),
                                         scale=ln.scale(um)).then_inc(normed, 1)
                m = n - 2
                if within(m, NT):
                    c.wait_ge(normed, m + 1)
                    c.dma_start(tab1[ds(m * P, P), 0:D], xn[:, (q - 2) % XB, :]).then_inc(sn[(q - 2) % XB], 16)
                    c.wait_ge(turned, m + 1)
                    wait(c, prod, m - 1)
                    nc.scalar.activation(xnT[:, u, :], psT[u][:], ACT.Copy).then_inc(copied, 1)
            skewed(c, NT, 2, step, XB)
            for q in range(XB):
                c.wait_ge(sn[q], 16 * ((NT + XB - 1 - q) // XB))

        @b.tensor
        def _(t):
            t.wait_ge(wl, 16)

            def step(n, k, q):
                u = q % 2
                if within(n, NT):
                    t.wait_ge(normed, n + 1)
                    wait(t, copied, n - 1)
                    for kt in range(KT):
                        ins = nc.tensor.transpose(psT[u][:, kt * P:(kt + 1) * P], xn[:, q, kt * P:(kt + 1) * P], K.ident[:])
                    ins.then_inc(turned, 1)
                m, um = n - 1, 1 - u
                if within(m, NT):
                    t.wait_ge(copied, m + 1)
                    wait(t, read, m - 1)
                    for kt in range(KT):
                        ins = nc.tensor.matmul(psL[um][:, 0:E0], xnT[:, um, kt * P:(kt + 1) * P], wr[:, kt, :],
                                               start=(kt == 0), stop=(kt == KT - 1))
                    ins.then_inc(prod, 1)
            skewed(t, NT, 1, step, XB)

        @b.vector
        def _(v):
            vv = nc.vector
            d = Chain(v, dch)
            d(vv.tensor_scalar(den[:], acc[:, :, D:D + H0], 1e-30, None, ALU.max))
            d(vv.reciprocal(den[:], den[:]))
            d(vv.tensor_scalar(K.rdeg[:], acc[:, :, D + H0:D + EXW], 1.0, None, ALU.max))
            d(vv.reciprocal(K.rdeg[:], K.rdeg[:]))

            def step(n, k, q):
                u = q % 2
                if within(n, NT):
                    o = x1[:, q, :]
                    wait(v, sx[q], k * 16)
                    wait(v, normed, n - XB + 1)
                    vv.tensor_tensor(o.rearrange("p (h d) -> p h d", h=H0),
                                     acc[:, ds(n, 1), 0:D].rearrange("p o (h d) -> p (o h) d", h=H0),
                                     den[:, ds(n, 1), :].rearrange("p o h -> p (o h)").unsqueeze(2)
                                     .to_broadcast([P, H0, HD]), ALU.mult).then_inc(mean, 1)
                    v.wait_ge(xl[q], k * 16 + 16)
                    v.wait_ge(mean, n + 1)
                    vv.tensor_tensor(o, o, xt[:, q, :], ALU.add).then_inc(summed, 1)
                    v.wait_ge(summed, n + 1)
                    ln.stats(v, n, u, o)
                m = n - 1
                if within(m, NT):
                    ln.finish(v, m, 1 - u, normed)
                m, um = n - 4, u
                if within(m, NT):
                    v.wait_ge(prod, m + 1)
                    vv.tensor_scalar(lg[:, ds(m, 1), :].rearrange("p o e -> p (o e)"), psL[um][:, 0:E0], 0.0, None,
                                     ALU.add).then_inc(read, 1)
            skewed(v, NT, 4, step, XB)
            v.wait_ge(read, NT)


def phase_route0(nc, K, lg, tab1, sid):
    BITS = 30
    W = NT * E0
    S = 16
    with Phase(nc, "r0") as p:
        pv = p.sb("pv", [P, 1])
        v_ = p.sb("v", [P, NT, E0])
        m8 = p.sb("m8", [P, E0])
        m1 = p.sb("m1", [E0, 1])
        dg = p.sb("dg", [E0, E0])
        rs = p.sb("rs", [P, E0])
        thr = p.sb("thr", [P, E0], I32)
        cand = p.sb("cand", [P, E0], I32)
        bit = p.sb("bit", [P, 1], I32)
        msk = p.sb("msk", [P, E0], I32)
        hit = p.sb("hit", [P, NT, E0])
        gt = p.sb("gt", [P, NT, E0])
        need = p.sb("need", [P, E0])
        tot = p.sb("tot", [P, NT, E0])
        inc = p.sb("inc", [P, NT, E0])
        rank = p.sb("rank", [P, NT, E0])
        zero = p.sb("zero", [P, NT])
        tri = p.sb("tri", [P, P])
        ri = p.sb("ri", [P, 3, NT, E0], I32)
        rf = p.sb("rf", [P, 2, NT, E0])
        tio = p.sb("tio", [P, NT])
        oa = p.sb("oa", [P, W, S], BF16)
        ob = p.sb("ob", [P, W, 2, S], BF16)
        obm = p.sb("obm", [P, W, S], BF16)
        idf = p.sb("idf", [S, E0, S])
        idi = p.sb("idi", [S, E0, S], I32)
        ps = [p.ps(f"ps{u}", [P, D]) for u in range(4)]
        psC = [p.ps(f"psC{u}", [P, D]) for u in range(2)]
        g1 = p.sem("g1"); vch = p.sem("vch"); tv = p.sem("tv"); vt = p.sem("vt"); ex = p.sem("ex"); xe = p.sem("xe")
        lc = p.sem("lc"); cs = p.sem("cs"); cd = p.sem("cd"); dd = p.sem("dd"); st = p.sem("st")
        b = p.block(K.counted)

        @b.gpsimd
        def _(g):
            nc.gpsimd.affine_select(out=tri[:], in_=K.ones[:], compare_op=ALU.is_gt, fill=0.0, base=0,
                                    pattern=[[1, P]], channel_multiplier=-1).then_inc(g1, 1)
            nc.gpsimd.iota(tio[:], [[1, NT]], base=0, channel_multiplier=0,
                           allow_small_or_imprecise_dtypes=True).then_inc(g1, 1)

        @b.sync
        def _(s):
            s.wait_ge(dd, 1)
            s.dma_start(tab1[:, D:D + E0].rearrange("(t p) e -> p t e", p=P), v_[:]).then_inc(st, 16)
            s.wait_ge(dd, 2)
            s.dma_start(sid.rearrange("e (a b) -> a e b", b=S), idi[:]).then_inc(st, 16)
            s.wait_ge(st, 32)

        @b.scalar
        def _(c):
            c.wait_ge(ex, 1)
            nc.scalar.activation(v_[:], v_[:], ACT.Exp).then_inc(xe, 1)

        flat = lambda t: t[:].rearrange("p t e -> p (t e)")

        @b.tensor
        def _(t):
            tens = nc.tensor
            t.wait_ge(tv, 1)
            tens.transpose(ps[0][0:E0, 0:P], m8[:], K.ident[:]).then_inc(vt, 1)
            t.wait_ge(tv, 2)
            tens.matmul(ps[1][:, 0:E0], K.ones[0:E0, :], dg[:], start=True, stop=True).then_inc(vt, 1)
            t.wait_ge(tv, 3)
            tens.matmul(ps[2][:, 0:E0], K.ones[:], rs[:], start=True, stop=True).then_inc(vt, 1)

            def count(n, k, u):
                t.wait_ge(cs, n + 1)
                tens.matmul(psC[u][:, 0:E0], K.ones[:], m8[:], start=True, stop=True).then_inc(cd, 1)
            pairs(t, BITS, count)
            t.wait_ge(tv, 4)
            t.wait_ge(g1, 2)
            tens.matmul(ps[0][:, 0:E0], K.ones[:], m8[:], start=True, stop=True)
            tens.matmul(ps[1][:, 0:W], tri[:], flat(hit), start=True, stop=True)
            tens.matmul(ps[2][:, 0:W], K.ones[:], flat(hit), start=True, stop=True).then_inc(vt, 1)
            t.wait_ge(tv, 5)
            tens.matmul(ps[1][:, 0:W], tri[:], flat(hit), start=True, stop=True)
            tens.matmul(ps[2][:, 0:W], K.ones[:], flat(hit), start=True, stop=True).then_inc(vt, 1)
            t.wait_ge(tv, 6)
            for e in range(E0):
                for k in range(NT):
                    ins = tens.matmul(ps[3][0:S, e * 2 * S:(e + 1) * 2 * S], oa[:, k * E0 + e, :],
                                      ob[:, k * E0 + e, :, :].rearrange("p a b -> p (a b)"),
                                      start=(k == 0), stop=(k == NT - 1))
            ins.then_inc(vt, 1)

        @b.vector
        def _(v):
            vv = nc.vector
            ch = Chain(v, vch)
            eh = lambda t: t[:].rearrange("p t e -> p e t")
            bc = lambda t: t.unsqueeze(1).to_broadcast([P, NT, E0])
            v.wait_ge(g1, 2)
            ch(vv.tensor_reduce(pv[:], K.ident[:, 0:TAIL], AX.X, ALU.add))
            ch(vv.memset(zero[:], 0.0))
            lastl = lg[:, NT - 1, :]
            ch(vv.tensor_scalar(lastl, lastl, pv[:], None, ALU.mult))
            ch(vv.tensor_scalar(rank[:, 0, 0:1], pv[:], BIG, -BIG, ALU.mult, ALU.add))
            ch(vv.tensor_scalar(lastl, lastl, rank[:, 0, 0:1], None, ALU.add))
            vv.tensor_reduce(m8[:], eh(lg), AX.X, ALU.max).then_inc(tv, 1)
            v.wait_ge(vt, 1)
            ch(vv.tensor_reduce(m1[:], ps[0][0:E0, 0:P], AX.X, ALU.max))
            vv.tensor_scalar(dg[:], K.ident[0:E0, 0:E0], m1[:], None, ALU.mult).then_inc(tv, 1)
            v.wait_ge(vt, 2)
            vv.tensor_tensor(v_[:], lg[:], bc(ps[1][:, 0:E0]), ALU.subtract).then_inc(ex, 1)
            v.wait_ge(xe, 1)
            vv.tensor_reduce(rs[:], eh(v_), AX.X, ALU.add).then_inc(tv, 1)
            v.wait_ge(vt, 3)
            ch(vv.reciprocal(need[:], ps[2][:, 0:E0]))
            vv.tensor_tensor(v_[:], v_[:], bc(need[:]), ALU.mult).then_inc(dd, 1)
            v.wait_ge(st, 16)
            ch(vv.tensor_scalar(v_[:, NT - 1, :], v_[:, NT - 1, :], pv[:], None, ALU.add))
            ch(vv.tensor_scalar(v_[:, NT - 1, :], v_[:, NT - 1, :], 1.0, None, ALU.subtract))
            ch(vv.memset(thr[:], 0))
            ch(vv.memset(bit[:], 1 << (BITS - 1)))

            def step(n, k, u):
                c = Chain(v, lc, n * 5)
                c(vv.tensor_tensor(cand[:], thr[:], bit[:].to_broadcast([P, E0]), ALU.bitwise_or))
                c(vv.tensor_tensor(hit[:], v_[:], bc(cand[:].bitcast(F32)), ALU.is_ge))
                vv.tensor_reduce(m8[:], eh(hit), AX.X, ALU.add).then_inc(cs, 1)
                v.wait_ge(cd, n + 1)
                c(vv.tensor_scalar(msk[:], psC[u][:, 0:E0], CAP0 - 0.5, -1.0, ALU.is_gt, ALU.mult))
                c(vv.scalar_tensor_tensor(thr[:], msk[:], bit[:], thr[:], ALU.bitwise_and, ALU.bitwise_or))
                c(vv.tensor_single_scalar(bit[:], bit[:], 1, ALU.logical_shift_right))
            pairs(v, BITS, step)
            tf = bc(thr[:].bitcast(F32))
            ch(vv.tensor_tensor(gt[:], v_[:], tf, ALU.is_gt))
            ch(vv.tensor_tensor(hit[:], v_[:], tf, ALU.is_equal))
            vv.tensor_reduce(m8[:], eh(gt), AX.X, ALU.add).then_inc(tv, 1)

            def ranks():
                ch(vv.tensor_copy(flat(tot), ps[2][:, 0:W]))
                for e in range(E0):
                    ins = vv.tensor_tensor_scan(inc[:, :, e], tot[:, :, e], zero[:], 0.0, ALU.add, ALU.add)
                ch(ins)
                ch(vv.tensor_tensor(inc[:], inc[:], tot[:], ALU.subtract))
                ch(vv.tensor_tensor(flat(rank), flat(inc), ps[1][:, 0:W], ALU.add))
            v.wait_ge(vt, 4)
            ch(vv.tensor_scalar(need[:], ps[0][:, 0:E0], -1.0, float(CAP0), ALU.mult, ALU.add))
            ranks()
            ch(vv.tensor_tensor(rank[:], rank[:], bc(need[:]), ALU.is_lt))
            ch(vv.tensor_tensor(hit[:], hit[:], rank[:], ALU.mult))
            vv.tensor_tensor(hit[:], hit[:], gt[:], ALU.add).then_inc(tv, 1)
            v.wait_ge(vt, 5)
            ranks()
            ch(vv.tensor_copy(ri[:, 0], rank[:]))
            ch(vv.tensor_single_scalar(ri[:, 1], ri[:, 0], 4, ALU.arith_shift_right))
            ch(vv.tensor_single_scalar(ri[:, 2], ri[:, 0], S - 1, ALU.bitwise_and))
            ch(vv.tensor_copy(rf[:], ri[:, 1:3]))
            ch(vv.tensor_scalar(gt[:], hit[:], -1000.0, 1000.0, ALU.mult, ALU.add))
            ch(vv.tensor_tensor(rf[:, 0], rf[:, 0], gt[:], ALU.add))
            io = K.iota[:, 0:S].unsqueeze(1).to_broadcast([P, W, S])
            for j, o in ((0, oa), (1, obm)):
                ch(vv.tensor_tensor(o[:], io, rf[:, j].rearrange("p t e -> p (t e)").unsqueeze(2).to_broadcast([P, W, S]),
                                    ALU.is_equal))
            ch(vv.tensor_scalar(ob[:, :, 0, :], obm[:], K.part[:], None, ALU.mult))
            vv.tensor_tensor(ob[:, :, 1, :].rearrange("p (t e) s -> p t e s", e=E0),
                             obm[:].rearrange("p (t e) s -> p t e s", e=E0),
                             tio[:].unsqueeze(2).unsqueeze(3).to_broadcast([P, NT, E0, S]), ALU.mult).then_inc(tv, 1)
            v.wait_ge(vt, 6)
            r = ps[3][0:S, 0:E0 * 2 * S].rearrange("a (e w b) -> a e w b", w=2, b=S)
            ch(vv.tensor_scalar(idf[:], r[:, :, 1, :], float(P), None, ALU.mult))
            ch(vv.tensor_tensor(idf[:], idf[:], r[:, :, 0, :], ALU.add))
            vv.tensor_copy(idi[:], idf[:]).then_inc(dd, 1)


def phase_experts0(nc, K, a, tab1, sid, xmid):
    HC = CAP0 // P
    NJ = E0 * HC
    R = D + E0
    with Phase(nc, "e0") as p:
        ix = p.sb("ix", [P, NJ], I32)
        g = p.sb("g", [P, NJ, R])
        w1 = p.sb("w1", [P, E0, KT, F0])
        w2 = p.sb("w2", [F0, E0, D])
        b1 = p.sb("b1", [F0, E0])
        b2 = p.sb("b2", [P, E0, D])
        xT = p.sb("xT", [P, 2, KT, CAP0])
        hT = p.sb("hT", [F0, 2, CAP0])
        y = p.sb("y", [P, 2, HC, D])
        psT = [p.ps(f"psT{u}", [P, D]) for u in range(4)]
        psH = [p.ps(f"psH{u}", [P, D]) for u in range(2)]
        psY = [p.ps(f"psY{u}", [P, D]) for u in range(2)]
        il = p.sem("il"); wl = [p.sem(f"wl{e}") for e in range(E0)]; cl = p.sem("cl"); got = [p.gather_sem(f"got{e}") for e in range(E0)]; turned = p.sem("turned"); cop = p.sem("cop")
        hd = p.sem("hd"); act = p.sem("act"); yd = p.sem("yd"); yb = p.sem("yb"); yr = p.sem("yr"); sca = p.gather_sem("sca")
        b = p.block(K.counted)

        @b.sync
        def _(s):
            with nc.allow_non_contiguous_dma(reason="slot tokens to one per partition"):
                s.dma_start(ix[:], sid.rearrange("e (c p) -> p (e c)", p=P)).then_inc(il, 16)
            s.dma_start(w1[:, 0], a["L0_ffn_W1"][0].rearrange("(kt p) f -> p kt f", p=P)).then_inc(wl[0], 16)
            s.dma_start(w2[:, 0], a["L0_ffn_W2"][0]).then_inc(wl[0], 16)
            with nc.allow_non_contiguous_dma(reason="biases to one per partition"):
                s.dma_start(b1[:], a["L0_ffn_b1"].rearrange("e f -> f e")).then_inc(cl, 16)
            s.dma_start(b2[:].rearrange("p e d -> p (e d)"),
                        a["L0_ffn_b2"].rearrange("e d -> (e d)").partition_broadcast(P)).then_inc(cl, 16)
            for e in range(1, E0):
                s.dma_start(w1[:, e], a["L0_ffn_W1"][e].rearrange("(kt p) f -> p kt f", p=P)).then_inc(wl[e], 16)
                s.dma_start(w2[:, e], a["L0_ffn_W2"][e]).then_inc(wl[e], 16)

        @b.gpsimd
        def _(q):
            q.wait_ge(il, 16)
            for j in range(NJ):
                q.indirect_dma_start(g[:, j, :], None, tab1,
                                     bass.IndirectOffsetOnAxis(ix[:, j:j + 1], 0)).then_inc(got[j // HC], 16)
            for e in range(E0):
                q.wait_ge(yr, HC * (e + 1))
                if e:
                    q.wait_ge(sca, 16 * HC * e)
                for c in range(HC):
                    j = e * HC + c
                    q.indirect_dma_start(xmid, bass.IndirectOffsetOnAxis(ix[:, j:j + 1], 0), y[:, e % 2, c, :], None,
                                         bounds_check=NP - 1, compute_op=ALU.add).then_inc(sca, 16)
            q.wait_ge(sca, 16 * HC * E0)

        @b.tensor
        def _(t):
            tens = nc.tensor
            for e in range(E0):
                u = e % 2
                t.wait_ge(got[e], 16 * HC)
                for c in range(HC):
                    wait(t, cop, 2 * e - 1 + c)
                    for kt in range(KT):
                        ins = tens.transpose(psT[2 * u + c][:, kt * P:(kt + 1) * P],
                                             g[:, e * HC + c, kt * P:(kt + 1) * P], K.ident[:])
                    ins.then_inc(turned, 1)
                t.wait_ge(cop, HC * (e + 1))
                t.wait_ge(wl[e], 32)
                wait(t, act, e - 1)
                for kt in range(KT):
                    ins = tens.matmul(psH[u][:, 0:CAP0], w1[:, e, kt, :], xT[:, u, kt, :],
                                      start=(kt == 0), stop=(kt == KT - 1))
                ins.then_inc(hd, 1)
                t.wait_ge(act, e + 1)
                for c in range(HC):
                    wait(t, yb, HC * e + c - 1)
                    tens.matmul(psY[c][:], hT[:, u, c * P:(c + 1) * P], w2[:, e, :],
                                start=True, stop=True).then_inc(yd, 1)

        @b.scalar
        def _(c_):
            for e in range(E0):
                u = e % 2
                for c in range(HC):
                    c_.wait_ge(turned, HC * e + c + 1)
                    wait(c_, hd, e - 1)
                    nc.scalar.activation(xT[:, u, :, c * P:(c + 1) * P],
                                         psT[2 * u + c][:].rearrange("p (k t) -> p k t", k=KT), ACT.Copy).then_inc(cop, 1)
                c_.wait_ge(hd, e + 1)
                wait(c_, yd, HC * (e - 1))
                if e == 0:
                    c_.wait_ge(cl, 32)
                nc.scalar.activation(hT[:, u, :], psH[u][:, 0:CAP0], ACT.Gelu, bias=b1[:, e:e + 1]).then_inc(act, 1)
                for c in range(HC):
                    c_.wait_ge(yb, HC * e + c + 1)
                    j = e * HC + c
                    nc.scalar.activation(y[:, u, c, :], y[:, u, c, :], ACT.Copy,
                                         scale=g[:, j, D + e:D + e + 1]).then_inc(yr, 1)

        @b.vector
        def _(v):
            for e in range(E0):
                for c in range(HC):
                    v.wait_ge(yd, HC * e + c + 1)
                    wait(v, sca, 16 * HC * (e - 1))
                    nc.vector.tensor_tensor(y[:, e % 2, c, :], psY[c][:], b2[:, e, :], ALU.add).then_inc(yb, 1)


def phase_norm2(nc, K, xmid, tab2):
    with Phase(nc, "n2") as p:
        xt = p.sb("xt", [P, XB, D])
        xn = p.sb("xn", [P, XB, D])
        ln = Norm(p, nc)
        normed = p.sem("normed")
        xl = [p.sem(f"xl{q}") for q in range(XB)]
        st = [p.sem(f"st{q}") for q in range(XB)]
        b = p.block(K.counted)

        @b.sync
        def _(s):
            def load(n, k, q):
                if within(n, NT):
                    wait(s, normed, n - XB + 1)
                    s.dma_start(xt[:, q, :], xmid[ds(n * P, P), :]).then_inc(xl[q], 16)
            skewed(s, NT, 0, load, XB)

        @b.scalar
        def _(c):
            def step(n, k, q):
                u = q % 2
                if within(n, NT):
                    ln.scalar(c, n, u)
                m, km, qm = back(n, k, q, 1, XB)
                um = qm % 2
                if within(m, NT):
                    c.wait_ge(ln.ready, m + 1)
                    wait(c, st[qm], km * 16)
                    nc.scalar.activation(xn[:, qm, :], xt[:, qm, :], ACT.Identity, bias=ln.offset(um),
                                         scale=ln.scale(um)).then_inc(normed, 1)
                m = n - 2
                if within(m, NT):
                    c.wait_ge(normed, m + 1)
                    c.dma_start(tab2[ds(m * P, P), :], xn[:, (q - 2) % XB, :]).then_inc(st[(q - 2) % XB], 16)
            skewed(c, NT, 2, step, XB)
            for q in range(XB):
                c.wait_ge(st[q], 16 * ((NT + XB - 1 - q) // XB))

        @b.vector
        def _(v):
            def step(n, k, q):
                u = q % 2
                if within(n, NT):
                    v.wait_ge(xl[q], k * 16 + 16)
                    ln.stats(v, n, u, xt[:, q, :])
                if within(n - 1, NT):
                    ln.finish(v, n - 1, 1 - u, normed)
            skewed(v, NT, 1, step, XB)


def phase_sage(nc, K, a, acc, own, xmid, mv, ys):
    ZT = NOV // (NT - 1)
    assert ZT * (NT - 1) == NOV
    XB = 4
    with Phase(nc, "sg") as p:
        w = p.sb("w", [P, KT, D])
        xt = p.sb("xt", [P, XB, D])
        xn = p.sb("xn", [P, 2, D])
        xT = p.sb("xT", [P, 2, KT, P])
        h = p.sb("h", [P, 2, D])
        sg = p.sb("sg", [P, 2, D])
        x3 = p.sb("x3", [P, 2, D])
        zeros = p.sb("zeros", [P, ZT, D])
        bst = p.sb("bst", [P, 6])
        junk = p.sb("junk", [P, 1])
        bmv = p.sb("bmv", [P, 2])
        psT = [p.ps(f"psT{u}", [P, D]) for u in range(2)]
        psH = [p.ps(f"psH{u}", [P, D]) for u in range(2)]
        wl = p.sem("wl"); md = p.sem("md"); turned = p.sem("turned"); cop = p.sem("cop"); prod = p.sem("prod")
        hs = p.sem("hs"); sgd = p.sem("sgd"); xd = p.sem("xd"); vch = p.sem("vch"); dch = p.sem("dch"); fin = p.sem("fin")
        vf = p.sem("vf"); zr = p.sem("zr"); zs = p.sem("zs")
        xl = [p.sem(f"xl{q}") for q in range(XB)]
        st = [p.sem(f"st{u}") for u in range(2)]
        b = p.block(K.counted)

        @b.sync
        def _(s):
            s.dma_start(w[:], a["L1_gnn_W_l"].rearrange("(k p) d -> p k d", p=P)).then_inc(wl, 16)

            def load(n, k, q):
                if within(n, NT):
                    wait(s, xd, n - XB + 1)
                    s.dma_start(xt[:, q, :], xmid[ds(n * P, P), :]).then_inc(xl[q], 16)
                    if not last(n):
                        s.dma_start(ys[ds(n * (ZT * P) + E1 * P, ZT * P), :].rearrange("(j p) d -> p j d", p=P),
                                    zeros[:]).then_inc(zs, 16)
            s.wait_ge(zr, 1)
            skewed(s, NT, 0, load, XB)
            s.wait_ge(zs, 16 * (NT - 1))

        @b.gpsimd
        def _(g):
            nc.gpsimd.memset(zeros[:], 0.0).then_inc(zr, 1)

        @b.scalar
        def _(c):
            def step(n, k, q):
                u = q % 2
                if within(n, NT):
                    c.wait_ge(turned, n + 1)
                    wait(c, prod, n - 1)
                    nc.scalar.activation(xT[:, u], psT[u][:].rearrange("p (k t) -> p k t", k=KT),
                                         ACT.Copy).then_inc(cop, 1)
                m = n - 2
                if within(m, NT):
                    c.wait_ge(hs, m + 1)
                    wait(c, xd, m - 1)
                    nc.scalar.activation(sg[:, u, :], h[:, u, :], ACT.Sigmoid).then_inc(sgd, 1)
                m, u = n - 4, q % 2
                if within(m, NT):
                    c.wait_ge(xd, m + 1)
                    c.dma_start(xmid[ds(m * P, P), :], x3[:, u, :]).then_inc(st[u], 16)
            skewed(c, NT, 4, step, XB)
            c.wait_ge(vf, 1)
            nc.scalar.activation(mv[:, :, 1:2], mv[:, :, 1:2], ACT.Sqrt).then_inc(fin, 1)
            for u in range(2):
                c.wait_ge(st[u], 16 * ((NT + 1 - u) // 2))

        @b.tensor
        def _(t):
            t.wait_ge(wl, 16)

            def step(n, k, q):
                u = q % 2
                if within(n, NT):
                    t.wait_ge(md, n + 1)
                    wait(t, cop, n - 1)
                    for kt in range(KT):
                        ins = nc.tensor.transpose(psT[u][:, kt * P:(kt + 1) * P], xn[:, u, kt * P:(kt + 1) * P],
                                                  K.ident[:])
                    ins.then_inc(turned, 1)
                m, um = n - 1, 1 - u
                if within(m, NT):
                    t.wait_ge(cop, m + 1)
                    wait(t, hs, m - 1)
                    for kt in range(KT):
                        ins = nc.tensor.matmul(psH[um][:], xT[:, um, kt, :], w[:, kt, :],
                                               start=(kt == 0), stop=(kt == KT - 1))
                    ins.then_inc(prod, 1)
            skewed(t, NT, 1, step, XB)

        @b.vector
        def _(v):
            vv = nc.vector
            d = Chain(v, dch)

            def step(n, k, q):
                u = q % 2
                if within(n, NT):
                    wait(v, turned, n - 1)
                    vv.tensor_scalar(xn[:, u, :], acc[:, ds(n, 1), 0:D].rearrange("p o d -> p (o d)"),
                                     K.rdeg[:, ds(n, 1), :].rearrange("p o d -> p (o d)"), None, ALU.mult).then_inc(md, 1)
                m, um = n - 2, u
                if within(m, NT):
                    v.wait_ge(prod, m + 1)
                    wait(v, sgd, m - 1)
                    vv.tensor_tensor(h[:, um, :], psH[um][:], own[:, ds(m, 1), :].rearrange("p o d -> p (o d)"),
                                     ALU.add).then_inc(hs, 1)
                m, km, qm = back(n, k, q, 3, XB)
                um = qm % 2
                if within(m, NT):
                    v.wait_ge(sgd, m + 1)
                    ch = Chain(v, vch, m * 4)
                    ch(vv.tensor_tensor(sg[:, um, :], sg[:, um, :], h[:, um, :], ALU.mult))
                    v.wait_ge(xl[qm], km * 16 + 16)
                    wait(v, st[um], km * 32 + 16 * (qm // 2))
                    vv.tensor_tensor(x3[:, um, :], sg[:, um, :], xt[:, qm, :], ALU.add).then_inc(xd, 1)
                    v.wait_ge(xd, m + 1)
                    ch(vv.bn_stats(bst[:], x3[:, um, :]))
                    vv.tensor_scalar(junk[:], bst[:, 0:1], 1.0, None, ALU.mult)
                    ch(vv.bn_aggr(bmv[:], bst[:]))
                    ch(vv.tensor_scalar(mv[:, ds(m, 1), :].rearrange("p o d -> p (o d)"), bmv[:], 0.0, None, ALU.add))
            skewed(v, NT, 3, step, XB)
            vv.tensor_scalar(mv[:, :, 1:2], mv[:, :, 1:2], EPS, None, ALU.add).then_inc(vf, 1)
            v.wait_ge(fin, 1)
            d(vv.reciprocal(mv[:, :, 1:2], mv[:, :, 1:2]))


def phase_shared(nc, K, a, xmid, tab3, xsh, sc):
    XB = 4
    with Phase(nc, "sh") as p:
        w13 = p.sb("w13", [P, 2, KT, D])
        w2 = p.sb("w2", [P, KT, D])
        gw = p.sb("gw", [E1, D])
        gT = p.sb("gT", [P, KT, E1])
        xt = p.sb("xt", [P, XB, D])
        xn = p.sb("xn", [P, 2, D])
        xT = p.sb("xT", [P, 2, KT, P])
        sg = p.sb("sg", [P, 2, D])
        hh = p.sb("hh", [P, 2, D])
        hT = p.sb("hT", [P, 2, KT, P])
        z = p.sb("z", [P, 2, D])
        psT = p.ps("psT", [P, D])
        psU = p.ps("psU", [P, D])
        psA = [p.ps(f"psA{u}", [P, D]) for u in range(2)]
        psB = [p.ps(f"psB{u}", [P, D]) for u in range(2)]
        psG = p.ps("psG", [P, D])
        psY = p.ps("psY", [P, D])
        wl = p.sem("wl"); nd = p.sem("nd"); turned = p.sem("turned"); cop = p.sem("cop"); ab = p.sem("ab")
        sgd = p.sem("sgd"); hd = p.sem("hd"); ht = p.sem("ht"); hc = p.sem("hc"); yd = p.sem("yd"); zd = p.sem("zd")
        scd = p.sem("scd"); gt = p.sem("gt"); gc = p.sem("gc"); vch = p.sem("vch")
        xl = [p.sem(f"xl{q}") for q in range(XB)]
        sn = [p.sem(f"sn{u}") for u in range(2)]
        sz = [p.sem(f"sz{u}") for u in range(2)]
        b = p.block(K.counted)

        @b.sync
        def _(s):
            s.dma_start(gw[:], a["L1_ffn_gate_w"]).then_inc(wl, 16)
            for j, nm in enumerate(("L1_ffn_sw1", "L1_ffn_sw3")):
                s.dma_start(w13[:, j], a[nm].rearrange("(k p) d -> p k d", p=P)).then_inc(wl, 16)
            s.dma_start(w2[:], a["L1_ffn_sw2"].rearrange("(k p) d -> p k d", p=P)).then_inc(wl, 16)

            def load(n, k, q):
                if within(n, NT):
                    wait(s, zd, n - XB + 1)
                    s.dma_start(xt[:, q, :], xmid[ds(n * P, P), :]).then_inc(xl[q], 16)
            skewed(s, NT, 0, load, XB)

        @b.scalar
        def _(c):
            c.wait_ge(gt, 1)
            nc.scalar.activation(gT[:], psG[:, 0:KT * E1].rearrange("p (k e) -> p k e", k=KT), ACT.Copy).then_inc(gc, 1)

            def step(n, k, q):
                m, u = n - 1, (q - 1) % 2
                if within(m, NT):
                    c.wait_ge(ab, m + 1)
                    wait(c, hd, m - 1)
                    nc.scalar.activation(sg[:, u, :], psA[u][:], ACT.Sigmoid)
                    nc.scalar.activation(sc[:, ds(m, 1), :].rearrange("p o e -> p (o e)"), psG[:, 0:E1],
                                         ACT.Sigmoid).then_inc(sgd, 1)
                m, u = n - 2, q % 2
                if within(m, NT):
                    c.wait_ge(ht, m + 1)
                    wait(c, yd, m - 1)
                    nc.scalar.activation(hT[:, u], psU[:].rearrange("p (k t) -> p k t", k=KT), ACT.Copy).then_inc(hc, 1)
                if within(n, NT):
                    c.wait_ge(turned, n + 1)
                    wait(c, ab, n - 1)
                    nc.scalar.activation(xT[:, u], psT[:].rearrange("p (k t) -> p k t", k=KT), ACT.Copy).then_inc(cop, 1)
                    c.wait_ge(nd, n + 1)
                    c.dma_start(tab3[ds(n * P, P), :], xn[:, u, :]).then_inc(sn[u], 16)
                m, u = n - 3, (q - 3) % 2
                if within(m, NT):
                    c.wait_ge(zd, m + 1)
                    c.dma_start(xsh[ds(m * P, P), :], z[:, u, :]).then_inc(sz[u], 16)
            skewed(c, NT, 3, step, XB)
            c.wait_ge(sgd, NT)
            for u in range(2):
                c.wait_ge(sn[u], 16 * ((NT + 1 - u) // 2))
                c.wait_ge(sz[u], 16 * ((NT + 1 - u) // 2))

        @b.tensor
        def _(t):
            tens = nc.tensor
            t.wait_ge(wl, 64)
            for kt in range(KT):
                ins = tens.transpose(psG[:, kt * E1:(kt + 1) * E1], gw[:, kt * P:(kt + 1) * P], K.ident[0:E1, 0:E1])
            ins.then_inc(gt, 1)
            t.wait_ge(gc, 1)

            def step(n, k, q):
                m, u = n - 1, (q - 1) % 2
                if within(m, NT):
                    t.wait_ge(cop, m + 1)
                    wait(t, hd, m - 1)
                    wait(t, sgd, m)
                    for kt in range(KT):
                        tens.matmul(psA[u][:], xT[:, u, kt, :], w13[:, 0, kt, :], start=(kt == 0), stop=(kt == KT - 1))
                        tens.matmul(psB[u][:], xT[:, u, kt, :], w13[:, 1, kt, :], start=(kt == 0), stop=(kt == KT - 1))
                        ins = tens.matmul(psG[:, 0:E1], xT[:, u, kt, :], gT[:, kt, :], start=(kt == 0), stop=(kt == KT - 1))
                    ins.then_inc(ab, 1)
                m, u = n - 2, q % 2
                if within(m, NT):
                    t.wait_ge(hd, m + 1)
                    wait(t, hc, m)
                    for kt in range(KT):
                        ins = tens.transpose(psU[:, kt * P:(kt + 1) * P], hh[:, u, kt * P:(kt + 1) * P], K.ident[:])
                    ins.then_inc(ht, 1)
                if within(n, NT):
                    t.wait_ge(nd, n + 1)
                    wait(t, cop, n)
                    for kt in range(KT):
                        ins = tens.transpose(psT[:, kt * P:(kt + 1) * P], xn[:, u, kt * P:(kt + 1) * P], K.ident[:])
                    ins.then_inc(turned, 1)
                if within(m, NT):
                    t.wait_ge(hc, m + 1)
                    wait(t, zd, m)
                    for kt in range(KT):
                        ins = tens.matmul(psY[:], hT[:, u, kt, :], w2[:, kt, :], start=(kt == 0), stop=(kt == KT - 1))
                    ins.then_inc(yd, 1)
            skewed(t, NT, 2, step, XB)

        @b.vector
        def _(v):
            vv = nc.vector

            def step(n, k, q):
                if within(n, NT):
                    u = q % 2
                    v.wait_ge(xl[q], k * 16 + 16)
                    wait(v, turned, n - 1)
                    wait(v, sn[u], k * 32 + 16 * (q // 2))
                    mean = K.mv[:, ds(n, 1), 0:1].rearrange("p o d -> p (o d)")
                    rstd = K.mv[:, ds(n, 1), 1:2].rearrange("p o d -> p (o d)")
                    vv.tensor_scalar(xn[:, u, :], xt[:, q, :], mean, rstd, ALU.subtract, ALU.mult).then_inc(nd, 1)
                m, km, qm = back(n, k, q, 2, XB)
                if within(m, NT):
                    u = qm % 2
                    v.wait_ge(sgd, m + 1)
                    ch = Chain(v, vch, m)
                    ch(vv.tensor_tensor(sg[:, u, :], sg[:, u, :], psA[u][:], ALU.mult))
                    wait(v, ht, m - 1)
                    vv.tensor_tensor(hh[:, u, :], sg[:, u, :], psB[u][:], ALU.mult).then_inc(hd, 1)
                m, km, qm = back(n, k, q, 3, XB)
                if within(m, NT):
                    u = qm % 2
                    v.wait_ge(yd, m + 1)
                    wait(v, sz[u], km * 32 + 16 * (qm // 2))
                    vv.tensor_tensor(z[:, u, :], psY[:], xt[:, qm, :], ALU.add).then_inc(zd, 1)
            skewed(v, NT, 3, step, XB)


def phase_route1(nc, K, sc):
    W = NT * E1
    CH = 5
    TC = NT // CH
    with Phase(nc, "r1") as p:
        top = p.sb("top", [P, NT, 8])
        tix = p.sb("tix", [P, NT, 8], U32)
        exf = p.sb("exf", [P, NT, TOP])
        den = p.sb("den", [P, NT, 1])
        ok = p.sb("ok", [P, NT, TOP])
        oh = p.sb("oh", [P, TOP, NT, E1])
        both = p.sb("both", [P, NT, E1])
        within = p.sb("within", [P, NT, E1])
        tot = p.sb("tot", [P, E1, NT])
        keep = p.sb("keep", [P, E1, NT])
        inc = p.sb("inc", [P, E1, NT])
        n_e = p.sb("n_e", [P, E1])
        ni = p.sb("ni", [P, 2, E1], I32)
        ovt = p.sb("ovt", [P, E1])
        ovi = p.sb("ovi", [P, E1])
        ovx = p.sb("ovx", [P, E1])
        zero = p.sb("zero", [P, E1])
        pos = p.sb("pos", [P, NT, TOP])
        ovb = p.sb("ovb", [P, NT, TOP])
        qi = p.sb("qi", [P, 3, NT, TOP], I32)
        qf = p.sb("qf", [P, 2, NT, TOP])
        far = p.sb("far", [P, NT, TOP])
        item = p.sb("item", [P, NT, TOP])
        valid = p.sb("valid", [P, NT, TOP])
        tmp = p.sb("tmp", [P, NT, TOP])
        oq = p.sb("oq", [P, 1])
        pv = p.sb("pv", [P, 1])
        tri = p.sb("tri", [P, P])
        tio = p.sb("tio", [P, NT, TOP])
        oa = p.sb("oa", [P, 2, NI1], BF16)
        ob = p.sb("ob", [P, 2, 2, P], BF16)
        idf = p.sb("idf", [NI1, P])
        ps = [p.ps(f"ps{u}", [P, D]) for u in range(4)]
        psI = p.ps("psI", [P, D])
        psT = p.ps("psT", [P, D])
        g1 = p.sem("g1"); vch = p.sem("vch"); tv = p.sem("tv"); vt = p.sem("vt"); od = p.sem("od"); om = p.sem("om")
        oc = p.sem("oc")
        b = p.block(K.counted)

        @b.gpsimd
        def _(g):
            nc.gpsimd.affine_select(out=tri[:], in_=K.ones[:], compare_op=ALU.is_gt, fill=0.0, base=0,
                                    pattern=[[1, P]], channel_multiplier=-1).then_inc(g1, 1)
            nc.gpsimd.iota(tio[:], [[1, NT], [0, TOP]], base=0, channel_multiplier=0,
                           allow_small_or_imprecise_dtypes=True).then_inc(g1, 1)

        @b.tensor
        def _(t):
            tens = nc.tensor
            t.wait_ge(g1, 2)
            for c in range(CH):
                t.wait_ge(tv, 1 + c)
                cols = both[:, c * TC:(c + 1) * TC, :].rearrange("p t e -> p (t e)")
                tens.matmul(ps[0][:, 0:TC * E1], tri[:], cols, start=True, stop=True)
                tens.matmul(ps[1][:, 0:TC * E1], K.ones[:], cols, start=True, stop=True).then_inc(vt, 1)
            t.wait_ge(tv, CH + 2)
            tens.matmul(ps[2][0:1, 0:P], oq[:], K.ident[:], start=True, stop=True).then_inc(vt, 1)

            def pairm(n, k, u):
                t.wait_ge(od, n + 1)
                ins = tens.matmul(psI[0:NI1, 0:2 * P], oa[:, u, :], ob[:, u].rearrange("p w b -> p (w b)"),
                                  start=isinstance(n, int) and n == 0, stop=isinstance(n, int) and n == NT * TOP - 1,
                                  skip_group_check=True)
                ins.then_inc(om, 1)
            for u in range(2):
                pairm(u, 0, u)
            with t.Fori(1, NT - 1) as k:
                for u in range(2):
                    pairm(k * 2 + u, k, u)
            for u in range(2):
                pairm(NT * TOP - 2 + u, NT - 1, u)
            t.wait_ge(oc, 1)
            tens.transpose(psT[:, 0:NI1], idf[:], K.ident[0:NI1, 0:NI1]).then_inc(vt, 1)

        @b.vector
        def _(v):
            vv = nc.vector
            ch = Chain(v, vch)
            v.wait_ge(g1, 2)
            for n in range(NT):
                ins = vv.max(top[:, n, :], sc[:, n, :])
            ch(ins)
            for n in range(NT):
                ins = vv.max_index(tix[:, n, :], top[:, n, :], sc[:, n, :])
            ch(ins)
            ch(vv.tensor_copy(exf[:], tix[:, :, 0:TOP]))
            ch(vv.tensor_tensor(den[:], top[:, :, 0:1], top[:, :, 1:2], ALU.add))
            ch(vv.tensor_scalar(den[:], den[:], 1e-20, None, ALU.add))
            ch(vv.reciprocal(den[:], den[:]))
            ch(vv.tensor_tensor(ok[:], top[:, :, 0:TOP], den[:].to_broadcast([P, NT, TOP]), ALU.mult))
            ch(vv.tensor_reduce(pv[:], K.ident[:, 0:TAIL], AX.X, ALU.add))
            ch(vv.tensor_scalar(pv[:], pv[:], -1000.0, 1000.0, ALU.mult, ALU.add))
            ch(vv.tensor_scalar(exf[:, NT - 1, :], exf[:, NT - 1, :], pv[:], None, ALU.add))
            io = K.iota[:, 0:E1].unsqueeze(1).to_broadcast([P, NT, E1])
            for k in range(TOP):
                ins = vv.tensor_tensor(oh[:, k], io, exf[:, :, k:k + 1].to_broadcast([P, NT, E1]), ALU.is_equal)
            ch(ins)
            vv.memset(zero[:], 0.0)
            ch(vv.memset(keep[:], 1.0))
            ch(vv.memset(keep[:, :, 0:1], 0.0))
            vv.tensor_tensor(both[:], oh[:, 0], oh[:, 1], ALU.add).then_inc(tv, 1)
            for c in range(CH):
                v.wait_ge(vt, 1 + c)
                vv.tensor_copy(within[:, c * TC:(c + 1) * TC, :].rearrange("p t e -> p (t e)"), ps[0][:, 0:TC * E1])
                vv.tensor_copy(tot[:, :, c * TC:(c + 1) * TC],
                               ps[1][:, 0:TC * E1].rearrange("p (t e) -> p e t", e=E1)).then_inc(tv, 1)
            v.wait_ge(tv, CH + 1)
            fl = lambda t: t[:].rearrange("p e t -> p (e t)")
            ch(vv.tensor_tensor_scan(fl(inc), fl(keep), fl(tot), 0.0, ALU.mult, ALU.add))
            ch(vv.tensor_scalar(n_e[:], inc[:, :, NT - 1], float(CAP1), None, ALU.min))
            ch(vv.tensor_tensor(inc[:], inc[:], tot[:], ALU.subtract))
            ch(vv.tensor_tensor(within[:], within[:], inc[:].rearrange("p e t -> p t e"), ALU.add))
            ch(vv.tensor_scalar(n_e[:], n_e[:], -1.0, None, ALU.add))
            ch(vv.tensor_copy(ni[:, 0], n_e[:]))
            ch(vv.tensor_single_scalar(ni[:, 1], ni[:, 0], 7, ALU.arith_shift_right))
            ch(vv.tensor_copy(ovt[:], ni[:, 1]))
            ch(vv.tensor_scalar(ovt[:], ovt[:], 0.0, None, ALU.max))
            ch(vv.tensor_tensor_scan(ovi[:], ovt[:], zero[:], 0.0, ALU.add, ALU.add))
            ch(vv.tensor_scalar(ovx[0:1, 0:1], ovi[0:1, E1 - 1:E1], float(E1 - 1), None, ALU.add))
            ch(vv.tensor_copy(K.nov[:], ovx[0:1, 0:1]))
            ch(vv.tensor_single_scalar(K.nov[:], K.nov[:], 2, ALU.arith_shift_right))
            ch(vv.tensor_tensor(ovx[:], ovi[:], ovt[:], ALU.subtract))
            ch(vv.tensor_scalar(zero[:], ovi[:], K.part[:], None, ALU.is_le))
            ch(vv.tensor_reduce(oq[:], zero[:], AX.X, ALU.add))
            vv.tensor_scalar(oq[:], oq[:], float(E1 - 1), None, ALU.min).then_inc(tv, 1)
            v.wait_ge(vt, CH + 1)
            ch(vv.tensor_copy(K.ovf[:], ps[2][0:1, 0:P]))
            for k in range(TOP):
                ch(vv.tensor_tensor(both[:], oh[:, k], within[:], ALU.mult))
                ch(vv.tensor_reduce(pos[:, :, k], both[:], AX.X, ALU.add))
                ch(vv.tensor_tensor(both[:], oh[:, k], ovx[:].unsqueeze(1).to_broadcast([P, NT, E1]), ALU.mult))
                ch(vv.tensor_reduce(ovb[:, :, k], both[:], AX.X, ALU.add))
            ch(vv.tensor_copy(qi[:, 0], pos[:]))
            ch(vv.tensor_single_scalar(qi[:, 1], qi[:, 0], 7, ALU.arith_shift_right))
            ch(vv.tensor_single_scalar(qi[:, 2], qi[:, 0], P - 1, ALU.bitwise_and))
            ch(vv.tensor_copy(qf[:], qi[:, 1:3]))
            ch(vv.tensor_scalar(far[:], qf[:, 0], 0.5, None, ALU.is_gt))
            ch(vv.tensor_tensor(tmp[:], qf[:, 0], ovb[:], ALU.add))
            ch(vv.tensor_scalar(tmp[:], tmp[:], float(E1 - 1), None, ALU.add))
            ch(vv.tensor_tensor(tmp[:], tmp[:], exf[:], ALU.subtract))
            ch(vv.tensor_tensor(tmp[:], tmp[:], far[:], ALU.mult))
            ch(vv.tensor_tensor(item[:], tmp[:], exf[:], ALU.add))
            ch(vv.tensor_scalar(valid[:], pos[:], float(CAP1), None, ALU.is_lt))
            ch(vv.tensor_scalar(tmp[:], item[:], float(P), None, ALU.mult))
            ch(vv.tensor_tensor(tmp[:], tmp[:], qf[:, 1], ALU.add))
            ch(vv.tensor_tensor(tmp[:], tmp[:], valid[:], ALU.mult))
            ch(vv.tensor_scalar(tmp[:], tmp[:], float(NI1 * P - 1), None, ALU.min))
            ch(vv.tensor_copy(K.pair[:], tmp[:]))
            ch(vv.tensor_scalar(ok[:], ok[:], ROUTE_SCALE, None, ALU.mult))
            ch(vv.tensor_tensor(K.gate[:], ok[:], valid[:], ALU.mult))
            ch(vv.tensor_scalar(valid[:], valid[:], -1000.0, 1000.0, ALU.mult, ALU.add))
            ch(vv.tensor_tensor(item[:], item[:], valid[:], ALU.add))
            fi = item[:].rearrange("p t k -> p (t k)")
            lo = qf[:, 1].rearrange("p t k -> p (t k)")
            ti = tio[:].rearrange("p t k -> p (t k)")

            def pairo(n, k, u):
                wait(v, om, n - 1)
                vv.tensor_scalar(oa[:, u, :], K.iota[:, 0:NI1], fi[:, ds(n, 1)], None, ALU.is_equal)
                vv.tensor_scalar(ob[:, u, 0, :], K.iota[:], lo[:, ds(n, 1)], K.part[:], ALU.is_equal, ALU.mult)
                vv.tensor_scalar(ob[:, u, 1, :], K.iota[:], lo[:, ds(n, 1)], ti[:, ds(n, 1)], ALU.is_equal,
                                 ALU.mult).then_inc(od, 1)
            pairs(v, NT * TOP, pairo)
            v.wait_ge(om, NT * TOP)
            ch(vv.tensor_scalar(idf[:], psI[0:NI1, P:2 * P], float(P), None, ALU.mult))
            vv.tensor_tensor(idf[:], idf[:], psI[0:NI1, 0:P], ALU.add).then_inc(oc, 1)
            v.wait_ge(vt, CH + 2)
            ch(vv.tensor_copy(K.slot[:], psT[:, 0:NI1]))


def phase_experts1(nc, K, a, tab3, ys):
    NW = 4
    FT = F1 // P
    with Phase(nc, "e1") as p:
        g = p.sb("g", [P, NW, D])
        w13 = p.sb("w13", [P, NW, KT, 2 * F1])
        w2 = p.sb("w2", [P, NW, FT, D])
        xT = p.sb("xT", [P, 2, KT, P])
        sg = p.sb("sg", [P, 2, F1])
        hh = p.sb("hh", [P, 2, F1])
        hT = p.sb("hT", [P, 2, FT, P])
        y = p.sb("y", [P, NW, D])
        fin = p.sb("fin", [1, 1])
        psX = [p.ps(f"psX{u}", [P, D]) for u in range(2)]
        psH = [p.ps(f"psH{u}", [P, D]) for u in range(2)]
        psU = [p.ps(f"psU{u}", [P, D]) for u in range(2)]
        psY = [p.ps(f"psY{u}", [P, D]) for u in range(2)]
        got = [p.gather_sem(f"got{q}") for q in range(NW)]
        wl = [p.sem(f"wl{q}") for q in range(NW)]
        vl = [p.sem(f"vl{q}") for q in range(NW)]
        st = [p.sem(f"st{q}") for q in range(NW)]
        turned = p.sem("turned")
        cop = p.sem("cop")
        up = p.sem("up")
        sgd = p.sem("sgd")
        hd = p.sem("hd")
        ht = p.sem("ht")
        hc = p.sem("hc")
        yd = p.sem("yd")
        yc = p.sem("yc")
        vch = p.sem("vch")
        b = p.block(K.counted)

        def turns(eng):
            return eng.value_load(K.nov[0:1, 0:1], min_val=E1 // NW - 1, max_val=NI1 // NW - 1)

        def prev(n, k, q, j):
            return n - j, k + (q - j) // NW, (q - j) % NW

        def n_ok(n, q, j):
            if ended[0]:
                return q < j
            return not isinstance(n, int) or n >= j

        ended = [False]

        def run(eng, skew, step):
            nt = turns(eng)
            first = 2
            for n in range(first * NW):
                step(n, n // NW, n % NW)
            with eng.Fori(first, nt + 1) as k:
                for q in range(NW):
                    step(k * NW + q, k, q)
            ended[0] = True
            for q in range(skew):
                step(nt * NW + (NW + q), nt + 1, q)
            ended[0] = False
            return nt

        def load(s, n, k, q, e):
            wait(s, up, n - NW + 1)
            for j, nm in enumerate(("L1_ffn_w1", "L1_ffn_w3")):
                s.dma_start(w13[:, q, :, j * F1:(j + 1) * F1],
                            a[nm][ds(e, 1)].rearrange("o (k p) f -> p (o k) f", p=P)).then_inc(wl[q], 16)
            wait(s, yd, n - NW + 1)
            s.dma_start(w2[:, q], a["L1_ffn_w2"][ds(e, 1)].rearrange("o (k p) d -> p (o k) d", p=P)).then_inc(vl[q], 16)

        @b.sync
        def _(s):
            for q in range(NW):
                load(s, q, 0, q, q)
            with s.Fori(1, E1 // NW) as k:
                for q in range(NW):
                    load(s, k * NW + q, k, q, k * NW + q)
            with s.Fori(E1 // NW, turns(s) + 1) as k:
                for q in range(NW):
                    e = s.value_load(K.ovf[0:1, ds(k * NW + (q - E1), 1)], min_val=0, max_val=E1 - 1)
                    load(s, k * NW + q, k, q, e)

        @b.gpsimd
        def _(g_):
            def gather(n):
                wait(g_, turned, n - NW + 1)
                g_.indirect_dma_start(g[:, n % NW, :], None, tab3,
                                      bass.IndirectOffsetOnAxis(K.slot[:, n:n + 1], 0)).then_inc(got[n % NW], 16)
            for n in range(E1):
                gather(n)
            nt = turns(g_)
            for k in range(E1 // NW, NI1 // NW):
                with g_.If(nt > k - 1):
                    for q in range(NW):
                        gather(k * NW + q)

        @b.tensor
        def _(t):
            tens = nc.tensor

            def step(n, k, q):
                u = q % 2
                m, km, qm = prev(n, k, q, 1)
                if n_ok(n, q, 1):
                    um = qm % 2
                    t.wait_ge(cop, m + 1)
                    t.wait_ge(wl[qm], km * 32 + 32)
                    wait(t, hd, m - 1)
                    for kt in range(KT):
                        ins = tens.matmul(psH[um][:], xT[:, um, kt, :], w13[:, qm, kt, :],
                                          start=(kt == 0), stop=(kt == KT - 1))
                    ins.then_inc(up, 1)
                m, km, qm = prev(n, k, q, 2)
                um = qm % 2
                if n_ok(n, q, 2):
                    t.wait_ge(hd, m + 1)
                    wait(t, hc, m - 1)
                    for c in range(FT):
                        ins = tens.transpose(psU[um][:, c * P:(c + 1) * P], hh[:, um, c * P:(c + 1) * P], K.ident[:])
                    ins.then_inc(ht, 1)
                if n_ok(n, q, 0):
                    t.wait_ge(got[q], k * 16 + 16)
                    wait(t, cop, n - 1)
                    for kt in range(KT):
                        ins = tens.transpose(psX[u][:, kt * P:(kt + 1) * P], g[:, q, kt * P:(kt + 1) * P], K.ident[:])
                    ins.then_inc(turned, 1)
                if n_ok(n, q, 2):
                    t.wait_ge(hc, m + 1)
                    t.wait_ge(vl[qm], km * 16 + 16)
                    wait(t, yc, m - 1)
                    for c in range(FT):
                        ins = tens.matmul(psY[um][:], hT[:, um, c, :], w2[:, qm, c, :], start=(c == 0), stop=(c == FT - 1))
                    ins.then_inc(yd, 1)
            run(t, 2, step)

        @b.scalar
        def _(c):
            def step(n, k, q):
                m, km, qm = prev(n, k, q, 1)
                um = qm % 2
                if n_ok(n, q, 1):
                    c.wait_ge(up, m + 1)
                    nc.scalar.activation(sg[:, um, :], psH[um][:, 0:F1], ACT.Sigmoid).then_inc(sgd, 1)
                m, km, qm = prev(n, k, q, 2)
                um = qm % 2
                if n_ok(n, q, 2):
                    c.wait_ge(ht, m + 1)
                    wait(c, yd, m - 1)
                    nc.scalar.activation(hT[:, um], psU[um][:, 0:F1].rearrange("p (c t) -> p c t", t=P),
                                         ACT.Copy).then_inc(hc, 1)
                if n_ok(n, q, 0):
                    u = q % 2
                    c.wait_ge(turned, n + 1)
                    wait(c, up, n - 1)
                    nc.scalar.activation(xT[:, u], psX[u][:].rearrange("p (k t) -> p k t", k=KT), ACT.Copy).then_inc(cop, 1)
                m, km, qm = prev(n, k, q, 3)
                if n_ok(n, q, 3):
                    c.wait_ge(yc, m + 1)
                    c.dma_start(ys[ds(m * P, P), :], y[:, qm, :]).then_inc(st[qm], 16)
            nt = run(c, 3, step)
            for q in range(NW):
                c.wait_ge(st[q], nt * 16 + 16)
            nc.scalar.activation(fin[:], K.part[0:1, :], ACT.Copy)

        @b.vector
        def _(v):
            vv = nc.vector

            def step(n, k, q):
                m, km, qm = prev(n, k, q, 1)
                um = qm % 2
                if n_ok(n, q, 1):
                    v.wait_ge(sgd, m + 1)
                    ch = Chain(v, vch, m)
                    ch(vv.tensor_tensor(sg[:, um, :], sg[:, um, :], psH[um][:, 0:F1], ALU.mult))
                    wait(v, ht, m - 1)
                    vv.tensor_tensor(hh[:, um, :], sg[:, um, :], psH[um][:, F1:2 * F1], ALU.mult).then_inc(hd, 1)
                m, km, qm = prev(n, k, q, 2)
                um = qm % 2
                if n_ok(n, q, 2):
                    v.wait_ge(yd, m + 1)
                    wait(v, st[qm], km * 16)
                    vv.tensor_copy(y[:, qm, :], psY[um][:]).then_inc(yc, 1)
            run(v, 2, step)


def phase_combine(nc, K, xsh, ys, out):
    with Phase(nc, "cb") as p:
        z = p.sb("z", [P, XB, D])
        g = p.sb("g", [P, XB, TOP, D])
        o = p.sb("o", [P, XB, D])
        zl = [p.sem(f"zl{q}") for q in range(XB)]
        got = [p.gather_sem(f"got{q}") for q in range(XB)]
        st = [p.sem(f"st{q}") for q in range(XB)]
        half = p.sem("half")
        od = p.sem("od")
        b = p.block(K.counted)

        @b.sync
        def _(s):
            def load(n, k, q):
                if within(n, NT):
                    wait(s, od, n - XB + 1)
                    s.dma_start(z[:, q, :], xsh[ds(n * P, P), :]).then_inc(zl[q], 16)
            skewed(s, NT, 0, load, XB)

        @b.gpsimd
        def _(q):
            for n in range(NT):
                wait(q, od, n - XB + 1)
                for k in range(TOP):
                    q.indirect_dma_start(g[:, n % XB, k, :], None, ys,
                                         bass.IndirectOffsetOnAxis(K.pair[:, n, k:k + 1], 0)).then_inc(got[n % XB], 16)

        @b.scalar
        def _(c):
            def store(n, k, q):
                if within(n, NT):
                    c.wait_ge(od, n + 1)
                    c.dma_start(tile_rows(out, n), o[0:rows_of(n), q, :]).then_inc(st[q], 16)
            skewed(c, NT, 0, store, XB)
            for q in range(XB):
                c.wait_ge(st[q], 16 * ((NT + XB - 1 - q) // XB))

        @b.vector
        def _(v):
            def step(n, k, q):
                if within(n, NT):
                    v.wait_ge(zl[q], k * 16 + 16)
                    v.wait_ge(got[q], k * 32 + 32)
                    wait(v, st[q], k * 16)
                    w = lambda j: K.gate[:, ds(n, 1), j:j + 1].rearrange("p o d -> p (o d)")
                    nc.vector.scalar_tensor_tensor(o[:, q, :], g[:, q, 0, :], w(0), z[:, q, :], ALU.mult,
                                                   ALU.add).then_inc(half, 1)
                    v.wait_ge(half, n + 1)
                    nc.vector.scalar_tensor_tensor(o[:, q, :], g[:, q, 1, :], w(1), o[:, q, :], ALU.mult,
                                                   ALU.add).then_inc(od, 1)
            skewed(v, NT, 0, step, XB)


def kernel(**inputs):
    import concourse.bacc as bacc
    from concourse.bass_utils import run_bass_kernel_spmd as run

    nc = bacc.Bacc("TRN2", target_bir_lowering=False, num_devices=1)
    arrays, aps = {}, {}
    for name, value in inputs.items():
        v = np.ascontiguousarray(value)
        arrays[f"in_{name}"] = v
        aps[name] = nc.dram_tensor(f"in_{name}", v.shape, mybir.dt.from_np(v.dtype), kind="ExternalInput").ap()
    out = nc.dram_tensor("out_x", (N, D), F32, kind="ExternalOutput").ap()
    build(nc, aps, out, 9)
    return run(nc, [arrays], core_ids=[0]).results[0]["out_x"]
```
